# Optimizing a Trainium2 kernel written in Bass

```python
import numpy as np
import jax
import jax.numpy as jnp

def _softmax(x, axis=-1):
    return jax.nn.softmax(x, axis=axis)

def _gelu(x):
    return jax.nn.gelu(x, approximate=True)

def _silu(x):
    return jax.nn.silu(x)

def _sigmoid(x):
    return jax.nn.sigmoid(x)

def _layernorm(x, axis=-1, eps=1e-05):
    m = jnp.mean(x, axis=axis, keepdims=True)
    v = jnp.var(x, axis=axis, keepdims=True)
    return (x - m) / jnp.sqrt(v + eps)

def _scatter_add(tgt, idx, src, axis=0):
    return tgt.at[idx].add(src)

def _segment_sum(src, seg, n):
    return jax.ops.segment_sum(src, seg, n)
kernel_name = 'mk_adaln_ffn_d2_seqx_r4_a40d4a'

def setup_inputs(seed: int=0):
    np.random.seed(seed)
    _w = jnp.asarray

    def _rec_inputs():
        import jax
        import jax.numpy as jnp
        _rk = jax.random.key(seed)
        x = 8.748e-05 + 1 * jax.random.normal(jax.random.fold_in(_rk, 1), (8, 256, 512), jnp.float32)
        _lenS = 256 - jax.random.randint(jax.random.fold_in(_rk, 7), (8,), 0, max(1, 256 // 4) + 1, jnp.int32)
        _lenS2 = 256 - jax.random.randint(jax.random.fold_in(_rk, 8), (8,), 0, max(1, 256 // 4) + 1, jnp.int32)
        cond_2048 = -9.80646e-05 + 1.00041 * jax.random.normal(jax.random.fold_in(_rk, 11), (8, 512), jnp.float32)
        return (x, cond_2048)
    x, cond_2048 = _rec_inputs()

    def _L0_cond_setup():
        import jax, jax.numpy as jnp
        import numpy as np
        DT = 0.01
        EPSILON = 0.08
        ALPHA = 0.7
        BETA = 0.8
        CLAMP = 20.0
        B, T, N = (64, 128, 512)

        def _derivative(q, p, drive, coupling, bias):
            i_couple = jnp.tanh(q) @ coupling.T
            dq = q - q ** 3 / 3.0 - p + drive + i_couple + bias
            dp = EPSILON * (q + ALPHA - BETA * p)
            return (dq, dp)

        def _rk4_step(q, p, drive, coupling, bias):
            dq1, dp1 = _derivative(q, p, drive, coupling, bias)
            dq2, dp2 = _derivative(q + 0.5 * DT * dq1, p + 0.5 * DT * dp1, drive, coupling, bias)
            dq3, dp3 = _derivative(q + 0.5 * DT * dq2, p + 0.5 * DT * dp2, drive, coupling, bias)
            dq4, dp4 = _derivative(q + DT * dq3, p + DT * dp3, drive, coupling, bias)
            q_next = q + DT / 6.0 * (dq1 + 2 * dq2 + 2 * dq3 + dq4)
            p_next = p + DT / 6.0 * (dp1 + 2 * dp2 + 2 * dp3 + dp4)
            q_next = jnp.clip(q_next, -CLAMP, CLAMP)
            p_next = jnp.clip(p_next, -CLAMP, CLAMP)
            return (q_next, p_next)
        key = jax.random.key(seed)
        k1, k2, k3, k4 = jax.random.split(key, 4)
        return {'q0': jax.random.normal(k1, (B, N), dtype=jnp.float32), 'p0': jax.random.normal(k2, (B, N), dtype=jnp.float32), 'input_drive_seq': jax.random.normal(k3, (B, T, N), dtype=jnp.float32), 'coupling': jax.random.normal(k4, (N, N), dtype=jnp.float32) * 0.01, 'bias': jnp.zeros((N,), dtype=jnp.float32)}
    _L0_cond_all = _L0_cond_setup()
    _L0_cond_in = {k: v for k, v in _L0_cond_all.items() if k in ('coupling', 'bias')}
    del _L0_cond_all

    def _L0_ffn_setup():
        import jax, jax.numpy as jnp
        import numpy as np
        B, S, D, H = (4, 512, 512, 2048)

        def fwht(x):
            orig_shape = x.shape
            n = orig_shape[-1]
            x = x.reshape(-1, n)
            h = 1
            while h < n:
                xb = x.reshape(-1, n // (2 * h), 2, h)
                a = xb[:, :, 0, :]
                b = xb[:, :, 1, :]
                x = jnp.stack([a + b, a - b], axis=2).reshape(-1, n)
                h *= 2
            scale = jnp.asarray(1.0 / np.sqrt(n), dtype=x.dtype)
            return (x * scale).reshape(orig_shape)
        key = jax.random.key(seed)
        kx, k1, k2, k3 = jax.random.split(key, 4)
        x = jax.random.normal(kx, (B, S, D), dtype=jnp.float32)
        W1 = jax.random.normal(k1, (H, D), dtype=jnp.float32) * (1.0 / np.sqrt(D))
        W2 = jax.random.normal(k2, (D, H), dtype=jnp.float32) * (1.0 / np.sqrt(H))
        W3 = jax.random.normal(k3, (H, D), dtype=jnp.float32) * (1.0 / np.sqrt(D))
        return {'x': x, 'W1': W1, 'W2': W2, 'W3': W3}
    _L0_ffn_all = _L0_ffn_setup()
    _L0_ffn_in = {k: v for k, v in _L0_ffn_all.items() if k in ('W1', 'W2', 'W3')}
    del _L0_ffn_all

    def _L1_cond_setup():
        import jax, jax.numpy as jnp
        import numpy as np
        import math
        D_MODEL = 256
        NUM_HEAD = 16
        NEG_INF = -1e+30
        key = jax.random.key(seed)
        k_x, k_m, k_q, k_k, k_v = jax.random.split(key, 5)
        B, C, T = (4, D_MODEL, 512)
        x = jax.random.normal(k_x, (B, C, T), dtype=jnp.float32)
        mask = (jax.random.uniform(k_m, (B, T)) < 0.9).astype(jnp.float32)
        limit = math.sqrt(6.0 / (C + C))
        Wq = jax.random.uniform(k_q, (C, C), minval=-limit, maxval=limit, dtype=jnp.float32)
        Wk = jax.random.uniform(k_k, (C, C), minval=-limit, maxval=limit, dtype=jnp.float32)
        Wv = jax.random.uniform(k_v, (C, C), minval=-limit, maxval=limit, dtype=jnp.float32)
        b = jnp.zeros((1,), dtype=jnp.float32)
        return {'x': x, 'mask': mask, 'Wq': Wq, 'Wk': Wk, 'Wv': Wv, 'b': b}
    _L1_cond_all = _L1_cond_setup()
    _L1_cond_in = {k: v for k, v in _L1_cond_all.items() if k in ('Wq', 'Wk', 'Wv', 'b')}
    del _L1_cond_all

    def _L1_ffn_setup():
        import jax, jax.numpy as jnp
        import numpy as np
        NUM_EXPERTS = 8
        EXPERTS_PER_TOK = 2
        key = jax.random.key(seed)
        k1, k2, k3, k4, k5 = jax.random.split(key, 5)
        B, T, D, F, E = (4, 256, 512, 256, NUM_EXPERTS)
        return {'x': jax.random.normal(k1, (B, T, D), dtype=jnp.float32), 'router_w': jax.random.normal(k2, (D, E), dtype=jnp.float32) * 0.02, 'gate_proj': jax.random.normal(k3, (E, D, F), dtype=jnp.float32) * 0.02, 'up_proj': jax.random.normal(k4, (E, D, F), dtype=jnp.float32) * 0.02, 'down_proj': jax.random.normal(k5, (E, F, D), dtype=jnp.float32) * 0.02}
    _L1_ffn_all = _L1_ffn_setup()
    _L1_ffn_in = {k: v for k, v in _L1_ffn_all.items() if k in ('router_w', 'gate_proj', 'up_proj', 'down_proj')}
    del _L1_ffn_all
    return {'x': x, 'cond_2048': cond_2048, 'L0_cond_coupling': _L0_cond_in['coupling'], 'L0_cond_bias': _L0_cond_in['bias'], 'L0_ffn_W1': _L0_ffn_in['W1'], 'L0_ffn_W2': _L0_ffn_in['W2'], 'L0_ffn_W3': _L0_ffn_in['W3'], 'L1_cond_Wq': _L1_cond_in['Wq'], 'L1_cond_Wk': _L1_cond_in['Wk'], 'L1_cond_Wv': _L1_cond_in['Wv'], 'L1_cond_b': _L1_cond_in['b'], 'L1_ffn_router_w': _L1_ffn_in['router_w'], 'L1_ffn_gate_proj': _L1_ffn_in['gate_proj'], 'L1_ffn_up_proj': _L1_ffn_in['up_proj'], 'L1_ffn_down_proj': _L1_ffn_in['down_proj']}

def reference(x, cond_2048, L0_cond_coupling, L0_cond_bias, L0_ffn_W1, L0_ffn_W2, L0_ffn_W3, L1_cond_Wq, L1_cond_Wk, L1_cond_Wv, L1_cond_b, L1_ffn_router_w, L1_ffn_gate_proj, L1_ffn_up_proj, L1_ffn_down_proj):
    import jax
    import jax.numpy as jnp

    def _L0_cond_ref(q0, p0, input_drive_seq, coupling, bias):
        import jax, jax.numpy as jnp
        import numpy as np
        DT = 0.01
        EPSILON = 0.08
        ALPHA = 0.7
        BETA = 0.8
        CLAMP = 20.0
        B, T, N = (64, 128, 512)

        def _derivative(q, p, drive, coupling, bias):
            i_couple = jnp.tanh(q) @ coupling.T
            dq = q - q ** 3 / 3.0 - p + drive + i_couple + bias
            dp = EPSILON * (q + ALPHA - BETA * p)
            return (dq, dp)

        def _rk4_step(q, p, drive, coupling, bias):
            dq1, dp1 = _derivative(q, p, drive, coupling, bias)
            dq2, dp2 = _derivative(q + 0.5 * DT * dq1, p + 0.5 * DT * dp1, drive, coupling, bias)
            dq3, dp3 = _derivative(q + 0.5 * DT * dq2, p + 0.5 * DT * dp2, drive, coupling, bias)
            dq4, dp4 = _derivative(q + DT * dq3, p + DT * dp3, drive, coupling, bias)
            q_next = q + DT / 6.0 * (dq1 + 2 * dq2 + 2 * dq3 + dq4)
            p_next = p + DT / 6.0 * (dp1 + 2 * dp2 + 2 * dp3 + dp4)
            q_next = jnp.clip(q_next, -CLAMP, CLAMP)
            p_next = jnp.clip(p_next, -CLAMP, CLAMP)
            return (q_next, p_next)
        drive_tbn = jnp.swapaxes(input_drive_seq, 0, 1)

        def scan_fn(carry, drive):
            q, p = carry
            q, p = _rk4_step(q, p, drive, coupling, bias)
            return ((q, p), q)
        (_, _), q_trace_tbn = jax.lax.scan(scan_fn, (q0, p0), drive_tbn)
        return jnp.swapaxes(q_trace_tbn, 0, 1)

    def _L0_ffn_ref(x, W1, W2, W3):
        import jax, jax.numpy as jnp
        import numpy as np
        B, S, D, H = (4, 512, 512, 2048)

        def fwht(x):
            orig_shape = x.shape
            n = orig_shape[-1]
            x = x.reshape(-1, n)
            h = 1
            while h < n:
                xb = x.reshape(-1, n // (2 * h), 2, h)
                a = xb[:, :, 0, :]
                b = xb[:, :, 1, :]
                x = jnp.stack([a + b, a - b], axis=2).reshape(-1, n)
                h *= 2
            scale = jnp.asarray(1.0 / np.sqrt(n), dtype=x.dtype)
            return (x * scale).reshape(orig_shape)
        up_gate = jnp.einsum('bsd,hd->bsh', x, W1)
        up_lin = jnp.einsum('bsd,hd->bsh', x, W3)
        hidden = jax.nn.silu(up_gate) * up_lin
        hidden = fwht(hidden)
        out = jnp.einsum('bsh,dh->bsd', hidden, W2)
        return out

    def _L1_cond_ref(x, mask, Wq, Wk, Wv, b):
        import jax, jax.numpy as jnp
        import numpy as np
        import math
        D_MODEL = 256
        NUM_HEAD = 16
        NEG_INF = -1e+30
        B, C, T = x.shape
        H = NUM_HEAD
        Dh = C // H

        def proj(W):
            y = jnp.einsum('oc,bct->bto', W, x)
            return y.reshape(B, T, H, Dh).transpose(0, 2, 1, 3)
        Q, K, V = (proj(Wq), proj(Wk), proj(Wv))
        att = jnp.einsum('bhqd,bhkd->bhqk', Q, K) * (1.0 / math.sqrt(Dh))
        att = att + b[0]
        m = mask[:, None, None, :]
        att = att * m + (1.0 - m) * NEG_INF
        att = jax.nn.softmax(att, axis=-1)
        y = jnp.einsum('bhqk,bhkd->bhqd', att, V)
        y = y.transpose(0, 2, 1, 3).reshape(B, T, C)
        return y.transpose(0, 2, 1)

    def _L1_ffn_ref(x, router_w, gate_proj, up_proj, down_proj):
        import jax, jax.numpy as jnp
        import numpy as np
        NUM_EXPERTS = 8
        EXPERTS_PER_TOK = 2
        E, K = (NUM_EXPERTS, EXPERTS_PER_TOK)
        scores = jnp.einsum('btd,de->bte', x, router_w).astype(jnp.float32)
        routing_weights, routing_idx = jax.lax.top_k(jax.nn.softmax(scores, axis=-1), K)
        routing_weights = (routing_weights / jnp.sum(routing_weights, axis=-1, keepdims=True)).astype(x.dtype)
        onehot = jax.nn.one_hot(routing_idx, E, dtype=x.dtype)
        dispatch_mask = jnp.sum(onehot, axis=2)
        combine_weights = jnp.einsum('btke,btk->bte', onehot, routing_weights)
        dispatched = x[:, :, None, :] * dispatch_mask[..., None]
        gate = jnp.einsum('bted,edf->btef', dispatched, gate_proj)
        up = jnp.einsum('bted,edf->btef', dispatched, up_proj)
        act = jax.nn.silu(gate) * up
        expert_out = jnp.einsum('btef,efd->bted', act, down_proj)
        return jnp.einsum('bted,bte->btd', expert_out, combine_weights)
    x = x + _L0_ffn_ref(_L0_cond_ref(cond_2048, cond_2048, x, L0_cond_coupling, L0_cond_bias), L0_ffn_W1, L0_ffn_W2, L0_ffn_W3)
    x = x + _L1_ffn_ref(_L1_cond_ref(x, cond_2048, L1_cond_Wq, L1_cond_Wk, L1_cond_Wv, L1_cond_b), L1_ffn_router_w, L1_ffn_gate_proj, L1_ffn_up_proj, L1_ffn_down_proj)
    return x

_drawn_inputs = setup_inputs


def setup_inputs(seed=0):
    import zlib

    import numpy as np

    out = dict(_drawn_inputs(seed))
    spreads = {'L0_cond_bias': (0.0, 0.1)}
    factors = {}
    for name, (base, spread) in spreads.items():
        noise = np.random.default_rng([zlib.crc32(name.encode()), seed]).standard_normal(out[name].shape)
        drawn = base * np.exp(spread * noise) if base else spread * noise
        out[name] = jnp.asarray(drawn.astype(out[name].dtype))
    for name, factor in factors.items():
        out[name] = (out[name] * factor).astype(out[name].dtype)
    return out
```

```python
from contextlib import ExitStack

import concourse.bass as bass
from concourse import mybir

ALU = mybir.AluOpType
ACT = mybir.ActivationFunctionType
AX = mybir.AxisListType
F32 = mybir.dt.float32
F16 = mybir.dt.float16
U32 = mybir.dt.uint32

P = 128
B, S, D = 8, 256, 512
DC = D // P
SC = DC * B
H = 2048
HC = H // P
E, TOPK = 8, 2
FC = HC // E
C = S
CT = C // P
NH, DH = 16, 16
BS = P // B
NB = S // BS

DT, EPS, ALPHA, BETA, CLAMP = 0.01, 0.08, 0.7, 0.8, 20.0
SHIFT = ALPHA / BETA
STEP = [DT / 2, DT / 2, DT, DT / 6]
WS = 64.0
CS = 256.0
NEG = 1e30


class Tally:

    def __init__(self, eng, sem, per, stop=None):
        self.eng, self.sem, self.per, self.stop = eng, sem, per, stop

    def start(self, turn):
        self.turn, self.k = turn, 0

    def then_wait(self, ins):
        ins.then_inc(self.sem, 1)
        self.k += 1
        self.eng.wait_ge(self.sem, self.turn * self.per + self.k)
        if self.stop is not None:
            self.eng.sem_inc(self.stop, 1)

    def finish(self):
        assert self.k == self.per, (self.k, self.per)


def oscillator_and_ffn(nc, drive, cond, bias, coup, had, w_up, w_down, x_tb, x1_dram, WU, WD):
    with ExitStack() as ctx:
        def sb(name, shape, dt=F32):
            return ctx.enter_context(nc.sbuf_tensor(name, shape, dt))

        def psum(name):
            return ctx.enter_context(nc.psum_tensor(name, [P, 512], F32))

        def sem(name):
            return ctx.enter_context(nc.semaphore(name))

        Dr = sb("Dr", [P, S, SC])
        XsMem = sb("XsMem", [P, 8192])
        Xs = XsMem[:, :].bitcast(F16).rearrange("p (a k t b) -> p a k t b", a=2, k=DC, b=B)
        W2m = XsMem[:, :].rearrange("p (c n) -> p c n", n=D)
        stage = sb("stage", [P, 8192])
        CW = sb("CW", [P, 2, DC, D], F16)
        hadS = sb("hadS", [P, P])
        condS = sb("condS", [P, SC])
        biasS = sb("biasS", [P, DC])
        biasM = sb("biasM", [P, DC])
        zero = sb("zero", [P, P], F16)
        qs = sb("qs", [P, 2, SC])
        Qb = sb("Qb", [P, 3, SC])
        Th = sb("Th", [P, 2, SC], F16)
        Tf = sb("Tf", [P, 2, SC])
        Tl = sb("Tl", [P, 2, SC], F16)
        t1 = sb("t1", [P, SC])
        t2 = sb("t2", [P, SC])
        Y = sb("Y", [P, SC])
        U = sb("U", [P, SC])
        Z = sb("Z", [P, SC])
        Cn = sb("Cn", [P, SC])
        G = sb("G", [P, 2, SC])
        M = sb("M", [P, 4, SC])
        w1 = sb("w1", [P, SC])
        w2 = sb("w2", [P, SC])
        zm = sb("zm", [P, SC])
        th, ga, hf = stage[:, 1024:1152], stage[:, 1152:1280], stage[:, 1280:1408]
        hid = sb("hid", [P, 2, P], F16)
        xres, x1t = stage[:, 0:D], stage[:, D:2 * D]

        icb = [psum("ic0"), psum("ic1")]
        gate_ps, up_ps, acc_ps = psum("gate_ps"), psum("up_ps"), psum("acc_ps")
        had_ps = [psum("had0"), psum("had1")]

        in_coup, in_drive, in_small, in_w2 = sem("in_coup"), sem("in_drive"), sem("in_small"), sem("in_w2")
        in_up = [sem("in_up0"), sem("in_up1")]
        up_hi, up_lo = sem("up_hi"), sem("up_lo")
        coup_hi, coup_lo, drive_ok, biasm_ok = sem("coup_hi"), sem("coup_lo"), sem("drive_ok"), sem("biasm_ok")
        had_done, had_out, butterfly, down_hi, down_lo = (sem("had_done"), sem("had_out"), sem("butterfly"),
                                                          sem("down_hi"), sem("down_lo"))
        zero_ok = sem("zero_ok")
        q_ready, tanh_hi, tanh_full, tanh_lo = sem("q_ready"), sem("tanh_hi"), sem("tanh_full"), sem("tanh_lo")
        ic_ready, rec_ready, xs_ready = sem("ic_ready"), sem("rec_ready"), sem("xs_ready")
        gate_done, up_done, th_done, hid_done, down_done = (sem("gate_done"), sem("up_done"), sem("th_done"),
                                                            sem("hid_done"), sem("down_done"))
        xres_in, evac, x1_out = sem("xres_in"), sem("evac"), sem("x1_out")
        dve_own, dve_ffn, pool_own = sem("dve_own"), sem("dve_ffn"), sem("pool_own")
        halt = sem("halt")

        block = ctx.enter_context(nc.Block())
        UPQ = HC // 4

        @block.sync
        def _(sp):
            sp.dma_start(stage[:, 0:DC * D], coup).then_inc(in_coup, 16)
            sp.dma_start(condS[:], cond).then_inc(in_small, 16)
            sp.dma_start(biasS[:], bias).then_inc(in_small, 16)
            sp.dma_start(hadS[:], had).then_inc(in_small, 16)
            sp.dma_start(Dr[:], drive).then_inc(in_drive, 16)
            sp.dma_start(W2m, w_down).then_inc(in_w2, 16)
            for n in range(4):
                if n < 2:
                    sp.wait_ge(coup_hi, 1)
                    sp.wait_ge(coup_lo, 1)
                else:
                    sp.wait_ge(up_hi, n - 1)
                    sp.wait_ge(up_lo, n - 1)
                sp.dma_start(stage[:, (n % 2) * 4096:(n % 2 + 1) * 4096],
                             w_up[:, n * 4096:(n + 1) * 4096]).then_inc(in_up[n % 2], 16)
            with sp.Fori(0, NB) as blk:
                sp.wait_ge(evac, blk + 1)
                sp.dma_start(xres, x_tb[blk]).then_inc(xres_in, 16)
                sp.wait_ge(evac, blk + 2)
                sp.dma_start(x1_dram[blk], x1t).then_inc(x1_out, 16)
                sp.wait_ge(x1_out, 16 * blk + 16)
                sp.sem_inc(halt, 1)

        @block.tensor
        def _(pe):
            pe.wait_ge(in_small, 48)
            pe.wait_ge(in_w2, 16)
            for c in range(HC):
                if c >= 2:
                    pe.wait_ge(had_out, c - 1)
                pe.matmul(had_ps[c % 2][:, :], hadS[:], W2m[:, c, :], start=True, stop=True).then_inc(had_done, 1)
            pe.wait_ge(coup_hi, 1)
            pe.wait_ge(coup_lo, 1)
            pe.wait_ge(zero_ok, 1)

            def couple(t, s):
                g = t * 4 + s
                out = icb[s % 2]
                pe.wait_ge(tanh_hi, g + 1)
                first = True
                for w in (0, 1):
                    for m in range(DC):
                        for k in range(DC):
                            pe.matmul(out[:, m * B:(m + 1) * B], CW[:, w, k, m * P:(m + 1) * P],
                                      Th[:, s % 2, k * B:(k + 1) * B], start=first, stop=False,
                                      skip_group_check=True)
                            first = False
                pe.wait_ge(tanh_lo, g + 1)
                for m in range(DC):
                    for k in range(DC):
                        last = pe.matmul(out[:, m * B:(m + 1) * B], CW[:, 0, k, m * P:(m + 1) * P],
                                         Tl[:, s % 2, k * B:(k + 1) * B], start=False, stop=(m == DC - 1 and k == DC - 1),
                                         skip_group_check=True)
                last.then_inc(ic_ready, 1)

            def project(t0, hc, which, out, done):
                pe.wait_ge(xs_ready, t0 + BS)
                n = 0
                for wp, xp in ((0, 0), (1, 0), (0, 1)):
                    for k in range(DC):
                        last = pe.matmul(out[:, 0:P], WU[:, hc, which, wp, k, :],
                                         Xs[:, xp, k, bass.ds(t0, BS), :], start=(n == 0), stop=(n == 3 * DC - 1))
                        n += 1
                last.then_inc(done, 1)

            def down(idx, hc):
                pe.wait_ge(hid_done, idx + 1)
                for hp, wp in ((0, 0), (0, 1), (1, 0)):
                    last = pe.matmul(acc_ps[:, :], hid[:, hp, :], WD[:, hc, wp, :], start=False, stop=False,
                                     skip_group_check=True)
                last.then_inc(down_done, 1)

            def clear(ob):
                pe.wait_ge(evac, ob)
                pe.matmul(acc_ps[:, :], zero[:], WD[:, 0, 0, :], start=True, stop=False, skip_group_check=True)

            with pe.Fori(0, BS // 2) as pair:
                for u in range(2):
                    for s in range(4):
                        couple(pair * 2 + u, s)
            pe.wait_ge(down_hi, 1)
            pe.wait_ge(down_lo, 1)
            pe.wait_ge(up_hi, 4)
            pe.wait_ge(up_lo, 4)
            with pe.Fori(1, NB) as ob:
                clear(ob)
                with pe.Fori(0, BS // 2) as pair:
                    for u in range(2):
                        hc = pair * 2 + u
                        t = ob * BS + hc
                        idx = t - BS
                        t0 = (ob - 1) * BS
                        couple(t, 0)
                        project(t0, hc, 0, gate_ps, gate_done)
                        couple(t, 1)
                        project(t0, hc, 1, up_ps, up_done)
                        couple(t, 2)
                        couple(t, 3)
                        down(idx, hc)
            clear(NB)
            with pe.Fori(0, HC) as hc:
                idx = hc + (NB - 1) * BS
                pe.wait_ge(hid_done, idx)
                project((NB - 1) * BS, hc, 0, gate_ps, gate_done)
                project((NB - 1) * BS, hc, 1, up_ps, up_done)
                down(idx, hc)

        @block.scalar
        def _(act):
            act.wait_ge(in_coup, 16)
            act.activation(CW[:, 0, :, :].rearrange("p k n -> p (k n)"), stage[:, 0:DC * D], ACT.Copy, scale=CS).then_inc(coup_hi, 1)
            act.wait_ge(in_drive, 16)
            act.wait_ge(biasm_ok, 1)
            for k in range(DC):
                v = Dr[:, :, k * B:(k + 1) * B]
                last = act.activation(v, v, ACT.Identity, bias=biasM[:, k:k + 1], scale=1.0)
            last.then_inc(drive_ok, 1)
            for c in range(HC):
                act.wait_ge(had_done, c + 1)
                act.activation(W2m[:, c, :], had_ps[c % 2][:, :], ACT.Copy).then_inc(had_out, 1)
            for n in range(4):
                act.wait_ge(in_up[n % 2], 16 * (n // 2 + 1))
                src = stage[:, (n % 2) * 4096:(n % 2 + 1) * 4096].rearrange("p (h w k m) -> p h w k m", h=UPQ, w=2, k=DC)
                for w in range(2):
                    last = act.activation(WU[:, n * UPQ:(n + 1) * UPQ, w, 0, :, :].rearrange("p h k m -> p h (k m)"),
                                          src[:, :, w].rearrange("p h k m -> p h (k m)"), ACT.Copy, scale=WS)
                last.then_inc(up_hi, 1)
            act.wait_ge(butterfly, 4)
            act.activation(WD[:, :, 0, :], W2m, ACT.Copy, scale=WS / H ** 0.5).then_inc(down_hi, 1)

            def tanhs(t, s):
                g = t * 4 + s
                src = Qb[:, s - 1, :] if s else qs[:, u, :]
                act.wait_ge(q_ready, g + 1)
                act.activation(Th[:, s % 2, :], src, ACT.Tanh).then_inc(tanh_hi, 1)
                act.activation(Tf[:, s % 2, :], src, ACT.Tanh).then_inc(tanh_full, 1)

            def gate_tanh(idx):
                act.wait_ge(gate_done, idx + 1)
                act.activation(th, gate_ps[:, 0:P], ACT.Tanh, scale=0.5 / WS).then_inc(th_done, 1)

            with act.Fori(0, BS // 2) as pair:
                for u in range(2):
                    for s in range(4):
                        tanhs(pair * 2 + u, s)
            with act.Fori(1, NB) as ob:
                with act.Fori(0, BS // 2) as pair:
                    for u in range(2):
                        t = ob * BS + pair * 2 + u
                        for s in range(4):
                            tanhs(t, s)
                            if s == 1:
                                gate_tanh(t - BS)
            with act.Fori(0, HC) as hc:
                gate_tanh(hc + (NB - 1) * BS)

        @block.vector
        def _(dve):
            own = Tally(dve, dve_own, 4 * 4 + 2 + 3)
            ffn = Tally(dve, dve_ffn, 3)
            dve.memset(zero[:], 0.0).then_inc(zero_ok, 1)
            dve.wait_ge(in_small, 48)
            dve.tensor_scalar_add(biasM[:], biasS[:], -SHIFT).then_inc(biasm_ok, 1)
            dve.tensor_copy(qs[:, 0, :], condS[:]).then_inc(q_ready, 1)
            dve.wait_ge(coup_hi, 1)
            dve.scalar_tensor_tensor(CW[:, 1, :, :].rearrange("p k n -> p (k n)"), stage[:, 0:DC * D], CS,
                                     CW[:, 0, :, :].rearrange("p k n -> p (k n)"), ALU.mult, ALU.subtract).then_inc(coup_lo, 1)
            for n in range(4):
                dve.wait_ge(up_hi, n + 1)
                src = stage[:, (n % 2) * 4096:(n % 2 + 1) * 4096].rearrange("p (h w k m) -> p h w k m", h=UPQ, w=2, k=DC)
                for w in range(2):
                    a = WU[:, n * UPQ:(n + 1) * UPQ, w].rearrange("p h a k m -> p h a (k m)")
                    last = dve.scalar_tensor_tensor(a[:, :, 1], src[:, :, w].rearrange("p h k m -> p h (k m)"), WS,
                                                    a[:, :, 0], ALU.mult, ALU.subtract)
                last.then_inc(up_lo, 1)
            dve.wait_ge(had_out, HC)
            dve.wait_ge(up_lo, 4)
            bufs = [XsMem[:, :], stage[:, :]]
            for lv in range(4):
                w = D << lv
                a = bufs[lv % 2].rearrange("p (g x w) -> p g x w", x=2, w=w)
                o = bufs[(lv + 1) % 2].rearrange("p (g x w) -> p g x w", x=2, w=w)
                dve.tensor_tensor(o[:, :, 0], a[:, :, 0], a[:, :, 1], ALU.add)
                dve.tensor_tensor(o[:, :, 1], a[:, :, 0], a[:, :, 1], ALU.subtract).then_inc(butterfly, 1)
                dve.wait_ge(butterfly, lv + 1)
            dve.wait_ge(down_hi, 1)
            dve.scalar_tensor_tensor(WD[:, :, 1, :], W2m, WS / H ** 0.5, WD[:, :, 0, :],
                                     ALU.mult, ALU.subtract).then_inc(down_lo, 1)
            dve.memset(stage[:, D:D + 1], 0.0).then_inc(evac, 1)

            def stage_ops(t, s, u):
                g = t * 4 + s
                q = qs[:, u, :]
                Q = Qb[:, s - 1, :] if s else q
                a = STEP[s]
                own.then_wait(dve.tensor_tensor(t1[:], Q, Q, ALU.mult))
                own.then_wait(dve.scalar_tensor_tensor(t2[:], t1[:], -3.0, Q, ALU.add, ALU.mult))
                dve.wait_ge(tanh_full, g + 1)
                dve.tensor_tensor(Tl[:, s % 2, :], Tf[:, s % 2, :], Th[:, s % 2, :], ALU.subtract).then_inc(tanh_lo, 1)
                dve.wait_ge(rec_ready, g + 1)
                if s == 1:
                    own.then_wait(dve.tensor_tensor(Z[:], Q, q, ALU.subtract))
                elif s == 2:
                    own.then_wait(dve.scalar_tensor_tensor(Z[:], Q, 2.0, Z[:], ALU.mult, ALU.add))
                if s < 3:
                    own.then_wait(dve.scalar_tensor_tensor(Y[:], G[:, s % 2, :], a, q, ALU.mult, ALU.add))
                else:
                    own.then_wait(dve.tensor_tensor(Z[:], Z[:], Q, ALU.add))
                    own.then_wait(dve.scalar_tensor_tensor(Y[:], G[:, s % 2, :], 3 * a, Z[:], ALU.mult, ALU.add))
                    own.then_wait(dve.tensor_scalar_mul(Y[:], Y[:], 1 / 3))
                own.then_wait(dve.scalar_tensor_tensor(U[:], t2[:], -a / 3, Y[:], ALU.mult, ALU.add))
                dve.wait_ge(ic_ready, g + 1)
                if s < 3:
                    dve.scalar_tensor_tensor(Qb[:, s, :], icb[s % 2][:, 0:SC], a / CS, U[:], ALU.mult, ALU.add).then_inc(q_ready, 1)
                else:
                    own.then_wait(dve.scalar_tensor_tensor(Cn[:], icb[s % 2][:, 0:SC], a / CS, U[:], ALU.mult, ALU.add))
                    dve.tensor_scalar(qs[:, 1 - u, :], Cn[:], CLAMP, -CLAMP, ALU.min, ALU.max).then_inc(q_ready, 1)
                dve.wait_ge(q_ready, g + 2)

            def hidden(idx):
                dve.wait_ge(th_done, idx + 1)
                ffn.then_wait(dve.scalar_tensor_tensor(ga, th, 1.0, gate_ps[:, 0:P], ALU.add, ALU.mult))
                dve.wait_ge(up_done, idx + 1)
                ffn.then_wait(dve.scalar_tensor_tensor(hf, ga, 0.5 / (WS * WS), up_ps[:, 0:P], ALU.mult, ALU.mult))

            def split_hidden(idx):
                ffn.then_wait(dve.tensor_copy(hid[:, 0, :], hf))
                dve.tensor_tensor(hid[:, 1, :], hf, hid[:, 0, :], ALU.subtract).then_inc(hid_done, 1)

            def block_out(ob):
                dve.wait_ge(down_done, ob * HC)
                dve.wait_ge(xres_in, 16 * ob)
                dve.scalar_tensor_tensor(x1t, acc_ps[:, :], 1 / WS, xres, ALU.mult, ALU.add).then_inc(evac, 1)

            with dve.Fori(0, BS // 2) as pair:
                for u in range(2):
                    own.start(pair * 2 + u)
                    for s in range(4):
                        stage_ops(pair * 2 + u, s, u)
                    own.finish()
            with dve.Fori(1, NB) as ob:
                with dve.Fori(0, BS // 2) as pair:
                    for u in range(2):
                        t = ob * BS + pair * 2 + u
                        own.start(t)
                        ffn.start(t - BS)
                        for s in range(4):
                            stage_ops(t, s, u)
                            if s == 1:
                                hidden(t - BS)
                            if s == 2:
                                split_hidden(t - BS)
                        own.finish()
                        ffn.finish()
                block_out(ob)
            dve.wait_ge(in_small, 48)
            with dve.Fori(0, HC) as hc:
                idx = hc + (NB - 1) * BS
                ffn.start(idx)
                hidden(idx)
                dve.wait_ge(down_done, idx)
                split_hidden(idx)
                ffn.finish()
            block_out(NB)

        @block.gpsimd
        def _(pool):
            own = Tally(pool, pool_own, 3 * 4 + 1 + 2 + 1 + 6 + 1, halt)
            pool.wait_ge(in_small, 48)
            pool.tensor_scalar(M[:, 0, :], condS[:], -1.0, SHIFT, ALU.mult, ALU.add).then_inc(zero_ok, 1)
            pool.wait_ge(zero_ok, 2)
            pool.wait_ge(drive_ok, 1)
            pool.tensor_tensor(G[:, 0, :], M[:, 0, :], Dr[:, 0, :], ALU.add).then_inc(rec_ready, 1)

            def recover(t, u, more):
                m = M[:, 0, :]
                for s in (1, 2, 3):
                    a = STEP[s - 1]
                    own.then_wait(pool.tensor_scalar_mul(w1[:], M[:, s - 1, :], -a * EPS * BETA))
                    own.then_wait(pool.tensor_tensor(w1[:], w1[:], m, ALU.add))
                    Q = Qb[:, s - 2, :] if s > 1 else qs[:, u, :]
                    pool.wait_ge(q_ready, t * 4 + s)
                    pool.sem_inc(halt, 1)
                    own.then_wait(pool.tensor_scalar_mul(w2[:], Q, -a * EPS))
                    own.then_wait(pool.tensor_tensor(M[:, s, :], w1[:], w2[:], ALU.add))
                    pool.tensor_tensor(G[:, s % 2, :], M[:, s, :], Dr[:, t, :], ALU.add).then_inc(rec_ready, 1)
                    if s == 1:
                        own.then_wait(pool.tensor_tensor(zm[:], M[:, 1, :], m, ALU.subtract))
                    elif s == 2:
                        own.then_wait(pool.tensor_tensor(zm[:], zm[:], M[:, 2, :], ALU.add))
                        own.then_wait(pool.tensor_tensor(zm[:], zm[:], M[:, 2, :], ALU.add))
                    else:
                        own.then_wait(pool.tensor_tensor(zm[:], zm[:], M[:, 3, :], ALU.add))
                own.then_wait(pool.tensor_scalar_mul(w1[:], M[:, 3, :], -DT / 6 * EPS * BETA))
                own.then_wait(pool.tensor_scalar_mul(zm[:], zm[:], 1 / 3))
                own.then_wait(pool.tensor_tensor(w1[:], w1[:], zm[:], ALU.add))
                pool.wait_ge(q_ready, t * 4 + 4)
                pool.sem_inc(halt, 1)
                own.then_wait(pool.tensor_scalar_mul(w2[:], Qb[:, 2, :], -DT / 6 * EPS))
                own.then_wait(pool.tensor_tensor(w1[:], w1[:], w2[:], ALU.add))
                own.then_wait(pool.tensor_scalar(M[:, 0, :], w1[:], CLAMP + SHIFT, SHIFT - CLAMP, ALU.min, ALU.max))
                if more:
                    pool.tensor_tensor(G[:, 0, :], M[:, 0, :], Dr[:, t + 1, :], ALU.add).then_inc(rec_ready, 1)

            def split_trace(t, u):
                pool.wait_ge(q_ready, t * 4 + 5)
                pool.sem_inc(halt, 1)
                q = qs[:, 1 - u, :].rearrange("p (k b) -> p k b", k=DC)
                own.then_wait(pool.tensor_copy(Xs[:, 0, :, t, :], q))
                pool.tensor_tensor(Xs[:, 1, :, t, :], q, Xs[:, 0, :, t, :], ALU.subtract).then_inc(xs_ready, 1)

            pool.wait_ge(down_lo, 1)
            with pool.Fori(0, S // 2 - 1) as pair:
                for u in range(2):
                    own.start(pair * 2 + u)
                    recover(pair * 2 + u, u, True)
                    split_trace(pair * 2 + u, u)
                    own.finish()
            for t in (S - 2, S - 1):
                own.start(t)
                recover(t, t % 2, t < S - 1)
                split_trace(t, t % 2)
                own.finish()


def attention(nc, x1_dram, qk_dram, mask, b0, w_qk, ident, moe_up, WU, YH, YL):
    qk_tiles = qk_dram.rearrange("b a o p s n -> b a o p s n")
    qk_heads = qk_dram.rearrange("b a o (j r d) s n -> b a o r s d j n", j=NH // 4, r=2)
    with ExitStack() as ctx:
        def sb(name, shape, dt=F32):
            return ctx.enter_context(nc.sbuf_tensor(name, shape, dt))

        def sem(name):
            return ctx.enter_context(nc.semaphore(name))

        V = sb("V", [P, B, DC, C])

        with ExitStack() as c1:
            def sb1(name, shape, dt=F32):
                return c1.enter_context(nc.sbuf_tensor(name, shape, dt))

            def sem1(name):
                return c1.enter_context(nc.semaphore(name))

            def psum1(name):
                return c1.enter_context(nc.psum_tensor(name, [P, 512], F32))

            wst = sb1("wst", [P, 3, CT, C])
            wsp = sb1("wsp", [P, 2, 3, CT, C], F16)
            xb = sb1("xb", [P, CT, D])
            xh = sb1("xh", [P, 2, CT, D], F16)
            mr = sb1("mr", [P, D])
            kf = sb1("kf", [P, D])
            qkp = sb1("qkp", [P, 2, 2, 2, D], F16)
            qp = [psum1(f"qp{i}") for i in range(2)]
            kp = [psum1(f"kp{i}") for i in range(2)]
            vp = [psum1(f"vp{i}") for i in range(4)]
            in_w, w_hi, w_lo = sem1("in_w"), sem1("w_hi"), sem1("w_lo")
            in_x, in_m, x_hi, x_lo = sem1("in_x"), sem1("in_m"), sem1("x_hi"), sem1("x_lo")
            q_mm, k_mm, v_mm = sem1("q_mm"), sem1("k_mm"), sem1("v_mm")
            q_hi, q_lo, k_full, k_hi, k_lo, v_out, qk_out = (sem1("q_hi"), sem1("q_lo"), sem1("k_full"), sem1("k_hi"),
                                                             sem1("k_lo"), sem1("v_out"), sem1("qk_out"))
            halt = sem1("halt")
            block = c1.enter_context(nc.Block())

            @block.sync
            def _(sp):
                sp.dma_start(wst[:], w_qk).then_inc(in_w, 16)
                with sp.Fori(0, B) as b:
                    sp.wait_ge(x_lo, b + 1)
                    sp.dma_start(xb[:], x1_dram[b]).then_inc(in_x, 16)
                    sp.wait_ge(k_full, 2 * b + 2)
                    sp.dma_start(mr[:], mask[b].partition_broadcast(P)).then_inc(in_m, 16)
                    for ot in range(2):
                        sp.wait_ge(q_lo, 2 * b + ot + 3)
                        sp.dma_start(qk_tiles[b, 0, ot], qkp[:, 0, ot]).then_inc(qk_out, 16)
                    for ot in range(2):
                        sp.wait_ge(k_lo, 2 * b + ot + 3)
                        sp.dma_start(qk_tiles[b, 1, ot], qkp[:, 1, ot]).then_inc(qk_out, 16)
                    sp.wait_ge(qk_out, 64 * b + 64)
                    sp.sem_inc(halt, 1)

            @block.tensor
            def _(pe):
                pe.wait_ge(w_lo, 1)
                pe.wait_ge(w_hi, 1)
                with pe.Fori(0, B) as b:
                    pe.wait_ge(x_hi, b + 1)
                    pe.wait_ge(x_lo, b + 2)
                    for which, ps, done in ((0, qp, q_mm), (1, kp, k_mm)):
                        pe.wait_ge(k_full if which else q_lo, 2 * b + 2)
                        for ot in range(2):
                            n = 0
                            for wp, xp in ((0, 0), (1, 0), (0, 1)):
                                for ct in range(CT):
                                    last = pe.matmul(ps[ot][:, :], wsp[:, wp, which, ct, ot * P:(ot + 1) * P],
                                                     xh[:, xp, ct, :], start=(n == 0), stop=(n == 5))
                                    n += 1
                            last.then_inc(done, 1)
                    pe.wait_ge(v_out, 4 * b + 4)
                    for kc in range(DC):
                        n = 0
                        for wp, xp in ((0, 0), (1, 0), (0, 1)):
                            for ct in range(CT):
                                last = pe.matmul(vp[kc][:, 0:C], xh[:, xp, ct, kc * P:(kc + 1) * P],
                                                 wsp[:, wp, 2, ct, :], start=(n == 0), stop=(n == 5))
                                n += 1
                        last.then_inc(v_mm, 1)

            @block.scalar
            def _(act):
                act.wait_ge(in_w, 16)
                act.activation(wsp[:, 0].rearrange("p a c n -> p (a c n)"), wst[:].rearrange("p a c n -> p (a c n)"), ACT.Copy, scale=WS).then_inc(w_hi, 1)
                act.sem_inc(v_out, DC)
                with act.Fori(0, B) as b:
                    act.wait_ge(in_x, 16 * b + 16)
                    act.activation(xh[:, 0].rearrange("p c n -> p (c n)"), xb[:].rearrange("p c n -> p (c n)"), ACT.Copy).then_inc(x_hi, 1)
                    for ot in range(2):
                        act.wait_ge(q_mm, 2 * b + ot + 1)
                        act.activation(qkp[:, 0, ot, 0, :], qp[ot][:, :], ACT.Copy, scale=1 / WS).then_inc(q_hi, 1)
                    for kc in range(DC):
                        act.wait_ge(v_mm, 4 * b + kc + 1)
                        act.activation(V[:, b, kc, :], vp[kc][:, 0:C], ACT.Copy, scale=1 / WS).then_inc(v_out, 1)

            @block.vector
            def _(dve):
                dve.wait_ge(w_hi, 1)
                dve.scalar_tensor_tensor(wsp[:, 1].rearrange("p a c n -> p (a c n)"), wst[:].rearrange("p a c n -> p (a c n)"), WS,
                                         wsp[:, 0].rearrange("p a c n -> p (a c n)"), ALU.mult, ALU.subtract).then_inc(w_lo, 1)
                dve.sem_inc(x_lo, 1)
                for s in (q_lo, k_full, k_lo):
                    dve.sem_inc(s, 2)
                with dve.Fori(0, B) as b:
                    dve.wait_ge(x_hi, b + 1)
                    dve.tensor_tensor(xh[:, 1], xb[:], xh[:, 0], ALU.subtract).then_inc(x_lo, 1)
                    for ot in range(2):
                        dve.wait_ge(q_hi, 2 * b + ot + 1)
                        dve.scalar_tensor_tensor(qkp[:, 0, ot, 1, :], qp[ot][:, :], 1 / WS, qkp[:, 0, ot, 0, :],
                                                 ALU.mult, ALU.subtract).then_inc(q_lo, 1)
                    dve.wait_ge(in_m, 16 * b + 16)
                    for ot in range(2):
                        dve.wait_ge(k_mm, 2 * b + ot + 1)
                        dve.wait_ge(k_lo, 2 * b + ot + 2)
                        dve.scalar_tensor_tensor(kf[:], kp[ot][:, :], -1 / (WS * DH ** 0.5), mr[:], ALU.mult, ALU.mult).then_inc(k_full, 1)
                        dve.wait_ge(k_full, 2 * b + ot + 3)
                        dve.tensor_copy(qkp[:, 1, ot, 0, :], kf[:]).then_inc(k_hi, 1)
                        dve.wait_ge(k_hi, 2 * b + ot + 1)
                        dve.tensor_tensor(qkp[:, 1, ot, 1, :], kf[:], qkp[:, 1, ot, 0, :], ALU.subtract).then_inc(k_lo, 1)

        idS = sb("idS", [P, P])
        QR = sb("QR", [P, NH // 2, D], F16)
        KR = sb("KR", [P, NH // 2, D], F16)
        mrow = sb("mrow", [P, D])
        mt = sb("mt", [P, 2, D])
        negC = sb("negC", [P, D])
        b0S = sb("b0S", [P, 1])
        negL = sb("negL", [P, 2, D])
        nM = sb("nM", [P, 4, DC])
        rs = sb("rs", [P, 4, DC])
        ri = sb("ri", [P, DC])
        Pr = sb("Pr", [P, 2, DC, D])
        PT = sb("PT", [P, 2, DC, D])
        yF = sb("yF", [P, DC, C])
        wstage = sb("wstage", [P, 2, 1024])
        Lps = [ctx.enter_context(nc.psum_tensor(f"Lps{i}", [P, 512], F32)) for i in range(2)]
        Tps = [ctx.enter_context(nc.psum_tensor(f"Tps{i}", [P, 512], F32)) for i in range(4)]
        Ops = [ctx.enter_context(nc.psum_tensor(f"Ops{i}", [P, DC, 128], F32)) for i in range(2)]
        in_id, qk_in = sem("in_id"), [sem("qk_in0"), sem("qk_in1")]
        in_mask, negc_t, negc_ok = sem("in_mask"), sem("negc_t"), sem("negc_ok")
        s_L, s_neg, s_exp, s_T, s_evA, s_evD, s_pv, s_norm, s_y, s_ri = (
            sem("s_L"), sem("s_neg"), sem("s_exp"), sem("s_T"), sem("s_evA"), sem("s_evD"), sem("s_pv"),
            sem("s_norm"), sem("s_y"), sem("s_ri"))
        s_yh, in_moe, moe_t, moe_hi, moe_lo = sem("s_yh"), [sem("in_moe0"), sem("in_moe1")], sem("moe_t"), sem("moe_hi"), sem("moe_lo")
        halt = sem("halt2")
        block = ctx.enter_context(nc.Block())

        AHEAD = 8

        def load_qk(sp, b, half):
            for tensor, dst in ((0, QR), (1, KR)):
                for par in range(2):
                    for slot in range(4):
                        part = slot % 2 if tensor == 0 else slot // 2
                        row = par * 64 + slot * 16
                        sp.dma_start(dst[row:row + 16, half * 4:(half + 1) * 4, :],
                                     qk_heads[b, tensor, half, par, part]).then_inc(qk_in[half], 16)

        QKI = 16 * 16

        @block.sync
        def _(sp):
            sp.dma_start(idS[:], ident).then_inc(in_id, 16)
            sp.dma_start(b0S[:], b0.partition_broadcast(P)).then_inc(in_id, 16)
            sp.dma_start(mrow[:], mask[0].partition_broadcast(P)).then_inc(in_mask, 16)
            for half in range(2):
                load_qk(sp, 0, half)
            with sp.Fori(0, B - 1) as b:
                sp.wait_ge(negc_ok, b + 1)
                sp.dma_start(mrow[:], mask[b + 1].partition_broadcast(P)).then_inc(in_mask, 16)
                for half in range(2):
                    sp.wait_ge(s_L, b * 64 + 32 * (half + 1))
                    load_qk(sp, b + 1, half)

        @block.gpsimd
        def _(pool):
            pool.sem_inc(s_y, 1)
            pool.wait_ge(in_id, 32)
            pool.sem_inc(halt, 1)

            def mask_terms(b):
                pool.wait_ge(in_mask, 16 * b + 16)
                pool.sem_inc(halt, 1)
                pool.tensor_scalar(mt[:, 0], mrow[:], -1.0, 1.0, ALU.mult, ALU.add).then_inc(negc_t, 1)
                pool.wait_ge(negc_t, 3 * b + 1)
                pool.sem_inc(halt, 1)
                pool.tensor_scalar_mul(mt[:, 0], mt[:, 0], NEG).then_inc(negc_t, 1)
                pool.tensor_scalar(mt[:, 1], mrow[:], b0S[:, 0:1], None, ALU.mult).then_inc(negc_t, 1)
                pool.wait_ge(negc_t, 3 * b + 3)
                pool.sem_inc(halt, 1)
                pool.wait_ge(s_neg, 64 * b + AHEAD)
                pool.sem_inc(halt, 1)
                pool.tensor_tensor(negC[:], mt[:, 0], mt[:, 1], ALU.subtract).then_inc(negc_ok, 1)

            with pool.Fori(0, B) as b:
                mask_terms(b)
                for j in range(2):
                    pool.dma_start(wstage[:, j], moe_up[b * 2 + j]).then_inc(in_moe[j], 16)
                for j in range(2):
                    n = b * 2 + j
                    w = wstage[:, j].rearrange("p (w k m) -> p w k m", w=2, k=DC)
                    pool.wait_ge(in_moe[j], 16 * b + 16)
                    pool.sem_inc(halt, 1)
                    pool.tensor_scalar_mul(wstage[:, j], wstage[:, j], WS).then_inc(moe_t, 1)
                    pool.wait_ge(moe_t, n + 1)
                    pool.sem_inc(halt, 1)
                    for which in range(2):
                        o = WU[:, n, which]
                        pool.tensor_copy(o[:, 0], w[:, which]).then_inc(moe_hi, 1)
                        pool.wait_ge(moe_hi, 2 * n + which + 1)
                        pool.sem_inc(halt, 1)
                        pool.tensor_tensor(o[:, 1], w[:, which], o[:, 0], ALU.subtract).then_inc(moe_lo, 1)
                pool.wait_ge(moe_lo, 4 * b + 4)
                pool.sem_inc(halt, 1)
                pool.wait_ge(s_norm, 16 * b + 16 + AHEAD)
                pool.sem_inc(halt, 1)
                pool.tensor_copy(YH[:, b], yF[:]).then_inc(s_yh, 1)
                pool.wait_ge(s_yh, b + 1)
                pool.sem_inc(halt, 1)
                pool.tensor_tensor(YL[:, b], yF[:], YH[:, b], ALU.subtract).then_inc(s_y, 1)

        @block.tensor
        def _(pe):
            for s in (s_T, s_pv):
                pe.sem_inc(s, AHEAD)
            pe.wait_ge(in_id, 32)

            def scores(b, h, qt):
                n = (b * NH + h) * DC + qt
                base = 64 * (h % 2)
                pe.wait_ge(s_neg, n - 1 + AHEAD)
                pe.matmul(Lps[qt % 2][:, :], QR[base:base + 64, h // 2, qt * P:(qt + 1) * P],
                          KR[base:base + 64, h // 2, :], start=True, stop=True).then_inc(s_L, 1)

            def transposes(b, h, kc):
                i = b * NH + h
                if kc == 0:
                    pe.wait_ge(s_exp, i * DC + DC + AHEAD)
                pe.wait_ge(s_evD if kc % 2 else s_evA, 2 * i + kc // 2 - 1 + AHEAD)
                for qt in range(DC):
                    last = pe.transpose(Tps[kc][:, qt * P:(qt + 1) * P], Pr[:, h % 2, qt, kc * P:(kc + 1) * P], idS[:])
                last.then_inc(s_T, 1)

            def values(b, h):
                i = b * NH + h
                pe.wait_ge(s_evA, 2 * i + 2 + AHEAD)
                pe.wait_ge(s_evD, 2 * i + 2 + AHEAD)
                pe.wait_ge(s_norm, i - 1 + AHEAD)
                for qt in range(DC):
                    for kc in range(DC):
                        last = pe.matmul(Ops[h % 2][:, qt, 0:DH], PT[:, h % 2, kc, qt * P:(qt + 1) * P],
                                         V[:, b, kc, h * DH:(h + 1) * DH], start=(kc == 0), stop=(kc == DC - 1))
                last.then_inc(s_pv, 1)

            with pe.Fori(0, B) as b:
                pe.wait_ge(qk_in[0], b * QKI + QKI)
                for h in range(NH + 2):
                    for qt in range(DC):
                        if h < NH:
                            if h == NH // 2 and qt == 0:
                                pe.wait_ge(qk_in[1], b * QKI + QKI)
                            scores(b, h, qt)
                        if 1 <= h <= NH:
                            transposes(b, h - 1, qt)
                    if h >= 2:
                        values(b, h - 2)

        def evacuate(eng, copy, b, h, kc, done):
            i = b * NH + h
            eng.wait_ge(s_T, i * DC + kc + 1 + AHEAD)
            eng.wait_ge(s_pv, i - 1 + AHEAD)
            copy(PT[:, h % 2, kc, :], Tps[kc][:, :]).then_inc(done, 1)

        @block.scalar
        def _(act):
            act.sem_inc(s_exp, AHEAD)
            act.sem_inc(s_evA, AHEAD)

            def exps(b, h, qt):
                i = b * NH + h
                n = i * DC + qt
                act.wait_ge(s_neg, n + 1 + AHEAD)
                if qt == 0:
                    act.wait_ge(s_T, i * DC - DC + AHEAD)
                act.activation(Pr[:, h % 2, qt, :], negL[:, qt % 2, :], ACT.Exp, bias=nM[:, h % 4, qt:qt + 1],
                               scale=-1.0, accum_out=rs[:, h % 4, qt:qt + 1]).then_inc(s_exp, 1)

            def copy(out, in_):
                return act.activation(out, in_, ACT.Copy)

            with act.Fori(0, B) as b:
                for h in range(NH + 1):
                    for qt in range(DC):
                        if h < NH:
                            exps(b, h, qt)
                        if h >= 1 and qt % 2 == 0:
                            evacuate(act, copy, b, h - 1, qt, s_evA)

        @block.vector
        def _(dve):
            for s in (s_neg, s_evD, s_norm):
                dve.sem_inc(s, AHEAD)

            def negate_and_max(b, h, qt):
                n = (b * NH + h) * DC + qt
                dve.wait_ge(s_L, n + 1)
                dve.wait_ge(s_exp, n - 1 + AHEAD)
                dve.sem_inc(halt, 1)
                dve.tensor_tensor_reduce(out=negL[:, qt % 2, :], in0=Lps[qt % 2][:, :], in1=negC[:], scale=1.0,
                                         scalar=3.0e38, op0=ALU.add, op1=ALU.min,
                                         accum_out=nM[:, h % 4, qt:qt + 1]).then_inc(s_neg, 1)

            def normalize(b, h):
                i = b * NH + h
                dve.wait_ge(s_pv, i + 1 + AHEAD)
                if h == 0:
                    dve.wait_ge(s_y, b + 1)
                dve.wait_ge(s_norm, i + AHEAD)
                dve.reciprocal(ri[:], rs[:, h % 4, :]).then_inc(s_ri, 1)
                dve.wait_ge(s_ri, i + 1)
                dve.tensor_tensor(yF[:, :, h * DH:(h + 1) * DH], Ops[h % 2][:, :, 0:DH],
                                  ri[:].unsqueeze(2).to_broadcast([P, DC, DH]), ALU.mult).then_inc(s_norm, 1)

            with dve.Fori(0, B) as b:
                dve.wait_ge(negc_ok, b + 1)
                for h in range(NH + 2):
                    for qt in range(DC):
                        if h < NH:
                            negate_and_max(b, h, qt)
                        if 1 <= h <= NH and qt % 2:
                            evacuate(dve, dve.tensor_copy, b, h - 1, qt, s_evD)
                    if h >= 2:
                        normalize(b, h - 2)


def experts(nc, x1_dram, router, w_down, iota, WU, WD, YH, YL, out):
    with ExitStack() as ctx:
        def sb(name, shape, dt=F32):
            return ctx.enter_context(nc.sbuf_tensor("moe_" + name, shape, dt))

        def sem(name):
            return ctx.enter_context(nc.semaphore("moe_" + name))

        def psum(name):
            return ctx.enter_context(nc.psum_tensor("moe_" + name, [P, 512], F32))

        TT = 4
        NG = B // 2
        dst = sb("dst", [P, HC, D])
        rst = sb("rst", [P, DC, E])
        rw = sb("rw", [P, 2, DC, E], F16)
        io = sb("io", [P, E])
        sc = sb("sc", [P, TT, E])
        top = sb("top", [P, TT, 8])
        idx = sb("idx", [P, TT, 8], U32)
        idf = sb("idf", [P, TT, 2])
        dif = sb("dif", [P, TT])
        ex = sb("ex", [P, TT])
        den = sb("den", [P, TT])
        wt = sb("wt", [P, 2, TT])
        c1 = sb("c1", [P, TT, E])
        comb = sb("comb", [P, TT, E])
        th = sb("th", [P, 2, 512])
        ga = sb("ga", [P, 512])
        hf = sb("hf", [P, 512])
        hid = sb("hid", [P, FC, 2, 512], F16)
        acc = sb("acc", [P, TT, D])
        gp = [psum("gp0"), psum("gp1")]
        up = [psum("up0"), psum("up1")]
        dp = [psum(f"dp{i}") for i in range(TT)]
        in_d, in_r, d_hi, d_lo, r_hi, r_lo = sem("in_d"), sem("in_r"), sem("d_hi"), sem("d_lo"), sem("r_hi"), sem("r_lo")
        sc_mm, dif_ok, ex_ok, comb_ok, own = sem("sc_mm"), sem("dif_ok"), sem("ex_ok"), sem("comb_ok"), sem("own_dve")
        g_mm, u_mm, th_ok, hid_ok, d_mm, folded = sem("g_mm"), sem("u_mm"), sem("th_ok"), sem("hid_ok"), sem("d_mm"), sem("folded")
        acc_in, stored, ffn_own, halt = sem("acc_in"), sem("stored"), sem("ffn_own"), sem("halt3")
        block = ctx.enter_context(nc.Block())

        @block.sync
        def _(sp):
            sp.dma_start(rst[:], router).then_inc(in_r, 16)
            sp.dma_start(io[:], iota).then_inc(in_r, 16)
            sp.dma_start(dst[:], w_down).then_inc(in_d, 16)
            with sp.Fori(0, NG) as g:
                for tt in range(TT):
                    sp.dma_start(acc[:, tt], x1_dram[g * 2 + tt // 2][:, tt % 2]).then_inc(acc_in, 16)
                for tt in range(TT):
                    sp.wait_ge(folded, (g * E + E) * TT + tt + 1)
                    sp.dma_start(out[g * 2 + tt // 2][:, tt % 2], acc[:, tt]).then_inc(stored, 16)
                sp.wait_ge(stored, (g * TT + TT) * 16)
                sp.sem_inc(halt, 1)

        @block.tensor
        def _(pe):
            pe.wait_ge(r_lo, 1)

            def gate_up(g, e, fc):
                n = (g * E + e) * FC + fc
                pe.wait_ge(hid_ok, n - FC + 1 + FC)
                for which, ps, done in ((0, gp[fc], g_mm), (1, up[fc], u_mm)):
                    k = 0
                    for wp, Yp in ((0, YH), (1, YH), (0, YL)):
                        for qt in range(DC):
                            last = pe.matmul(ps[:, :], WU[:, e * FC + fc, which, wp, qt, :],
                                             Yp[:, bass.ds(g * 2, 2), qt, :], start=(k == 0), stop=(k == 3 * DC - 1))
                            k += 1
                    last.then_inc(done, 1)

            def down(g, e):
                pe.wait_ge(hid_ok, (g * E + e) * FC + FC + FC)
                for tt in range(TT):
                    pe.wait_ge(folded, (g * E + e) * TT + tt + 1)
                    k = 0
                    for fc in range(FC):
                        for hp, wp in ((0, 0), (0, 1), (1, 0)):
                            last = pe.matmul(dp[tt][:, :], hid[:, fc, hp, tt * P:(tt + 1) * P], WD[:, e * FC + fc, wp, :],
                                             start=(k == 0), stop=(k == 3 * FC - 1))
                            k += 1
                    last.then_inc(d_mm, 1)

            with pe.Fori(0, NG) as g:
                pe.wait_ge(hid_ok, g * E * FC + FC)
                for tt in range(TT):
                    k = 0
                    for wp, Yp in ((0, YH), (1, YH), (0, YL)):
                        for qt in range(DC):
                            last = pe.matmul(gp[1][:, tt * E:(tt + 1) * E], Yp[:, g * 2 + tt // 2, qt, (tt % 2) * P:(tt % 2 + 1) * P],
                                             rw[:, wp, qt, :], start=(k == 0), stop=(k == 3 * DC - 1))
                            k += 1
                last.then_inc(sc_mm, 1)
                gate_up(g, 0, 0)
                pe.wait_ge(own, 8 * g + 1)
                pe.wait_ge(d_lo, 1)
                gate_up(g, 0, 1)
                with pe.Fori(1, E) as e:
                    gate_up(g, e, 0)
                    down(g, e - 1)
                    gate_up(g, e, 1)
                down(g, E - 1)

        @block.scalar
        def _(act):
            act.wait_ge(in_r, 32)
            act.activation(rw[:, 0].rearrange("p k e -> p (k e)"), rst[:].rearrange("p k e -> p (k e)"), ACT.Copy, scale=WS).then_inc(r_hi, 1)
            act.wait_ge(in_d, 16)
            act.activation(WD[:, :, 0, :], dst[:], ACT.Copy, scale=WS).then_inc(d_hi, 1)

            def gate_tanh(g, e, fc):
                n = (g * E + e) * FC + fc
                act.wait_ge(g_mm, n + 1)
                act.wait_ge(hid_ok, n + 1)
                act.activation(th[:, fc], gp[fc][:, :], ACT.Tanh, scale=0.5 / WS).then_inc(th_ok, 1)

            with act.Fori(0, NG) as g:
                act.wait_ge(dif_ok, g + 1)
                act.activation(ex[:], dif[:], ACT.Exp, scale=1 / WS).then_inc(ex_ok, 1)
                with act.Fori(0, E) as e:
                    for fc in range(FC):
                        gate_tanh(g, e, fc)

        @block.vector
        def _(dve):
            dve.wait_ge(in_r, 32)
            dve.wait_ge(r_hi, 1)
            dve.scalar_tensor_tensor(rw[:, 1].rearrange("p k e -> p (k e)"), rst[:].rearrange("p k e -> p (k e)"), WS,
                                     rw[:, 0].rearrange("p k e -> p (k e)"), ALU.mult, ALU.subtract).then_inc(r_lo, 1)
            dve.sem_inc(hid_ok, FC)
            dve.sem_inc(folded, TT)
            dve.wait_ge(d_hi, 1)
            dve.scalar_tensor_tensor(WD[:, :, 1, :], dst[:], WS, WD[:, :, 0, :], ALU.mult, ALU.subtract).then_inc(d_lo, 1)

            def route(g):
                k = [0]

                def step(ins):
                    ins.then_inc(own, 1)
                    k[0] += 1
                    dve.wait_ge(own, 8 * g + k[0])
                    dve.sem_inc(halt, 1)

                dve.wait_ge(sc_mm, g + 1)
                step(dve.tensor_copy(sc[:].rearrange("p t e -> p (t e)"), gp[1][:, 0:TT * E]))
                for tt in range(TT):
                    last = dve.max(top[:, tt], sc[:, tt])
                step(last)
                for tt in range(TT):
                    last = dve.max_index(idx[:, tt], top[:, tt], sc[:, tt])
                step(last)
                dve.tensor_tensor(dif[:], top[:, :, 1], top[:, :, 0], ALU.subtract).then_inc(dif_ok, 1)
                step(dve.tensor_copy(idf[:], idx[:, :, 0:2]))
                dve.wait_ge(ex_ok, g + 1)
                step(dve.tensor_scalar(den[:], ex[:], WS, WS, ALU.mult, ALU.add))
                step(dve.reciprocal(wt[:, 0], den[:]))
                step(dve.tensor_tensor(wt[:, 1], wt[:, 0], ex[:], ALU.mult))
                for tt in range(TT):
                    last = dve.tensor_scalar(c1[:, tt], io[:], idf[:, tt, 0:1], wt[:, 0, tt:tt + 1], ALU.is_equal, ALU.mult)
                    last = dve.tensor_scalar(comb[:, tt], io[:], idf[:, tt, 1:2], wt[:, 1, tt:tt + 1], ALU.is_equal, ALU.mult)
                step(last)
                dve.tensor_tensor(comb[:], comb[:], c1[:], ALU.add).then_inc(comb_ok, 1)
                dve.wait_ge(comb_ok, g + 1)

            def hidden(g, e, fc):
                n = (g * E + e) * FC + fc
                dve.wait_ge(th_ok, n + 1)
                dve.scalar_tensor_tensor(ga[:], th[:, fc], 1.0, gp[fc][:, :], ALU.add, ALU.mult).then_inc(ffn_own, 1)
                dve.wait_ge(ffn_own, 3 * n + 1)
                dve.wait_ge(u_mm, n + 1)
                dve.wait_ge(hid_ok, n + FC)
                dve.scalar_tensor_tensor(hf[:], ga[:], 0.5 / (WS * WS), up[fc][:, :], ALU.mult, ALU.mult).then_inc(ffn_own, 1)
                dve.wait_ge(ffn_own, 3 * n + 2)
                dve.tensor_copy(hid[:, fc, 0], hf[:]).then_inc(ffn_own, 1)
                dve.wait_ge(ffn_own, 3 * n + 3)
                dve.tensor_tensor(hid[:, fc, 1], hf[:], hid[:, fc, 0], ALU.subtract).then_inc(hid_ok, 1)

            def fold(g, e):
                for tt in range(TT):
                    n = (g * E + e) * TT + tt
                    dve.wait_ge(d_mm, n + 1)
                    dve.wait_ge(folded, n + 1)
                    dve.scalar_tensor_tensor(acc[:, tt], dp[tt][:, :], comb[:, tt, bass.ds(e, 1)],
                                             acc[:, tt], ALU.mult, ALU.add).then_inc(folded, 1)

            with dve.Fori(0, NG) as g:
                route(g)
                hidden(g, 0, 0)
                hidden(g, 0, 1)
                dve.wait_ge(acc_in, (g + 1) * TT * 16)
                dve.sem_inc(halt, 1)
                with dve.Fori(1, E) as e:
                    fold(g, e - 1)
                    hidden(g, e, 0)
                    hidden(g, e, 1)
                fold(g, E - 1)


def hadamard(n):
    import numpy as np
    h = np.ones((1, 1), np.float32)
    while h.shape[0] < n:
        h = np.block([[h, h], [h, -h]])
    return np.ascontiguousarray(h.astype(np.float32))


def lay_out(v):
    import numpy as np
    a = {k: np.asarray(x) for k, x in v.items()}
    c = np.ascontiguousarray

    def slices(gate, up):
        w = np.stack([gate, up], 1).reshape(HC, 2, P, DC, P)
        return c(w.transpose(4, 0, 1, 3, 2).reshape(P, HC * 2 * DC * P))

    x = a["x"]
    r = {
        "drive": c(x.reshape(B, S, DC, P).transpose(3, 1, 2, 0).reshape(P, S, SC)),
        "cond": c(a["cond_2048"].reshape(B, DC, P).transpose(2, 1, 0).reshape(P, SC)),
        "bias": c(a["L0_cond_bias"].reshape(DC, P).T),
        "coup": c(a["L0_cond_coupling"].T.reshape(DC, P, D).transpose(1, 0, 2).reshape(P, DC * D)),
        "had": hadamard(P),
        "w_up": slices(a["L0_ffn_W1"].reshape(HC, P, D), a["L0_ffn_W3"].reshape(HC, P, D)),
        "w_down": c(a["L0_ffn_W2"].T.reshape(HC, P, D).transpose(1, 0, 2)),
        "x_tb": c(x.transpose(1, 0, 2).reshape(NB, P, D)),
        "mask": c(a["cond_2048"]),
        "b0": c(a["L1_cond_b"].reshape(1)),
        "w_qkv": c(np.stack([a[n].T.reshape(CT, P, C) for n in ("L1_cond_Wq", "L1_cond_Wk", "L1_cond_Wv")], 1)
                   .transpose(2, 1, 0, 3)),
        "ident": np.eye(P, dtype=np.float32),
        "router": c(a["L1_ffn_router_w"].reshape(DC, P, E).transpose(1, 0, 2)),
        "moe_up": c(slices(a["L1_ffn_gate_proj"].transpose(0, 2, 1).reshape(HC, P, D),
                           a["L1_ffn_up_proj"].transpose(0, 2, 1).reshape(HC, P, D))
                    .reshape(P, HC, 2 * DC * P).transpose(1, 0, 2)),
        "moe_down": c(a["L1_ffn_down_proj"].reshape(HC, P, D).transpose(1, 0, 2)),
        "iota": np.broadcast_to(np.arange(E, dtype=np.float32), (P, E)).copy(),
    }
    return r


def build(nc, d, out):
    x1 = nc.dram_tensor("x1", (S, B, D), F32, kind="Internal").ap()
    qk = nc.dram_tensor("qk", (B, 2, 2, P, 2, D), F16, kind="Internal").ap()
    x1_blocks = x1.rearrange("(n t) b d -> n (t b) d", t=BS)
    x1_batch = x1.rearrange("(c p) b d -> b p c d", p=P)
    out_batch = out.rearrange("b (c p) d -> b p c d", p=P)
    with nc.sbuf_tensor("WU", [P, HC, 2, 2, DC, P], F16) as WU:
        with nc.sbuf_tensor("WD", [P, HC, 2, D], F16) as WD:
            oscillator_and_ffn(nc, d["drive"], d["cond"], d["bias"], d["coup"], d["had"], d["w_up"], d["w_down"],
                               d["x_tb"], x1_blocks, WU, WD)
        with nc.sbuf_tensor("YH", [P, B, DC, C], F16) as YH, nc.sbuf_tensor("YL", [P, B, DC, C], F16) as YL:
            attention(nc, x1_batch, qk, d["mask"], d["b0"], d["w_qkv"], d["ident"], d["moe_up"], WU, YH, YL)
            with nc.sbuf_tensor("WE", [P, HC, 2, D], F16) as WE:
                experts(nc, x1_batch, d["router"], d["moe_down"], d["iota"], WU, WE, YH, YL, out_batch)


def kernel(**inputs):
    import concourse.bacc as bacc
    from concourse.bass_utils import run_bass_kernel_spmd

    nc = bacc.Bacc("TRN2", target_bir_lowering=False, num_devices=1)
    arrays = lay_out(inputs)
    d = {n: nc.dram_tensor(n, a.shape, F32, kind="ExternalInput").ap() for n, a in arrays.items()}
    out = nc.dram_tensor("out", (B, S, D), F32, kind="ExternalOutput").ap()
    build(nc, d, out)
    return run_bass_kernel_spmd(nc, [arrays], core_ids=[0]).results[0]["out"]
```

```python
from contextlib import ExitStack

import concourse.bass as bass
from concourse import mybir

ALU = mybir.AluOpType
ACT = mybir.ActivationFunctionType
AX = mybir.AxisListType
F32 = mybir.dt.float32
F16 = mybir.dt.float16
U32 = mybir.dt.uint32

P = 128
B, S, D = 8, 256, 512
DC = D // P
SC = DC * B
H = 2048
HC = H // P
E, TOPK = 8, 2
FC = HC // E
C = S
CT = C // P
NH, DH = 16, 16
BS = P // B
NB = S // BS

DT, EPS, ALPHA, BETA, CLAMP = 0.01, 0.08, 0.7, 0.8, 20.0
SHIFT = ALPHA / BETA
STEP = [DT / 2, DT / 2, DT, DT / 6]
WS = 64.0
CS = 256.0
NEG = 1e30


class Tally:

    def __init__(self, eng, sem, per, stop=None):
        self.eng, self.sem, self.per, self.stop = eng, sem, per, stop

    def start(self, turn):
        self.turn, self.k = turn, 0

    def mark(self, ins):
        ins.then_inc(self.sem, 1)
        self.k += 1
        return self.turn * self.per + self.k

    def then_wait(self, ins):
        self.eng.wait_ge(self.sem, self.mark(ins))
        if self.stop is not None:
            self.eng.sem_inc(self.stop, 1)

    def finish(self):
        assert self.k == self.per, (self.k, self.per)


def oscillator_and_ffn(nc, drive, cond, bias, coup, had, w_up, w_down, x_tb, x1_dram, WU, WD):
    with ExitStack() as ctx:
        def sb(name, shape, dt=F32):
            return ctx.enter_context(nc.sbuf_tensor(name, shape, dt))

        def psum(name):
            return ctx.enter_context(nc.psum_tensor(name, [P, 512], F32))

        def sem(name):
            return ctx.enter_context(nc.semaphore(name))

        PIECE = 2
        PW = 2 * DC * P
        Dr = sb("Dr", [P, S, SC])
        W2m = sb("W2m", [P, HC, D])
        stage = sb("stage", [P, 2, PIECE * PW])
        CW = sb("CW", [P, 2, DC, D], F16)
        hadS = sb("hadS", [P, P])
        condS = sb("condS", [P, SC])
        biasS = sb("biasS", [P, DC])
        biasM = sb("biasM", [P, DC])
        zero = sb("zero", [P, P], F16)
        X = sb("X", [P, 5, 2 * SC])
        T = sb("T", [P, 2, DC, 2, B], F16)
        Tf = sb("Tf", [P, 2, SC])
        t1 = sb("t1", [P, SC])
        t2 = sb("t2", [P, SC])
        F = sb("F", [P, 2 * SC])
        Z = sb("Z", [P, 2 * SC])
        W = sb("W", [P, 2 * SC])
        xsum = sb("xsum", [P, D])
        part = sb("part", [P, SC])
        Cn = sb("Cn", [P, SC])
        G = sb("G", [P, 2, SC])
        gt = sb("gt", [P, SC])
        Xb = sb("Xb", [P, 2, DC, BS, B], F16)
        Xa = sb("Xa", [P, 2, DC, BS * B], F16)
        hid = sb("hid", [P, 2, P], F16)
        free = stage[:, 0, :]
        xres, x1t = free[:, 0:D], free[:, D:2 * D]
        th, ga, hf = free[:, 1024:1152], free[:, 1152:1280], free[:, 1280:1408]
        WDf = WD[:, :, :, :].rearrange("p h a n -> p (h a n)").bitcast(F32)

        icb = [psum("ic0"), psum("ic1")]
        gate_ps, up_ps, acc_ps = [psum("gate0"), psum("gate1")], [psum("up0"), psum("up1")], psum("acc_ps")
        had_ps = up_ps

        in_coup, in_drive0, in_drive, in_small, in_w2 = (sem("in_coup"), sem("in_drive0"), sem("in_drive"),
                                                         sem("in_small"), sem("in_w2"))
        in_up = [sem("in_up0"), sem("in_up1")]
        up_hi, up_lo = sem("up_hi"), sem("up_lo")
        coup_hi, coup_lo, drive_ok, biasm_ok = sem("coup_hi"), sem("coup_lo"), sem("drive_ok"), sem("biasm_ok")
        had_done, butterfly, down_hi, down_lo = sem("had_done"), sem("butterfly"), sem("down_hi"), sem("down_lo")
        zero_ok = sem("zero_ok")
        n_ready, n_state, drive_ready, q_state = sem("n_ready"), sem("n_state"), sem("drive_ready"), sem("q_state")
        q_ready, tanh_hi, tanh_full, tanh_lo = sem("q_ready"), sem("tanh_hi"), sem("tanh_full"), sem("tanh_lo")
        ic_ready, xs_ready, xa_ready = sem("ic_ready"), sem("xs_ready"), sem("xa_ready")
        gate_done, up_done, th_done, hf_done, hid_done, down_done = (
            sem("gate_done"), sem("up_done"), sem("th_done"), sem("hf_done"), sem("hid_done"), sem("down_done"))
        xres_in, evac, sum_out, hid_hi, x1_out = sem("xres_in"), sem("evac"), sem("sum_out"), sem("hid_hi"), sem("x1_out")
        dve_own, dve_ffn, pool_own, trace_hi = sem("dve_own"), sem("dve_ffn"), sem("pool_own"), sem("trace_hi")
        halt = sem("halt")

        block = ctx.enter_context(nc.Block())

        @block.sync
        def _(sp):
            sp.dma_start(W2m[:, 0:DC, :], coup).then_inc(in_coup, 16)
            sp.dma_start(condS[:], cond).then_inc(in_small, 16)
            sp.dma_start(biasS[:], bias).then_inc(in_small, 16)
            sp.dma_start(hadS[:], had).then_inc(in_small, 16)
            sp.dma_start(Dr[:, 0:BS, :], drive[:, 0:BS, :]).then_inc(in_drive0, 16)
            sp.wait_ge(coup_hi, 1)
            sp.wait_ge(coup_lo, 1)
            sp.dma_start(W2m[:], w_down).then_inc(in_w2, 16)
            sp.dma_start(stage[:, 0], w_up[:, 0:PIECE * PW]).then_inc(in_up[0], 16)
            sp.dma_start(Dr[:, BS:S, :], drive[:, BS:S, :]).then_inc(in_drive, 16)
            for n in range(1, HC // PIECE):
                if n >= 2:
                    sp.wait_ge(up_lo, 2 * PIECE * (n - 1))
                sp.dma_start(stage[:, n % 2], w_up[:, n * PIECE * PW:(n + 1) * PIECE * PW]).then_inc(in_up[n % 2], 16)
            with sp.Fori(0, NB) as blk:
                sp.wait_ge(evac, blk + 1)
                sp.dma_start(xres, x_tb[blk]).then_inc(xres_in, 16)
                sp.wait_ge(evac, blk + 2)
                sp.dma_start(x1_dram[blk], x1t).then_inc(x1_out, 16)
                sp.wait_ge(x1_out, 16 * blk + 16)
                sp.sem_inc(halt, 1)

        @block.tensor
        def _(pe):
            pe.wait_ge(coup_hi, 1)
            pe.wait_ge(coup_lo, 1)
            pe.wait_ge(zero_ok, 1)
            pe.wait_ge(in_small, 48)

            def couple(t, s):
                g = t * 4 + s
                out = icb[s % 2]
                pe.wait_ge(tanh_hi, g + 1)
                for m in range(DC):
                    for k in range(DC):
                        pe.matmul(out[:, m * 2 * B:m * 2 * B + B], CW[:, 1, k, m * P:(m + 1) * P],
                                  T[:, s % 2, k, 0, :], start=(m == 0 and k == 0), stop=False, skip_group_check=True)
                pe.wait_ge(tanh_lo, g + 1)
                for m in range(DC):
                    for k in range(DC):
                        last = pe.matmul(out[:, m * 2 * B:(m + 1) * 2 * B], CW[:, 0, k, m * P:(m + 1) * P],
                                         T[:, s % 2, k, :, :], start=False, stop=(m == DC - 1 and k == DC - 1),
                                         skip_group_check=True)
                last.then_inc(ic_ready, 1)

            PRODUCTS = [(wp, xp, k) for wp, xp in ((0, 0), (1, 0), (0, 1)) for k in range(DC)]

            def project(fb, hc, which, first, last):
                out, done = (up_ps if which else gate_ps)[hc % 2], up_done if which else gate_done
                if first == 0:
                    pe.wait_ge(xa_ready, fb + 1)
                for n in range(first, last):
                    wp, xp, k = PRODUCTS[n]
                    ins = pe.matmul(out[:, 0:P], WU[:, hc, which, wp, k, :], Xa[:, xp, k, :],
                                    start=(n == 0), stop=(n == 3 * DC - 1))
                if last == 3 * DC:
                    ins.then_inc(done, 1)

            def down(idx, hc, parts):
                for n in parts:
                    hp, wp = ((0, 0), (0, 1), (1, 0))[n]
                    pe.wait_ge(hid_done if hp else hid_hi, idx + 1)
                    ins = pe.matmul(acc_ps[:, :], hid[:, hp, :], WD[:, hc, wp, :], start=False, stop=False,
                                    skip_group_check=True)
                if 2 in parts:
                    ins.then_inc(down_done, 1)

            def clear(fb):
                pe.wait_ge(sum_out, fb + 1)
                pe.matmul(acc_ps[:, :], zero[:], WD[:, 0, 0, :], start=True, stop=False, skip_group_check=True)

            def transform(c):
                if c == 0:
                    pe.wait_ge(butterfly, 32)
                if c >= 2:
                    pe.wait_ge(down_lo, c - 1)
                pe.matmul(had_ps[c % 2][:, :], hadS[:], W2m[:, c, :], start=True, stop=True).then_inc(had_done, 1)

            for t in range(BS):
                for s in range(4):
                    couple(t, s)
                    if t >= BS // 2 and s % 2 == 0:
                        transform((t - BS // 2) * 2 + s // 2)
            pe.wait_ge(down_hi, HC)
            pe.wait_ge(down_lo, HC)
            pe.wait_ge(up_hi, 2 * HC)
            pe.wait_ge(up_lo, 2 * HC)

            def block_steps(ob, first):
                for hc in range(HC):
                    t = ob * BS + hc
                    prev = not (first and hc == 0)
                    couple(t, 0)
                    project(ob - 1, hc, 0, 0, 9)
                    couple(t, 1)
                    project(ob - 1, hc, 0, 9, 12)
                    project(ob - 1, hc, 1, 0, 6)
                    couple(t, 2)
                    project(ob - 1, hc, 1, 6, 11)
                    if hc == 1:
                        clear(ob - 1)
                    if prev:
                        down(t - BS - 1, (hc - 1) % HC, (0,))
                    couple(t, 3)
                    project(ob - 1, hc, 1, 11, 12)
                    if prev:
                        down(t - BS - 1, (hc - 1) % HC, (1, 2))

            block_steps(1, True)
            with pe.Fori(2, NB) as ob:
                block_steps(ob, False)
            for hc in range(HC + 1):
                idx = hc + (NB - 1) * BS
                if hc < HC:
                    if hc > 1:
                        pe.wait_ge(hid_done, idx - 1)
                    project(NB - 1, hc, 0, 0, 12)
                    project(NB - 1, hc, 1, 0, 12)
                if hc == 1:
                    clear(NB - 1)
                down(idx - 1, (hc - 1) % HC, (0, 1, 2))

        @block.scalar
        def _(act):
            act.wait_ge(in_coup, 16)
            act.activation(CW[:, 0, :, :].rearrange("p k n -> p (k n)"), W2m[:, 0:DC, :].rearrange("p k n -> p (k n)"),
                           ACT.Copy, scale=CS).then_inc(coup_hi, 1)
            act.wait_ge(biasm_ok, 1)

            def add_bias(t0, steps):
                for k in range(DC):
                    v = Dr[:, t0:t0 + steps, k * B:(k + 1) * B]
                    last = act.activation(v, v, ACT.Identity, bias=biasM[:, k:k + 1], scale=1.0)
                last.then_inc(drive_ok, 1)

            act.wait_ge(in_drive0, 16)
            add_bias(0, BS)

            def up_high(hc, which):
                act.wait_ge(in_up[hc // PIECE % 2], 16 * (hc // PIECE // 2 + 1))
                w = stage[:, hc // PIECE % 2, :].rearrange("p (h w n) -> p h w n", h=PIECE, w=2)
                act.activation(WU[:, hc, which, 0, :, :].rearrange("p k m -> p (k m)"), w[:, hc % PIECE, which],
                               ACT.Copy, scale=WS).then_inc(up_hi, 1)

            def down_high(c):
                act.wait_ge(had_done, c + 1)
                act.activation(WD[:, c, 0, :], had_ps[c % 2][:, :], ACT.Copy, scale=WS / H ** 0.5).then_inc(down_hi, 1)

            def tanhs(t, s):
                g = t * 4 + s
                src = X[:, 1 + s, 0:SC] if s else Cn[:]
                act.wait_ge(q_ready, g + 1)
                act.activation(T[:, s % 2, :, 0, :], src.rearrange("p (k b) -> p k b", k=DC), ACT.Tanh).then_inc(tanh_hi, 1)
                act.activation(Tf[:, s % 2, :], src, ACT.Tanh).then_inc(tanh_full, 1)

            def gate_tanh(idx, hc):
                act.wait_ge(gate_done, idx + 1)
                act.activation(th, gate_ps[hc % 2][:, 0:P], ACT.Tanh, scale=0.5 / WS).then_inc(th_done, 1)

            def hidden_high(idx):
                act.wait_ge(hf_done, idx + 1)
                act.activation(hid[:, 0, :], hf, ACT.Copy).then_inc(hid_hi, 1)

            def sum_copy(fb):
                act.wait_ge(down_done, (fb + 1) * HC)
                act.wait_ge(evac, fb + 1)
                act.activation(xsum[:], acc_ps[:, :], ACT.Copy, scale=1 / WS).then_inc(sum_out, 1)

            for t in range(BS):
                for s in range(4):
                    tanhs(t, s)
                    if s < 2:
                        up_high(t, s)
                    if s == 2 and t > 0:
                        if t == 1:
                            act.wait_ge(in_drive, 16)
                        add_bias(t * BS, BS)
                    if t >= BS // 2 and s % 2 == 1:
                        down_high((t - BS // 2) * 2 + s // 2)
            act.sem_inc(sum_out, 1)

            def block_steps(ob, first):
                for hc in range(HC):
                    t = ob * BS + hc
                    for s in range(4):
                        tanhs(t, s)
                        if s == 1:
                            if hc == 1 and not first:
                                sum_copy(ob - 2)
                            if not (first and hc == 0):
                                hidden_high(t - BS - 1)
                        if s == 2:
                            gate_tanh(t - BS, hc)

            block_steps(1, True)
            with act.Fori(2, NB) as ob:
                block_steps(ob, False)
            for hc in range(HC + 1):
                idx = hc + (NB - 1) * BS
                act.wait_ge(down_done, idx - 1)
                hidden_high(idx - 1)
                if hc == 1:
                    sum_copy(NB - 2)
                if hc < HC:
                    gate_tanh(idx, hc)
            sum_copy(NB - 1)

        @block.vector
        def _(dve):
            own = Tally(dve, dve_own, 3 * 4 + 3 + 1 + 4 + 4)
            ffn = Tally(dve, dve_ffn, 1)
            dve.memset(zero[:], 0.0).then_inc(zero_ok, 1)
            dve.wait_ge(in_small, 48)
            dve.tensor_scalar_add(biasM[:], biasS[:], -SHIFT).then_inc(biasm_ok, 1)
            dve.tensor_scalar(X[:, 0, SC:2 * SC], condS[:], 1 / EPS, -SHIFT / EPS, ALU.mult, ALU.add).then_inc(n_ready, 1)
            dve.wait_ge(n_ready, 1)
            dve.sem_inc(n_state, 1)
            dve.tensor_copy(X[:, 0, 0:SC], condS[:]).then_inc(q_state, 1)
            dve.tensor_copy(Cn[:], condS[:]).then_inc(q_ready, 1)
            dve.wait_ge(q_ready, 1)
            dve.wait_ge(coup_hi, 1)
            dve.scalar_tensor_tensor(CW[:, 1, :, :].rearrange("p k n -> p (k n)"), W2m[:, 0:DC, :].rearrange("p k n -> p (k n)"), CS,
                                     CW[:, 0, :, :].rearrange("p k n -> p (k n)"), ALU.mult, ALU.subtract).then_inc(coup_lo, 1)

            def up_low(hc, which):
                dve.wait_ge(up_hi, 2 * hc + which + 1)
                w = stage[:, hc // PIECE % 2, :].rearrange("p (h w n) -> p h w n", h=PIECE, w=2)
                o = WU[:, hc, which].rearrange("p a k m -> p a (k m)")
                dve.scalar_tensor_tensor(o[:, 1], w[:, hc % PIECE, which], WS, o[:, 0], ALU.mult, ALU.subtract).then_inc(up_lo, 1)

            def down_low(c):
                dve.wait_ge(down_hi, c + 1)
                dve.scalar_tensor_tensor(WD[:, c, 1, :], had_ps[c % 2][:, :], WS / H ** 0.5, WD[:, c, 0, :],
                                         ALU.mult, ALU.subtract).then_inc(down_lo, 1)

            def stage_ops(t, s, u):
                g = t * 4 + s
                a = STEP[s]
                start, here = X[:, u, :], X[:, 1 + s if s else u, :]
                Q, n = here[:, 0:SC], here[:, SC:2 * SC]
                square = own.mark(dve.tensor_tensor(t1[:], Q, Q, ALU.mult))
                if s == 0:
                    dve.wait_ge(n_state, t + 1)
                fn = own.mark(dve.scalar_tensor_tensor(F[:, SC:2 * SC], n, -BETA * EPS, Q, ALU.mult, ALU.add))
                dve.wait_ge(dve_own, square)
                cube = own.mark(dve.scalar_tensor_tensor(t2[:], t1[:], -3.0, Q, ALU.add, ALU.mult))
                if s == 1:
                    z = own.mark(dve.tensor_tensor(Z[:], here, start, ALU.subtract))
                elif s == 2:
                    z = own.mark(dve.scalar_tensor_tensor(Z[:], here, 2.0, Z[:], ALU.mult, ALU.add))
                elif s == 3:
                    z = own.mark(dve.tensor_tensor(Z[:], Z[:], here, ALU.add))
                dve.wait_ge(tanh_full, g + 1)
                dve.tensor_tensor(T[:, s % 2, :, 1, :], Tf[:, s % 2, :].rearrange("p (k b) -> p k b", k=DC),
                                  T[:, s % 2, :, 0, :], ALU.subtract).then_inc(tanh_lo, 1)
                dve.wait_ge(drive_ready, g + 1)
                dve.wait_ge(dve_own, z if s else cube)
                own.then_wait(dve.scalar_tensor_tensor(F[:, 0:SC], t2[:], -1 / 3, G[:, s % 2, :], ALU.mult, ALU.add))
                if s < 3:
                    dve.scalar_tensor_tensor(X[:, 2 + s, :], F[:], a, start, ALU.mult, ALU.add).then_inc(n_ready, 1)
                else:
                    own.then_wait(dve.scalar_tensor_tensor(W[:], F[:], 3 * a, Z[:], ALU.mult, ALU.add))
                    dve.tensor_scalar_mul(W[:], W[:], 1 / 3).then_inc(n_ready, 1)

            def stage_end(t, s, u):
                a = STEP[s] / CS
                ic = icb[s % 2][:, 0:2 * SC].rearrange("p (k x b) -> p k x b", k=DC, x=2)
                v = part[:].rearrange("p (k b) -> p k b", k=DC)
                base = X[:, 2 + s, 0:SC] if s < 3 else W[:, 0:SC]
                out = X[:, 2 + s, 0:SC] if s < 3 else Cn[:]
                dve.wait_ge(n_ready, t * 4 + s + 2)
                dve.wait_ge(ic_ready, t * 4 + s + 1)
                own.then_wait(dve.scalar_tensor_tensor(v, ic[:, :, 1, :], a, base.rearrange("p (k b) -> p k b", k=DC),
                                                       ALU.mult, ALU.add))
                dve.scalar_tensor_tensor(out.rearrange("p (k b) -> p k b", k=DC), ic[:, :, 0, :], a, v,
                                         ALU.mult, ALU.add).then_inc(q_ready, 1)
                dve.wait_ge(q_ready, t * 4 + s + 2)
                if s == 3:
                    dve.tensor_scalar(X[:, 1 - u, 0:SC], Cn[:], CLAMP, -CLAMP, ALU.min, ALU.max).then_inc(q_state, 1)
                    dve.wait_ge(q_state, t + 2)

            def take_block(fb, first=False):
                dve.wait_ge(xs_ready, (fb + 1) * BS)
                if not first:
                    dve.wait_ge(up_done, fb * HC)
                dve.tensor_copy(Xa[:].rearrange("p a k n -> p (a k n)"),
                                Xb[:].rearrange("p a k t b -> p (a k t b)")).then_inc(xa_ready, 1)

            def gated(idx, hc):
                dve.wait_ge(th_done, idx + 1)
                ffn.start(idx)
                return ffn.mark(dve.scalar_tensor_tensor(ga, th, 1.0, gate_ps[hc % 2][:, 0:P], ALU.add, ALU.mult))

            def hidden(idx, hc):
                dve.wait_ge(dve_ffn, idx + 1)
                dve.wait_ge(up_done, idx + 1)
                dve.scalar_tensor_tensor(hf, ga, 0.5 / (WS * WS), up_ps[hc % 2][:, 0:P], ALU.mult, ALU.mult).then_inc(hf_done, 1)

            def hidden_low(idx):
                dve.wait_ge(hid_hi, idx + 1)
                dve.tensor_tensor(hid[:, 1, :], hf, hid[:, 0, :], ALU.subtract).then_inc(hid_done, 1)

            for t in range(BS):
                own.start(t)
                for s in range(4):
                    stage_ops(t, s, t % 2)
                    if s in (1, 2):
                        up_low(t, s - 1)
                    if t >= BS // 2 and s % 2 == 1:
                        down_low((t - BS // 2) * 2 + s // 2)
                    stage_end(t, s, t % 2)
                own.finish()

            def block_steps(ob, first):
                for hc in range(HC):
                    t = ob * BS + hc
                    prev = not (first and hc == 0)
                    own.start(t)
                    for s in range(4):
                        stage_ops(t, s, hc % 2)
                        if s == 0 and prev:
                            hidden(t - BS - 1, hc - 1)
                        if s == 0 and hc == 0:
                            take_block(ob - 1, first)
                        if s == 1 and prev:
                            hidden_low(t - BS - 1)
                        if s == 2:
                            gated(t - BS, hc)
                        stage_end(t, s, hc % 2)
                    own.finish()

            block_steps(1, True)
            with dve.Fori(2, NB) as ob:
                block_steps(ob, False)
            take_block(NB - 1)
            for hc in range(HC + 1):
                idx = hc + (NB - 1) * BS
                hidden(idx - 1, hc - 1)
                hidden_low(idx - 1)
                if hc < HC:
                    gated(idx, hc)

        @block.gpsimd
        def _(pool):
            own = Tally(pool, pool_own, 4, halt)

            def net_drive(t, s, u):
                n = X[:, 1 + s if s else u, SC:2 * SC]
                pool.wait_ge(n_ready, t * 4 + s + 1)
                pool.sem_inc(halt, 1)
                if s == 0 and not (isinstance(t, int) and t == 0):
                    pool.tensor_scalar(n, W[:, SC:2 * SC], (CLAMP - SHIFT) / EPS, (-CLAMP - SHIFT) / EPS,
                                       ALU.min, ALU.max).then_inc(n_state, 1)
                    pool.wait_ge(n_state, t + 1)
                    pool.sem_inc(halt, 1)
                own.then_wait(pool.tensor_scalar_mul(gt[:], n, -EPS))
                pool.tensor_tensor(G[:, s % 2, :], gt[:], Dr[:, t, :], ALU.add).then_inc(drive_ready, 1)

            def split_trace(t, hc, u):
                pool.wait_ge(q_state, t + 2)
                pool.sem_inc(halt, 1)
                q = X[:, 1 - u, 0:SC].rearrange("p (k b) -> p k b", k=DC)
                pool.tensor_copy(Xb[:, 0, :, hc, :], q).then_inc(trace_hi, 1)
                pool.wait_ge(trace_hi, t + 1)
                pool.sem_inc(halt, 1)
                pool.tensor_tensor(Xb[:, 1, :, hc, :], q, Xb[:, 0, :, hc, :], ALU.subtract).then_inc(xs_ready, 1)

            def butterfly_piece(i):
                level, sign, part = i // 8, i // 4 % 2, i % 4
                w = D << level
                bufs = [W2m[:, :, :].rearrange("p h n -> p (h n)"), WDf]
                a, o = (bufs[(level + j) % 2].rearrange("p (g x w) -> p g x w", x=2, w=w) for j in range(2))
                if i % 8 == 0:
                    if level == 0:
                        pool.wait_ge(in_w2, 16)
                    else:
                        pool.wait_ge(butterfly, i)
                    pool.sem_inc(halt, 1)
                if w < 1024:
                    g, c = slice(2 * part, 2 * part + 2), slice(0, w)
                else:
                    g, c = part * 1024 // w, slice(part * 1024 % w, part * 1024 % w + 1024)
                pool.tensor_tensor(o[:, g, sign, c], a[:, g, 0, c], a[:, g, 1, c],
                                   ALU.subtract if sign else ALU.add).then_inc(butterfly, 1)

            for t in range(BS):
                own.start(t)
                for s in range(4):
                    if s == 0 and t == 0:
                        pool.wait_ge(drive_ok, 1)
                    net_drive(t, s, t % 2)
                    if t > 0 and s == 0:
                        split_trace(t - 1, t - 1, (t - 1) % 2)
                    if t < BS // 2:
                        butterfly_piece(t * 4 + s)
                own.finish()
            pool.wait_ge(drive_ok, NB)
            pool.sem_inc(halt, 1)
            pool.wait_ge(up_hi, 2 * HC)
            pool.wait_ge(up_lo, 2 * HC)
            pool.sem_inc(evac, 1)

            def add_residual(fb):
                pool.wait_ge(xres_in, 16 * fb + 16)
                pool.sem_inc(halt, 1)
                pool.wait_ge(sum_out, fb + 2)
                pool.tensor_tensor(x1t, xsum[:], xres, ALU.add).then_inc(evac, 1)

            def block_steps(ob, first):
                for hc in range(HC):
                    t = ob * BS + hc
                    own.start(t)
                    for s in range(4):
                        net_drive(t, s, hc % 2)
                        if s == 0:
                            if hc == 1:
                                pool.wait_ge(xa_ready, ob)
                                pool.sem_inc(halt, 1)
                            split_trace(t - 1, (hc - 1) % BS, (hc - 1) % 2)
                        if hc == 1 and s == 2 and not first:
                            add_residual(ob - 2)
                    own.finish()

            block_steps(1, True)
            with pool.Fori(2, NB) as ob:
                block_steps(ob, False)
            split_trace(S - 1, BS - 1, 1)
            add_residual(NB - 2)
            add_residual(NB - 1)


def attention(nc, x1_dram, qk_dram, mask, b0, w_qk, ident, moe_up, WU, YH, YL):
    qk_tiles = qk_dram.rearrange("b a o p s n -> b a o p s n")
    qk_heads = qk_dram.rearrange("b a o (j r d) s n -> b a o r s d j n", j=NH // 4, r=2)
    with ExitStack() as ctx:
        def sb(name, shape, dt=F32):
            return ctx.enter_context(nc.sbuf_tensor(name, shape, dt))

        def sem(name):
            return ctx.enter_context(nc.semaphore(name))

        V = sb("V", [P, B, DC, NH, 2, DH], F16)

        with ExitStack() as c1:
            def sb1(name, shape, dt=F32):
                return c1.enter_context(nc.sbuf_tensor(name, shape, dt))

            def sem1(name):
                return c1.enter_context(nc.semaphore(name))

            def psum1(name):
                return c1.enter_context(nc.psum_tensor(name, [P, 512], F32))

            wst = sb1("wst", [P, 3, CT, C])
            wsp = sb1("wsp", [P, 2, 3, CT, C], F16)
            xb = sb1("xb", [P, CT, D])
            xh = sb1("xh", [P, 2, CT, D], F16)
            mr = sb1("mr", [P, D])
            kf = sb1("kf", [P, D])
            qkp = sb1("qkp", [P, 2, 2, 2, D], F16)
            qp = [psum1(f"qp{i}") for i in range(2)]
            kp = [psum1(f"kp{i}") for i in range(2)]
            vp = [psum1(f"vp{i}") for i in range(4)]
            in_w, w_hi, w_lo = sem1("in_w"), sem1("w_hi"), sem1("w_lo")
            in_x, in_m, x_hi, x_lo = sem1("in_x"), sem1("in_m"), sem1("x_hi"), sem1("x_lo")
            q_mm, k_mm, v_mm = sem1("q_mm"), sem1("k_mm"), sem1("v_mm")
            q_hi, q_lo, k_full, k_hi, k_lo, v_hi, v_lo, qk_out = (sem1("q_hi"), sem1("q_lo"), sem1("k_full"), sem1("k_hi"),
                                                             sem1("k_lo"), sem1("v_hi"), sem1("v_lo"), sem1("qk_out"))
            halt = sem1("halt")
            block = c1.enter_context(nc.Block())

            @block.sync
            def _(sp):
                sp.dma_start(wst[:], w_qk).then_inc(in_w, 16)
                with sp.Fori(0, B) as b:
                    sp.wait_ge(x_lo, b + 1)
                    sp.dma_start(xb[:], x1_dram[b]).then_inc(in_x, 16)
                    sp.wait_ge(k_full, 2 * b + 2)
                    sp.dma_start(mr[:], mask[b].partition_broadcast(P)).then_inc(in_m, 16)
                    for ot in range(2):
                        sp.wait_ge(q_lo, 2 * b + ot + 3)
                        sp.dma_start(qk_tiles[b, 0, ot], qkp[:, 0, ot]).then_inc(qk_out, 16)
                    for ot in range(2):
                        sp.wait_ge(k_lo, 2 * b + ot + 3)
                        sp.dma_start(qk_tiles[b, 1, ot], qkp[:, 1, ot]).then_inc(qk_out, 16)
                    sp.wait_ge(qk_out, 64 * b + 64)
                    sp.sem_inc(halt, 1)

            @block.tensor
            def _(pe):
                pe.wait_ge(w_lo, 1)
                pe.wait_ge(w_hi, 1)
                with pe.Fori(0, B) as b:
                    pe.wait_ge(x_hi, b + 1)
                    pe.wait_ge(x_lo, b + 2)
                    for which, ps, done in ((0, qp, q_mm), (1, kp, k_mm)):
                        pe.wait_ge(k_full if which else q_lo, 2 * b + 2)
                        for ot in range(2):
                            n = 0
                            for wp, xp in ((0, 0), (1, 0), (0, 1)):
                                for ct in range(CT):
                                    last = pe.matmul(ps[ot][:, :], wsp[:, wp, which, ct, ot * P:(ot + 1) * P],
                                                     xh[:, xp, ct, :], start=(n == 0), stop=(n == 5))
                                    n += 1
                            last.then_inc(done, 1)
                    pe.wait_ge(v_lo, 4 * b + 4)
                    for kc in range(DC):
                        n = 0
                        for wp, xp in ((0, 0), (1, 0), (0, 1)):
                            for ct in range(CT):
                                last = pe.matmul(vp[kc][:, 0:C], xh[:, xp, ct, kc * P:(kc + 1) * P],
                                                 wsp[:, wp, 2, ct, :], start=(n == 0), stop=(n == 5))
                                n += 1
                        last.then_inc(v_mm, 1)

            @block.scalar
            def _(act):
                act.wait_ge(in_w, 16)
                act.activation(wsp[:, 0].rearrange("p a c n -> p (a c n)"), wst[:].rearrange("p a c n -> p (a c n)"), ACT.Copy, scale=WS).then_inc(w_hi, 1)
                with act.Fori(0, B) as b:
                    act.wait_ge(in_x, 16 * b + 16)
                    act.activation(xh[:, 0].rearrange("p c n -> p (c n)"), xb[:].rearrange("p c n -> p (c n)"), ACT.Copy).then_inc(x_hi, 1)
                    for ot in range(2):
                        act.wait_ge(q_mm, 2 * b + ot + 1)
                        act.activation(qkp[:, 0, ot, 0, :], qp[ot][:, :], ACT.Copy, scale=1 / WS).then_inc(q_hi, 1)
                    for kc in range(DC):
                        act.wait_ge(v_mm, 4 * b + kc + 1)
                        act.activation(V[:, b, kc, :, 0, :], vp[kc][:, 0:C].rearrange("p (h d) -> p h d", h=NH),
                                       ACT.Copy).then_inc(v_hi, 1)

            @block.vector
            def _(dve):
                dve.wait_ge(w_hi, 1)
                dve.scalar_tensor_tensor(wsp[:, 1].rearrange("p a c n -> p (a c n)"), wst[:].rearrange("p a c n -> p (a c n)"), WS,
                                         wsp[:, 0].rearrange("p a c n -> p (a c n)"), ALU.mult, ALU.subtract).then_inc(w_lo, 1)
                dve.sem_inc(x_lo, 1)
                dve.sem_inc(v_lo, DC)
                for s in (q_lo, k_full, k_lo):
                    dve.sem_inc(s, 2)
                with dve.Fori(0, B) as b:
                    dve.wait_ge(x_hi, b + 1)
                    dve.tensor_tensor(xh[:, 1], xb[:], xh[:, 0], ALU.subtract).then_inc(x_lo, 1)
                    for ot in range(2):
                        dve.wait_ge(q_hi, 2 * b + ot + 1)
                        dve.scalar_tensor_tensor(qkp[:, 0, ot, 1, :], qp[ot][:, :], 1 / WS, qkp[:, 0, ot, 0, :],
                                                 ALU.mult, ALU.subtract).then_inc(q_lo, 1)
                    dve.wait_ge(in_m, 16 * b + 16)
                    for ot in range(2):
                        dve.wait_ge(k_mm, 2 * b + ot + 1)
                        dve.wait_ge(k_lo, 2 * b + ot + 2)
                        dve.scalar_tensor_tensor(kf[:], kp[ot][:, :], -1 / (WS * DH ** 0.5), mr[:], ALU.mult, ALU.mult).then_inc(k_full, 1)
                        dve.wait_ge(k_full, 2 * b + ot + 3)
                        dve.tensor_copy(qkp[:, 1, ot, 0, :], kf[:]).then_inc(k_hi, 1)
                        dve.wait_ge(k_hi, 2 * b + ot + 1)
                        dve.tensor_tensor(qkp[:, 1, ot, 1, :], kf[:], qkp[:, 1, ot, 0, :], ALU.subtract).then_inc(k_lo, 1)
                    for kc in range(DC):
                        dve.wait_ge(v_hi, 4 * b + kc + 1)
                        dve.tensor_tensor(V[:, b, kc, :, 1, :], vp[kc][:, 0:C].rearrange("p (h d) -> p h d", h=NH),
                                          V[:, b, kc, :, 0, :], ALU.subtract).then_inc(v_lo, 1)

        idS = sb("idS", [P, P])
        QR = sb("QR", [P, NH // 2, D], F16)
        KR = sb("KR", [P, NH // 2, D], F16)
        mrow = sb("mrow", [P, D])
        mt = sb("mt", [P, 2, D])
        negC = sb("negC", [P, D])
        b0S = sb("b0S", [P, 1])
        negL = sb("negL", [P, DC, D])
        nM = sb("nM", [P, 4, DC])
        rs = sb("rs", [P, 4, DC])
        ri = sb("ri", [P, DC])
        Pr = sb("Pr", [P, 2, DC, D])
        PT = sb("PT", [P, 2, 2, DC, D], F16)
        yn = sb("yn", [P, 4, DC, 2 * DH])
        yf = sb("yf", [P, DC, DH])
        wstage = sb("wstage", [P, 2, 1024])
        Lps = [ctx.enter_context(nc.psum_tensor(f"Lps{i}", [P, 512], F32)) for i in range(2)]
        Tps = [ctx.enter_context(nc.psum_tensor(f"Tps{i}", [P, 512], F32)) for i in range(4)]
        Ops = [ctx.enter_context(nc.psum_tensor(f"Ops{i}", [P, DC, 128], F32)) for i in range(2)]
        in_id, qk_in = sem("in_id"), [sem("qk_in0"), sem("qk_in1")]
        in_mask, negc_t, negc_ok = sem("in_mask"), sem("negc_t"), sem("negc_ok")
        s_L, s_neg, s_exp, s_T, s_hi, s_lo, s_pv, s_norm, s_y, s_ri = (
            sem("s_L"), sem("s_neg"), sem("s_exp"), sem("s_T"), sem("s_hi"), sem("s_lo"), sem("s_pv"),
            sem("s_norm"), sem("s_y"), sem("s_ri"))
        s_yh, in_moe, moe_t, moe_hi, moe_lo = sem("s_yh"), [sem("in_moe0"), sem("in_moe1")], sem("moe_t"), sem("moe_hi"), sem("moe_lo")
        halt = sem("halt2")
        block = ctx.enter_context(nc.Block())

        AHEAD = 8

        def load_qk(sp, b, half):
            for tensor, dst in ((0, QR), (1, KR)):
                for par in range(2):
                    for slot in range(4):
                        part = slot % 2 if tensor == 0 else slot // 2
                        row = par * 64 + slot * 16
                        sp.dma_start(dst[row:row + 16, half * 4:(half + 1) * 4, :],
                                     qk_heads[b, tensor, half, par, part]).then_inc(qk_in[half], 16)

        QKI = 16 * 16

        @block.sync
        def _(sp):
            sp.dma_start(idS[:], ident).then_inc(in_id, 16)
            sp.dma_start(b0S[:], b0.partition_broadcast(P)).then_inc(in_id, 16)
            sp.dma_start(mrow[:], mask[0].partition_broadcast(P)).then_inc(in_mask, 16)
            for half in range(2):
                load_qk(sp, 0, half)
            with sp.Fori(0, B - 1) as b:
                sp.wait_ge(negc_t, 3 * b + 3)
                sp.dma_start(mrow[:], mask[b + 1].partition_broadcast(P)).then_inc(in_mask, 16)
                for half in range(2):
                    sp.wait_ge(s_L, b * 64 + 32 * (half + 1))
                    load_qk(sp, b + 1, half)
            sp.wait_ge(negc_t, 3 * B)
            sp.dma_start(mrow[:], mask[0].partition_broadcast(P)).then_inc(in_mask, 16)

        def before(b, h, d):
            return (b, h - d) if h >= d else (b - 1, h - d + NH)

        def all_heads(eng, step):
            for h in range(NH):
                step(0, h)
            with eng.Fori(1, B) as b:
                for h in range(NH):
                    step(b, h)
            for h in range(3):
                step(B, h)

        def exists(b, h, d):
            if not isinstance(b, int):
                return True
            return 0 <= b * NH + h - d < B * NH

        @block.gpsimd
        def _(pool):
            pool.sem_inc(s_y, AHEAD)
            pool.wait_ge(in_id, 32)
            pool.sem_inc(halt, 1)

            def mask_terms(b):
                pool.wait_ge(in_mask, 16 * b + 16)
                pool.sem_inc(halt, 1)
                pool.wait_ge(negc_ok, b + 1)
                pool.sem_inc(halt, 1)
                pool.tensor_scalar(mt[:, 0], mrow[:], -1.0, 1.0, ALU.mult, ALU.add).then_inc(negc_t, 1)
                pool.wait_ge(negc_t, 3 * b + 1)
                pool.sem_inc(halt, 1)
                pool.tensor_scalar_mul(mt[:, 0], mt[:, 0], NEG).then_inc(negc_t, 1)
                pool.tensor_scalar(mt[:, 1], mrow[:], b0S[:, 0:1], None, ALU.mult).then_inc(negc_t, 1)

            def mask_sum(b):
                pool.wait_ge(negc_t, 3 * b + 3)
                pool.sem_inc(halt, 1)
                pool.wait_ge(s_neg, 64 * b + AHEAD)
                pool.sem_inc(halt, 1)
                pool.tensor_tensor(negC[:], mt[:, 0], mt[:, 1], ALU.subtract).then_inc(negc_ok, 1)

            def load_weights(b):
                if not isinstance(b, int):
                    pool.wait_ge(moe_lo, 4 * b)
                    pool.sem_inc(halt, 1)
                for j in range(2):
                    pool.dma_start(wstage[:, j], moe_up[b * 2 + j]).then_inc(in_moe[j], 16)

            def scale_weights(b, j):
                pool.wait_ge(in_moe[j], 16 * b + 16)
                pool.sem_inc(halt, 1)
                pool.tensor_scalar_mul(wstage[:, j], wstage[:, j], WS).then_inc(moe_t, 1)

            def split_weights(b, j, which):
                n = b * 2 + j
                w = wstage[:, j].rearrange("p (w k m) -> p w k m", w=2, k=DC)
                o = WU[:, n, which]
                pool.wait_ge(moe_t, n + 1)
                pool.sem_inc(halt, 1)
                pool.tensor_copy(o[:, 0], w[:, which]).then_inc(moe_hi, 1)
                pool.wait_ge(moe_hi, 2 * n + which + 1)
                pool.sem_inc(halt, 1)
                pool.tensor_tensor(o[:, 1], w[:, which], o[:, 0], ALU.subtract).then_inc(moe_lo, 1)

            def split_output(b, h):
                i = b * NH + h
                cols = slice(h * DH, (h + 1) * DH)
                pool.wait_ge(s_norm, i + 1 + AHEAD)
                pool.sem_inc(halt, 1)
                pool.tensor_tensor(yf[:], yn[:, h % 4, :, 0:DH], yn[:, h % 4, :, DH:2 * DH], ALU.add).then_inc(s_y, 1)
                pool.wait_ge(s_y, 2 * i + 1 + AHEAD)
                pool.sem_inc(halt, 1)
                pool.tensor_scalar_mul(yf[:], yf[:], 1 / WS).then_inc(s_y, 1)
                pool.wait_ge(s_y, 2 * i + 2 + AHEAD)
                pool.sem_inc(halt, 1)
                pool.tensor_copy(YH[:, b, :, cols], yf[:]).then_inc(s_yh, 1)
                pool.wait_ge(s_yh, 2 * i + 1)
                pool.sem_inc(halt, 1)
                pool.tensor_tensor(YL[:, b, :, cols], yf[:], YH[:, b, :, cols], ALU.subtract).then_inc(s_yh, 1)
                pool.wait_ge(s_yh, 2 * i + 2)
                pool.sem_inc(halt, 1)

            def step(b, h):
                real = exists(b, h, 0)
                if h == 0 and real:
                    mask_sum(b)
                if h == 1 and real:
                    load_weights(b)
                if exists(b, h, 3):
                    split_output(*before(b, h, 3))
                if not real:
                    return
                if h in (4, 8):
                    scale_weights(b, h // 4 - 1)
                if h in (5, 6, 9, 10):
                    split_weights(b, (h - 5) // 4, (h - 5) % 4)
                if h == 12:
                    mask_terms(b + 1)

            pool.sem_inc(negc_ok, 1)
            mask_terms(0)

            all_heads(pool, step)

        @block.tensor
        def _(pe):
            for s in (s_T, s_pv):
                pe.sem_inc(s, AHEAD)
            pe.wait_ge(in_id, 32)

            def scores(b, h, qt):
                n = (b * NH + h) * DC + qt
                base = 64 * (h % 2)
                pe.wait_ge(s_neg, n - 1 + AHEAD)
                pe.matmul(Lps[qt % 2][:, :], QR[base:base + 64, h // 2, qt * P:(qt + 1) * P],
                          KR[base:base + 64, h // 2, :], start=True, stop=True).then_inc(s_L, 1)

            def transposes(b, h, kc):
                i = b * NH + h
                if kc == 0:
                    pe.wait_ge(s_exp, i * DC + DC + AHEAD)
                pe.wait_ge(s_lo, DC * i + kc - DC + 1 + AHEAD)
                for qt in range(DC):
                    last = pe.transpose(Tps[kc][:, qt * P:(qt + 1) * P], Pr[:, h % 2, qt, kc * P:(kc + 1) * P], idS[:])
                last.then_inc(s_T, 1)

            def values(b, h):
                i = b * NH + h
                pe.wait_ge(s_lo, DC * i + DC + AHEAD)
                pe.wait_ge(s_norm, i - 1 + AHEAD)
                for qt in range(DC):
                    out = Ops[h % 2][:, qt]
                    for kc in range(DC):
                        pe.matmul(out[:, 0:2 * DH], PT[:, h % 2, 0, kc, qt * P:(qt + 1) * P],
                                  V[:, b, kc, h].rearrange("p x d -> p (x d)"),
                                  start=(kc == 0), stop=False, skip_group_check=True)
                    for kc in range(DC):
                        last = pe.matmul(out[:, 0:DH], PT[:, h % 2, 1, kc, qt * P:(qt + 1) * P], V[:, b, kc, h, 0],
                                         start=False, stop=(kc == DC - 1), skip_group_check=True)
                last.then_inc(s_pv, 1)

            def step(b, h):
                def score(qt):
                    if exists(b, h, 0):
                        if h % (NH // 2) == 0 and qt == 0:
                            pe.wait_ge(qk_in[h // (NH // 2)], b * QKI + QKI)
                        scores(b, h, qt)

                def transpose(kc):
                    if exists(b, h, 1):
                        transposes(*before(b, h, 1), kc)

                for qt, kcs in ((0, ()), (1, (0, 1)), (2, (2, 3)), (3, ())):
                    score(qt)
                    for kc in kcs:
                        transpose(kc)
                if exists(b, h, 2):
                    values(*before(b, h, 2))

            all_heads(pe, step)

        @block.scalar
        def _(act):
            act.sem_inc(s_exp, AHEAD)
            act.sem_inc(s_hi, AHEAD)

            def exps(b, h, qt):
                i = b * NH + h
                n = i * DC + qt
                act.wait_ge(s_neg, n + 1 + AHEAD)
                if qt == 0:
                    act.wait_ge(s_T, i * DC - DC + AHEAD)
                act.activation(Pr[:, h % 2, qt, :], negL[:, qt, :], ACT.Exp, bias=nM[:, h % 4, qt:qt + 1],
                               scale=-1.0, accum_out=rs[:, h % 4, qt:qt + 1]).then_inc(s_exp, 1)

            def transposed_high(b, h, kc):
                i = b * NH + h
                act.wait_ge(s_T, i * DC + kc + 1 + AHEAD)
                act.wait_ge(s_pv, i - 1 + AHEAD)
                act.activation(PT[:, h % 2, 0, kc, :], Tps[kc][:, :], ACT.Copy).then_inc(s_hi, 1)

            def step(b, h):
                for qt, kcs in ((0, (0,)), (1, (1,)), (2, (2, 3)), (3, ())):
                    if exists(b, h, 0):
                        exps(b, h, qt)
                    for kc in kcs:
                        if exists(b, h, 1):
                            transposed_high(*before(b, h, 1), kc)

            all_heads(act, step)

        @block.vector
        def _(dve):
            for s in (s_neg, s_lo, s_norm):
                dve.sem_inc(s, AHEAD)

            def negate_and_max(b, h, qt):
                n = (b * NH + h) * DC + qt
                dve.wait_ge(s_L, n + 1)
                dve.wait_ge(s_exp, n - 3 + AHEAD)
                dve.sem_inc(halt, 1)
                dve.tensor_tensor_reduce(out=negL[:, qt, :], in0=Lps[qt % 2][:, :], in1=negC[:], scale=1.0,
                                         scalar=3.0e38, op0=ALU.add, op1=ALU.min,
                                         accum_out=nM[:, h % 4, qt:qt + 1]).then_inc(s_neg, 1)

            def normalize(b, h):
                i = b * NH + h
                dve.wait_ge(s_pv, i + 1 + AHEAD)
                dve.wait_ge(s_y, 2 * i - 7 + AHEAD)
                dve.wait_ge(s_norm, i + AHEAD)
                dve.reciprocal(ri[:], rs[:, h % 4, :]).then_inc(s_ri, 1)
                dve.wait_ge(s_ri, i + 1)
                dve.tensor_tensor(yn[:, h % 4], Ops[h % 2][:, :, 0:2 * DH],
                                  ri[:].unsqueeze(2).to_broadcast([P, DC, 2 * DH]), ALU.mult).then_inc(s_norm, 1)

            def transposed_low(b, h, kc):
                dve.wait_ge(s_hi, (b * NH + h) * DC + kc + 1 + AHEAD)
                dve.tensor_tensor(PT[:, h % 2, 1, kc, :], Tps[kc][:, :], PT[:, h % 2, 0, kc, :], ALU.subtract).then_inc(s_lo, 1)

            def step(b, h):
                if h == 0 and exists(b, h, 0):
                    dve.wait_ge(negc_ok, b + 2)
                    dve.sem_inc(halt, 1)
                for qt, kcs in ((0, ()), (1, (0,)), (2, (1, 2)), (3, (3,))):
                    if exists(b, h, 0):
                        negate_and_max(b, h, qt)
                    for kc in kcs:
                        if exists(b, h, 1):
                            transposed_low(*before(b, h, 1), kc)
                if exists(b, h, 2):
                    normalize(*before(b, h, 2))

            all_heads(dve, step)


def experts(nc, x1_dram, router, w_down, iota, WU, WD, YH, YL, out):
    with ExitStack() as ctx:
        def sb(name, shape, dt=F32):
            return ctx.enter_context(nc.sbuf_tensor("moe_" + name, shape, dt))

        def sem(name):
            return ctx.enter_context(nc.semaphore("moe_" + name))

        def psum(name):
            return ctx.enter_context(nc.psum_tensor("moe_" + name, [P, 512], F32))

        TT = 4
        NG = B // 2
        dst = sb("dst", [P, HC, D])
        rst = sb("rst", [P, DC, E])
        rw = sb("rw", [P, 2, DC, E], F16)
        io = sb("io", [P, E])
        sc = sb("sc", [P, TT, E])
        top = sb("top", [P, TT, 8])
        idx = sb("idx", [P, TT, 8], U32)
        idf = sb("idf", [P, TT, 2])
        dif = sb("dif", [P, TT])
        ex = sb("ex", [P, TT])
        den = sb("den", [P, TT])
        wt = sb("wt", [P, 2, TT])
        c1 = sb("c1", [P, TT, E])
        comb = sb("comb", [P, TT, E])
        th = sb("th", [P, 2, 512])
        ga = sb("ga", [P, 512])
        hf = sb("hf", [P, 512])
        hid = sb("hid", [P, FC, 2, 512], F16)
        acc = sb("acc", [P, TT, D])
        gp = [psum("gp0"), psum("gp1")]
        up = [psum("up0"), psum("up1")]
        dp = [psum(f"dp{i}") for i in range(TT)]
        in_d, in_r, d_hi, d_lo, r_hi, r_lo = sem("in_d"), sem("in_r"), sem("d_hi"), sem("d_lo"), sem("r_hi"), sem("r_lo")
        sc_mm, dif_ok, ex_ok, comb_ok, own = sem("sc_mm"), sem("dif_ok"), sem("ex_ok"), sem("comb_ok"), sem("own_dve")
        g_mm, u_mm, th_ok, hid_ok, d_mm, folded = sem("g_mm"), sem("u_mm"), sem("th_ok"), sem("hid_ok"), sem("d_mm"), sem("folded")
        acc_in, stored, ffn_own, halt = sem("acc_in"), sem("stored"), sem("ffn_own"), sem("halt3")
        block = ctx.enter_context(nc.Block())

        @block.sync
        def _(sp):
            sp.dma_start(rst[:], router).then_inc(in_r, 16)
            sp.dma_start(io[:], iota).then_inc(in_r, 16)
            sp.dma_start(dst[:], w_down).then_inc(in_d, 16)
            with sp.Fori(0, NG) as g:
                for tt in range(TT):
                    sp.dma_start(acc[:, tt], x1_dram[g * 2 + tt // 2][:, tt % 2]).then_inc(acc_in, 16)
                for tt in range(TT):
                    sp.wait_ge(folded, (g * E + E) * TT + tt + 1)
                    sp.dma_start(out[g * 2 + tt // 2][:, tt % 2], acc[:, tt]).then_inc(stored, 16)
                sp.wait_ge(stored, (g * TT + TT) * 16)
                sp.sem_inc(halt, 1)

        @block.tensor
        def _(pe):
            pe.wait_ge(r_lo, 1)

            def gate_up(g, e, fc):
                n = (g * E + e) * FC + fc
                pe.wait_ge(hid_ok, n - FC + 1 + FC)
                for which, ps, done in ((0, gp[fc], g_mm), (1, up[fc], u_mm)):
                    k = 0
                    for wp, Yp in ((0, YH), (1, YH), (0, YL)):
                        for qt in range(DC):
                            last = pe.matmul(ps[:, :], WU[:, e * FC + fc, which, wp, qt, :],
                                             Yp[:, bass.ds(g * 2, 2), qt, :], start=(k == 0), stop=(k == 3 * DC - 1))
                            k += 1
                    last.then_inc(done, 1)

            def down(g, e):
                pe.wait_ge(hid_ok, (g * E + e) * FC + FC + FC)
                for tt in range(TT):
                    pe.wait_ge(folded, (g * E + e) * TT + tt + 1)
                    k = 0
                    for fc in range(FC):
                        for hp, wp in ((0, 0), (0, 1), (1, 0)):
                            last = pe.matmul(dp[tt][:, :], hid[:, fc, hp, tt * P:(tt + 1) * P], WD[:, e * FC + fc, wp, :],
                                             start=(k == 0), stop=(k == 3 * FC - 1))
                            k += 1
                    last.then_inc(d_mm, 1)

            with pe.Fori(0, NG) as g:
                pe.wait_ge(hid_ok, g * E * FC + FC)
                for tt in range(TT):
                    k = 0
                    for wp, Yp in ((0, YH), (1, YH), (0, YL)):
                        for qt in range(DC):
                            last = pe.matmul(gp[1][:, tt * E:(tt + 1) * E], Yp[:, g * 2 + tt // 2, qt, (tt % 2) * P:(tt % 2 + 1) * P],
                                             rw[:, wp, qt, :], start=(k == 0), stop=(k == 3 * DC - 1))
                            k += 1
                last.then_inc(sc_mm, 1)
                gate_up(g, 0, 0)
                pe.wait_ge(own, 8 * g + 1)
                pe.wait_ge(d_lo, 1)
                gate_up(g, 0, 1)
                with pe.Fori(1, E) as e:
                    gate_up(g, e, 0)
                    down(g, e - 1)
                    gate_up(g, e, 1)
                down(g, E - 1)

        @block.scalar
        def _(act):
            act.wait_ge(in_r, 32)
            act.activation(rw[:, 0].rearrange("p k e -> p (k e)"), rst[:].rearrange("p k e -> p (k e)"), ACT.Copy, scale=WS).then_inc(r_hi, 1)
            act.wait_ge(in_d, 16)
            act.activation(WD[:, :, 0, :], dst[:], ACT.Copy, scale=WS).then_inc(d_hi, 1)

            def gate_tanh(g, e, fc):
                n = (g * E + e) * FC + fc
                act.wait_ge(g_mm, n + 1)
                act.wait_ge(hid_ok, n + 1)
                act.activation(th[:, fc], gp[fc][:, :], ACT.Tanh, scale=0.5 / WS).then_inc(th_ok, 1)

            with act.Fori(0, NG) as g:
                act.wait_ge(dif_ok, g + 1)
                act.activation(ex[:], dif[:], ACT.Exp, scale=1 / WS).then_inc(ex_ok, 1)
                with act.Fori(0, E) as e:
                    for fc in range(FC):
                        gate_tanh(g, e, fc)

        @block.vector
        def _(dve):
            dve.wait_ge(in_r, 32)
            dve.wait_ge(r_hi, 1)
            dve.scalar_tensor_tensor(rw[:, 1].rearrange("p k e -> p (k e)"), rst[:].rearrange("p k e -> p (k e)"), WS,
                                     rw[:, 0].rearrange("p k e -> p (k e)"), ALU.mult, ALU.subtract).then_inc(r_lo, 1)
            dve.sem_inc(hid_ok, FC)
            dve.sem_inc(folded, TT)
            dve.wait_ge(d_hi, 1)
            dve.scalar_tensor_tensor(WD[:, :, 1, :], dst[:], WS, WD[:, :, 0, :], ALU.mult, ALU.subtract).then_inc(d_lo, 1)

            def route(g):
                k = [0]

                def step(ins):
                    ins.then_inc(own, 1)
                    k[0] += 1
                    dve.wait_ge(own, 8 * g + k[0])
                    dve.sem_inc(halt, 1)

                dve.wait_ge(sc_mm, g + 1)
                step(dve.tensor_copy(sc[:].rearrange("p t e -> p (t e)"), gp[1][:, 0:TT * E]))
                for tt in range(TT):
                    last = dve.max(top[:, tt], sc[:, tt])
                step(last)
                for tt in range(TT):
                    last = dve.max_index(idx[:, tt], top[:, tt], sc[:, tt])
                step(last)
                dve.tensor_tensor(dif[:], top[:, :, 1], top[:, :, 0], ALU.subtract).then_inc(dif_ok, 1)
                step(dve.tensor_copy(idf[:], idx[:, :, 0:2]))
                dve.wait_ge(ex_ok, g + 1)
                step(dve.tensor_scalar(den[:], ex[:], WS, WS, ALU.mult, ALU.add))
                step(dve.reciprocal(wt[:, 0], den[:]))
                step(dve.tensor_tensor(wt[:, 1], wt[:, 0], ex[:], ALU.mult))
                for tt in range(TT):
                    last = dve.tensor_scalar(c1[:, tt], io[:], idf[:, tt, 0:1], wt[:, 0, tt:tt + 1], ALU.is_equal, ALU.mult)
                    last = dve.tensor_scalar(comb[:, tt], io[:], idf[:, tt, 1:2], wt[:, 1, tt:tt + 1], ALU.is_equal, ALU.mult)
                step(last)
                dve.tensor_tensor(comb[:], comb[:], c1[:], ALU.add).then_inc(comb_ok, 1)
                dve.wait_ge(comb_ok, g + 1)

            def hidden(g, e, fc):
                n = (g * E + e) * FC + fc
                dve.wait_ge(th_ok, n + 1)
                dve.scalar_tensor_tensor(ga[:], th[:, fc], 1.0, gp[fc][:, :], ALU.add, ALU.mult).then_inc(ffn_own, 1)
                dve.wait_ge(ffn_own, 3 * n + 1)
                dve.wait_ge(u_mm, n + 1)
                dve.wait_ge(hid_ok, n + FC)
                dve.scalar_tensor_tensor(hf[:], ga[:], 0.5 / (WS * WS), up[fc][:, :], ALU.mult, ALU.mult).then_inc(ffn_own, 1)
                dve.wait_ge(ffn_own, 3 * n + 2)
                dve.tensor_copy(hid[:, fc, 0], hf[:]).then_inc(ffn_own, 1)
                dve.wait_ge(ffn_own, 3 * n + 3)
                dve.tensor_tensor(hid[:, fc, 1], hf[:], hid[:, fc, 0], ALU.subtract).then_inc(hid_ok, 1)

            def fold(g, e):
                for tt in range(TT):
                    n = (g * E + e) * TT + tt
                    dve.wait_ge(d_mm, n + 1)
                    dve.wait_ge(folded, n + 1)
                    dve.scalar_tensor_tensor(acc[:, tt], dp[tt][:, :], comb[:, tt, bass.ds(e, 1)],
                                             acc[:, tt], ALU.mult, ALU.add).then_inc(folded, 1)

            with dve.Fori(0, NG) as g:
                route(g)
                hidden(g, 0, 0)
                hidden(g, 0, 1)
                dve.wait_ge(acc_in, (g + 1) * TT * 16)
                dve.sem_inc(halt, 1)
                with dve.Fori(1, E) as e:
                    fold(g, e - 1)
                    hidden(g, e, 0)
                    hidden(g, e, 1)
                fold(g, E - 1)


def hadamard(n):
    import numpy as np
    h = np.ones((1, 1), np.float32)
    while h.shape[0] < n:
        h = np.block([[h, h], [h, -h]])
    return np.ascontiguousarray(h.astype(np.float32))


def lay_out(v):
    import numpy as np
    a = {k: np.asarray(x) for k, x in v.items()}
    c = np.ascontiguousarray

    def slices(gate, up):
        w = np.stack([gate, up], 1).reshape(HC, 2, P, DC, P)
        return c(w.transpose(4, 0, 1, 3, 2).reshape(P, HC * 2 * DC * P))

    x = a["x"]
    r = {
        "drive": c(x.reshape(B, S, DC, P).transpose(3, 1, 2, 0).reshape(P, S, SC)),
        "cond": c(a["cond_2048"].reshape(B, DC, P).transpose(2, 1, 0).reshape(P, SC)),
        "bias": c(a["L0_cond_bias"].reshape(DC, P).T),
        "coup": c(a["L0_cond_coupling"].T.reshape(DC, P, D).transpose(1, 0, 2).reshape(P, DC * D)),
        "had": hadamard(P),
        "w_up": slices(a["L0_ffn_W1"].reshape(HC, P, D), a["L0_ffn_W3"].reshape(HC, P, D)),
        "w_down": c(a["L0_ffn_W2"].T.reshape(HC, P, D).transpose(1, 0, 2)),
        "x_tb": c(x.transpose(1, 0, 2).reshape(NB, P, D)),
        "mask": c(a["cond_2048"]),
        "b0": c(a["L1_cond_b"].reshape(1)),
        "w_qkv": c(np.stack([a[n].T.reshape(CT, P, C) for n in ("L1_cond_Wq", "L1_cond_Wk", "L1_cond_Wv")], 1)
                   .transpose(2, 1, 0, 3)),
        "ident": np.eye(P, dtype=np.float32),
        "router": c(a["L1_ffn_router_w"].reshape(DC, P, E).transpose(1, 0, 2)),
        "moe_up": c(slices(a["L1_ffn_gate_proj"].transpose(0, 2, 1).reshape(HC, P, D),
                           a["L1_ffn_up_proj"].transpose(0, 2, 1).reshape(HC, P, D))
                    .reshape(P, HC, 2 * DC * P).transpose(1, 0, 2)),
        "moe_down": c(a["L1_ffn_down_proj"].reshape(HC, P, D).transpose(1, 0, 2)),
        "iota": np.broadcast_to(np.arange(E, dtype=np.float32), (P, E)).copy(),
    }
    return r


def build(nc, d, out):
    x1 = nc.dram_tensor("x1", (S, B, D), F32, kind="Internal").ap()
    qk = nc.dram_tensor("qk", (B, 2, 2, P, 2, D), F16, kind="Internal").ap()
    x1_blocks = x1.rearrange("(n t) b d -> n (t b) d", t=BS)
    x1_batch = x1.rearrange("(c p) b d -> b p c d", p=P)
    out_batch = out.rearrange("b (c p) d -> b p c d", p=P)
    with nc.sbuf_tensor("WU", [P, HC, 2, 2, DC, P], F16) as WU:
        with nc.sbuf_tensor("WD", [P, HC, 2, D], F16) as WD:
            oscillator_and_ffn(nc, d["drive"], d["cond"], d["bias"], d["coup"], d["had"], d["w_up"], d["w_down"],
                               d["x_tb"], x1_blocks, WU, WD)
        with nc.sbuf_tensor("YH", [P, B, DC, C], F16) as YH, nc.sbuf_tensor("YL", [P, B, DC, C], F16) as YL:
            attention(nc, x1_batch, qk, d["mask"], d["b0"], d["w_qkv"], d["ident"], d["moe_up"], WU, YH, YL)
            with nc.sbuf_tensor("WE", [P, HC, 2, D], F16) as WE:
                experts(nc, x1_batch, d["router"], d["moe_down"], d["iota"], WU, WE, YH, YL, out_batch)


def kernel(**inputs):
    import concourse.bacc as bacc
    from concourse.bass_utils import run_bass_kernel_spmd

    nc = bacc.Bacc("TRN2", target_bir_lowering=False, num_devices=1)
    arrays = lay_out(inputs)
    d = {n: nc.dram_tensor(n, a.shape, F32, kind="ExternalInput").ap() for n, a in arrays.items()}
    out = nc.dram_tensor("out", (B, S, D), F32, kind="ExternalOutput").ap()
    build(nc, d, out)
    return run_bass_kernel_spmd(nc, [arrays], core_ids=[0]).results[0]["out"]
```

```python
from contextlib import ExitStack

import concourse.bass as bass
from concourse import mybir

ALU = mybir.AluOpType
ACT = mybir.ActivationFunctionType

F32 = mybir.dt.float32
F16 = mybir.dt.float16
U32 = mybir.dt.uint32

P = 128
B, S, D = 8, 256, 512
DC = D // P
SC = DC * B
H = 2048
HC = H // P
E = 8
FC = HC // E
C = S
CT = C // P
NH, DH = 16, 16
BS = P // B
NB = S // BS

DT, EPS, ALPHA, BETA, CLAMP = 0.01, 0.08, 0.7, 0.8, 20.0
SHIFT = ALPHA / BETA
STEP = [DT / 2, DT / 2, DT, DT / 6]
WS = 64.0
CS = 256.0
NEG = 1e30


class Tally:

    def __init__(self, eng, sem, per, stop=None):
        self.eng, self.sem, self.per, self.stop = eng, sem, per, stop

    def start(self, turn):
        self.turn, self.k = turn, 0

    def mark(self, ins):
        ins.then_inc(self.sem, 1)
        self.k += 1
        return self.turn * self.per + self.k

    def then_wait(self, ins):
        self.eng.wait_ge(self.sem, self.mark(ins))
        if self.stop is not None:
            self.eng.sem_inc(self.stop, 1)

    def finish(self):
        assert self.k == self.per, (self.k, self.per)


def oscillator_and_ffn(nc, drive, cond, bias, coup, had, w_up, w_down, x_tb, x1_dram, WU, WD):
    with ExitStack() as ctx:
        def sb(name, shape, dt=F32):
            return ctx.enter_context(nc.sbuf_tensor(name, shape, dt))

        def psum(name):
            return ctx.enter_context(nc.psum_tensor(name, [P, 512], F32))

        def sem(name):
            return ctx.enter_context(nc.semaphore(name))

        PIECE = 2
        PW = 2 * DC * P
        Dr = sb("Dr", [P, S, SC])
        W2m = sb("W2m", [P, HC, D])
        stage = sb("stage", [P, 2, PIECE * PW])
        CW = sb("CW", [P, 2, DC, D], F16)
        hadS = sb("hadS", [P, P])
        condS = sb("condS", [P, SC])
        biasS = sb("biasS", [P, DC])
        biasM = sb("biasM", [P, DC])
        zero = sb("zero", [P, P], F16)
        X = sb("X", [P, 5, 2 * SC])
        T = sb("T", [P, 2, DC, 2, B], F16)
        Tf = sb("Tf", [P, 2, SC])
        t1 = sb("t1", [P, SC])
        t2 = sb("t2", [P, SC])
        F = sb("F", [P, 2 * SC])
        Z = sb("Z", [P, 2 * SC])
        W = sb("W", [P, 2 * SC])
        xsum = sb("xsum", [P, D])
        part = sb("part", [P, SC])
        Cn = sb("Cn", [P, SC])
        G = sb("G", [P, 2, SC])
        gt = sb("gt", [P, SC])
        Xb = sb("Xb", [P, 2, DC, BS, B], F16)
        Xa = sb("Xa", [P, 2, DC, BS * B], F16)
        hid = sb("hid", [P, 2, P], F16)
        free = stage[:, 0, :]
        xres, x1t = free[:, 0:D], free[:, D:2 * D]
        th, ga, hf = free[:, 1024:1152], free[:, 1152:1280], free[:, 1280:1408]
        WDf = WD[:, :, :, :].rearrange("p h a n -> p (h a n)").bitcast(F32)

        icb = [psum("ic0"), psum("ic1")]
        gate_ps, up_ps, acc_ps = [psum("gate0"), psum("gate1")], [psum("up0"), psum("up1")], psum("acc_ps")
        had_ps = up_ps

        in_coup, in_drive0, in_drive, in_small, in_w2 = (sem("in_coup"), sem("in_drive0"), sem("in_drive"),
                                                         sem("in_small"), sem("in_w2"))
        in_up = [sem("in_up0"), sem("in_up1")]
        up_hi, up_lo = sem("up_hi"), sem("up_lo")
        coup_hi, coup_lo, drive_ok, biasm_ok = sem("coup_hi"), sem("coup_lo"), sem("drive_ok"), sem("biasm_ok")
        had_done, down_hi, down_lo = sem("had_done"), sem("down_hi"), sem("down_lo")
        butterfly = {"pool": sem("butterfly_pool"), "dve": sem("butterfly_dve")}
        zero_ok = sem("zero_ok")
        n_ready, n_state, drive_ready, q_state = sem("n_ready"), sem("n_state"), sem("drive_ready"), sem("q_state")
        q_ready, tanh_hi, tanh_full, tanh_lo = sem("q_ready"), sem("tanh_hi"), sem("tanh_full"), sem("tanh_lo")
        ic_ready, xs_ready, xa_ready = sem("ic_ready"), sem("xs_ready"), sem("xa_ready")
        gate_done, up_done, th_done, hf_done, hid_done, down_done = (
            sem("gate_done"), sem("up_done"), sem("th_done"), sem("hf_done"), sem("hid_done"), sem("down_done"))
        xres_in, evac, sum_out, hid_hi, x1_out = sem("xres_in"), sem("evac"), sem("sum_out"), sem("hid_hi"), sem("x1_out")
        dve_own, dve_ffn, pool_own, trace_hi = sem("dve_own"), sem("dve_ffn"), sem("pool_own"), sem("trace_hi")
        halt = sem("halt")

        turns = [(who, g) for g in range(12, 4 * BS) for who in (("pool", "dve") if g % 4 in (0, 3) or g >= 36 else ("pool",))][:4 * HC]
        FIRST_DOWN = 4 * BS - HC

        def wait_butterflies(eng, count):
            for who in ("pool", "dve"):
                n = sum(w == who for w, _ in turns[:count])
                if n:
                    eng.wait_ge(butterfly[who], n)

        def butterfly_pieces(who, eng, g):
            for i, turn in enumerate(turns):
                if turn != (who, g):
                    continue
                level, sign, part = i // HC, i // (HC // 2) % 2, i % (HC // 2)
                w = D << level
                bufs = [W2m[:, :, :].rearrange("p h n -> p (h n)"), WDf]
                a, o = (bufs[(level + j) % 2].rearrange("p (g x w) -> p g x w", x=2, w=w) for j in range(2))
                if i < HC:
                    eng.wait_ge(in_w2, 16)
                else:
                    wait_butterflies(eng, HC * level)
                grp, c = part * D // w, slice(part * D % w, part * D % w + D)
                eng.tensor_tensor(o[:, grp, sign, c], a[:, grp, 0, c], a[:, grp, 1, c],
                                  ALU.subtract if sign else ALU.add).then_inc(butterfly[who], 1)

        block = ctx.enter_context(nc.Block())

        @block.sync
        def _(sp):
            sp.dma_start(W2m[:, 0:DC, :], coup).then_inc(in_coup, 16)
            sp.dma_start(condS[:], cond).then_inc(in_small, 16)
            sp.dma_start(biasS[:], bias).then_inc(in_small, 16)
            sp.dma_start(hadS[:], had).then_inc(in_small, 16)
            sp.dma_start(Dr[:, 0:BS, :], drive[:, 0:BS, :]).then_inc(in_drive0, 16)
            sp.dma_start(stage[:, 0], w_up[:, 0:PIECE * PW]).then_inc(in_up[0], 16)
            sp.wait_ge(coup_hi, 1)
            sp.wait_ge(coup_lo, 1)
            sp.dma_start(W2m[:], w_down).then_inc(in_w2, 16)
            sp.dma_start(Dr[:, BS:S, :], drive[:, BS:S, :]).then_inc(in_drive, 16)
            for n in range(1, HC // PIECE):
                if n >= 2:
                    sp.wait_ge(up_lo, 2 * PIECE * (n - 1))
                sp.dma_start(stage[:, n % 2], w_up[:, n * PIECE * PW:(n + 1) * PIECE * PW]).then_inc(in_up[n % 2], 16)
            with sp.Fori(0, NB) as blk:
                sp.wait_ge(evac, blk + 1)
                sp.dma_start(xres, x_tb[blk]).then_inc(xres_in, 16)
                sp.wait_ge(evac, blk + 2)
                sp.dma_start(x1_dram[blk], x1t).then_inc(x1_out, 16)
                sp.wait_ge(x1_out, 16 * blk + 16)
                sp.sem_inc(halt, 1)

        @block.tensor
        def _(pe):
            pe.wait_ge(coup_hi, 1)
            pe.wait_ge(coup_lo, 1)
            pe.wait_ge(zero_ok, 1)
            pe.wait_ge(in_small, 48)

            def couple(t, s):
                g = t * 4 + s
                out = icb[s % 2]
                pe.wait_ge(tanh_hi, g + 1)
                for m in range(DC):
                    for k in range(DC):
                        pe.matmul(out[:, m * 2 * B:m * 2 * B + B], CW[:, 1, k, m * P:(m + 1) * P],
                                  T[:, s % 2, k, 0, :], start=(m == 0 and k == 0), stop=False, skip_group_check=True)
                pe.wait_ge(tanh_lo, g + 1)
                for m in range(DC):
                    for k in range(DC):
                        last = pe.matmul(out[:, m * 2 * B:(m + 1) * 2 * B], CW[:, 0, k, m * P:(m + 1) * P],
                                         T[:, s % 2, k, :, :], start=False, stop=(m == DC - 1 and k == DC - 1),
                                         skip_group_check=True)
                last.then_inc(ic_ready, 1)

            PRODUCTS = [(wp, xp, k) for wp, xp in ((0, 0), (1, 0), (0, 1)) for k in range(DC)]

            def project(fb, hc, which, first, last):
                out, done = (up_ps if which else gate_ps)[hc % 2], up_done if which else gate_done
                if first == 0:
                    pe.wait_ge(xa_ready, fb + 1)
                for n in range(first, last):
                    wp, xp, k = PRODUCTS[n]
                    ins = pe.matmul(out[:, 0:P], WU[:, hc, which, wp, k, :], Xa[:, xp, k, :],
                                    start=(n == 0), stop=(n == 3 * DC - 1))
                if last == 3 * DC:
                    ins.then_inc(done, 1)

            def down(idx, hc, parts):
                for n in parts:
                    hp, wp = ((0, 0), (0, 1), (1, 0))[n]
                    pe.wait_ge(hid_done if hp else hid_hi, idx + 1)
                    ins = pe.matmul(acc_ps[:, :], hid[:, hp, :], WD[:, hc, wp, :], start=False, stop=False,
                                    skip_group_check=True)
                if 2 in parts:
                    ins.then_inc(down_done, 1)

            def clear(fb):
                pe.wait_ge(sum_out, fb + 1)
                pe.matmul(acc_ps[:, :], zero[:], WD[:, 0, 0, :], start=True, stop=False, skip_group_check=True)

            def transform(c):
                wait_butterflies(pe, 3 * HC + c + 1)
                if c >= 2:
                    pe.wait_ge(down_lo, c - 1)
                pe.matmul(had_ps[c % 2][:, :], hadS[:], W2m[:, c, :], start=True, stop=True).then_inc(had_done, 1)

            for t in range(BS):
                for s in range(4):
                    couple(t, s)
                    if t * 4 + s >= FIRST_DOWN:
                        transform(t * 4 + s - FIRST_DOWN)
            pe.wait_ge(down_hi, HC)
            pe.wait_ge(down_lo, HC)
            pe.wait_ge(up_hi, 2 * HC)
            pe.wait_ge(up_lo, 2 * HC)

            def block_steps(ob, first):
                for hc in range(HC):
                    t = ob * BS + hc
                    prev = not (first and hc == 0)
                    couple(t, 0)
                    project(ob - 1, hc, 0, 0, 9)
                    couple(t, 1)
                    project(ob - 1, hc, 0, 9, 12)
                    project(ob - 1, hc, 1, 0, 6)
                    couple(t, 2)
                    project(ob - 1, hc, 1, 6, 11)
                    if hc == 1:
                        clear(ob - 1)
                    if prev:
                        down(t - BS - 1, (hc - 1) % HC, (0,))
                    couple(t, 3)
                    project(ob - 1, hc, 1, 11, 12)
                    if prev:
                        down(t - BS - 1, (hc - 1) % HC, (1, 2))

            block_steps(1, True)
            with pe.Fori(2, NB) as ob:
                block_steps(ob, False)
            for hc in range(HC + 1):
                idx = hc + (NB - 1) * BS
                if hc < HC:
                    if hc > 1:
                        pe.wait_ge(hid_done, idx - 1)
                    project(NB - 1, hc, 0, 0, 12)
                    project(NB - 1, hc, 1, 0, 12)
                if hc == 1:
                    clear(NB - 1)
                down(idx - 1, (hc - 1) % HC, (0, 1, 2))

        @block.scalar
        def _(act):
            act.wait_ge(in_coup, 16)
            act.activation(CW[:, 0, :, :].rearrange("p k n -> p (k n)"), W2m[:, 0:DC, :].rearrange("p k n -> p (k n)"),
                           ACT.Copy, scale=CS).then_inc(coup_hi, 1)
            act.wait_ge(biasm_ok, 1)

            def add_bias(t0, steps):
                for k in range(DC):
                    v = Dr[:, t0:t0 + steps, k * B:(k + 1) * B]
                    last = act.activation(v, v, ACT.Identity, bias=biasM[:, k:k + 1], scale=1.0)
                last.then_inc(drive_ok, 1)

            act.wait_ge(in_drive0, 16)
            add_bias(0, BS)

            def up_high(hc, which):
                act.wait_ge(in_up[hc // PIECE % 2], 16 * (hc // PIECE // 2 + 1))
                w = stage[:, hc // PIECE % 2, :].rearrange("p (h w n) -> p h w n", h=PIECE, w=2)
                act.activation(WU[:, hc, which, 0, :, :].rearrange("p k m -> p (k m)"), w[:, hc % PIECE, which],
                               ACT.Copy, scale=WS).then_inc(up_hi, 1)

            def down_high(c):
                act.wait_ge(had_done, c + 1)
                act.activation(WD[:, c, 0, :], had_ps[c % 2][:, :], ACT.Copy, scale=WS / H ** 0.5).then_inc(down_hi, 1)

            def tanhs(t, s):
                g = t * 4 + s
                src = X[:, 1 + s, 0:SC] if s else Cn[:]
                act.wait_ge(q_ready, g + 1)
                act.activation(T[:, s % 2, :, 0, :], src.rearrange("p (k b) -> p k b", k=DC), ACT.Tanh).then_inc(tanh_hi, 1)
                act.activation(Tf[:, s % 2, :], src, ACT.Tanh).then_inc(tanh_full, 1)

            def gate_tanh(idx, hc):
                act.wait_ge(gate_done, idx + 1)
                act.activation(th, gate_ps[hc % 2][:, 0:P], ACT.Tanh, scale=0.5 / WS).then_inc(th_done, 1)

            def hidden_high(idx):
                act.wait_ge(hf_done, idx + 1)
                act.activation(hid[:, 0, :], hf, ACT.Copy).then_inc(hid_hi, 1)

            def sum_copy(fb):
                act.wait_ge(down_done, (fb + 1) * HC)
                act.wait_ge(evac, fb + 1)
                act.activation(xsum[:], acc_ps[:, :], ACT.Copy, scale=1 / WS).then_inc(sum_out, 1)

            biased = 0
            for t in range(BS):
                for s in range(4):
                    tanhs(t, s)
                    if s < 2 and t > 0:
                        up_high(t - 1, s)
                    if s >= 2 and t == BS - 1:
                        up_high(t, s - 2)
                    if t >= 4 and (s == 2 or s == 0 and t >= BS - 3):
                        if biased == 0:
                            act.wait_ge(in_drive, 16)
                        biased += 1
                        add_bias(biased * BS, BS)
                    if t * 4 + s > FIRST_DOWN:
                        down_high(t * 4 + s - FIRST_DOWN - 1)
            down_high(HC - 1)
            act.sem_inc(sum_out, 1)

            def block_steps(ob, first):
                for hc in range(HC):
                    t = ob * BS + hc
                    for s in range(4):
                        tanhs(t, s)
                        if s == 1:
                            if hc == 1 and not first:
                                sum_copy(ob - 2)
                            if not (first and hc == 0):
                                hidden_high(t - BS - 1)
                        if s == 2:
                            gate_tanh(t - BS, hc)

            block_steps(1, True)
            with act.Fori(2, NB) as ob:
                block_steps(ob, False)
            for hc in range(HC + 1):
                idx = hc + (NB - 1) * BS
                act.wait_ge(down_done, idx - 1)
                hidden_high(idx - 1)
                if hc == 1:
                    sum_copy(NB - 2)
                if hc < HC:
                    gate_tanh(idx, hc)
            sum_copy(NB - 1)

        @block.vector
        def _(dve):
            own = Tally(dve, dve_own, 3 * 4 + 3 + 1 + 4 + 4)
            ffn = Tally(dve, dve_ffn, 1)
            dve.memset(zero[:], 0.0).then_inc(zero_ok, 1)
            dve.wait_ge(in_small, 48)
            dve.tensor_scalar_add(biasM[:], biasS[:], -SHIFT).then_inc(biasm_ok, 1)
            dve.tensor_scalar(X[:, 0, SC:2 * SC], condS[:], 1 / EPS, -SHIFT / EPS, ALU.mult, ALU.add).then_inc(n_ready, 1)
            dve.wait_ge(n_ready, 1)
            dve.sem_inc(n_state, 1)
            dve.tensor_copy(X[:, 0, 0:SC], condS[:]).then_inc(q_state, 1)
            dve.tensor_copy(Cn[:], condS[:]).then_inc(q_ready, 1)
            dve.wait_ge(q_ready, 1)
            dve.wait_ge(coup_hi, 1)
            dve.scalar_tensor_tensor(CW[:, 1, :, :].rearrange("p k n -> p (k n)"), W2m[:, 0:DC, :].rearrange("p k n -> p (k n)"), CS,
                                     CW[:, 0, :, :].rearrange("p k n -> p (k n)"), ALU.mult, ALU.subtract).then_inc(coup_lo, 1)

            def up_low(hc, which):
                dve.wait_ge(up_hi, 2 * hc + which + 1)
                w = stage[:, hc // PIECE % 2, :].rearrange("p (h w n) -> p h w n", h=PIECE, w=2)
                o = WU[:, hc, which].rearrange("p a k m -> p a (k m)")
                dve.scalar_tensor_tensor(o[:, 1], w[:, hc % PIECE, which], WS, o[:, 0], ALU.mult, ALU.subtract).then_inc(up_lo, 1)

            def down_low(c):
                dve.wait_ge(down_hi, c + 1)
                dve.scalar_tensor_tensor(WD[:, c, 1, :], had_ps[c % 2][:, :], WS / H ** 0.5, WD[:, c, 0, :],
                                         ALU.mult, ALU.subtract).then_inc(down_lo, 1)

            def stage_ops(t, s, u):
                g = t * 4 + s
                a = STEP[s]
                start, here = X[:, u, :], X[:, 1 + s if s else u, :]
                Q, n = here[:, 0:SC], here[:, SC:2 * SC]
                square = own.mark(dve.tensor_tensor(t1[:], Q, Q, ALU.mult))
                if s == 0:
                    dve.wait_ge(n_state, t + 1)
                fn = own.mark(dve.scalar_tensor_tensor(F[:, SC:2 * SC], n, -BETA * EPS, Q, ALU.mult, ALU.add))
                dve.wait_ge(dve_own, square)
                cube = own.mark(dve.scalar_tensor_tensor(t2[:], t1[:], -3.0, Q, ALU.add, ALU.mult))
                if s == 1:
                    z = own.mark(dve.tensor_tensor(Z[:], here, start, ALU.subtract))
                elif s == 2:
                    z = own.mark(dve.scalar_tensor_tensor(Z[:], here, 2.0, Z[:], ALU.mult, ALU.add))
                elif s == 3:
                    z = own.mark(dve.tensor_tensor(Z[:], Z[:], here, ALU.add))
                dve.wait_ge(tanh_full, g + 1)
                dve.tensor_tensor(T[:, s % 2, :, 1, :], Tf[:, s % 2, :].rearrange("p (k b) -> p k b", k=DC),
                                  T[:, s % 2, :, 0, :], ALU.subtract).then_inc(tanh_lo, 1)
                dve.wait_ge(drive_ready, g + 1)
                dve.wait_ge(dve_own, z if s else cube)
                own.then_wait(dve.scalar_tensor_tensor(F[:, 0:SC], t2[:], -1 / 3, G[:, s % 2, :], ALU.mult, ALU.add))
                if s < 3:
                    dve.scalar_tensor_tensor(X[:, 2 + s, :], F[:], a, start, ALU.mult, ALU.add).then_inc(n_ready, 1)
                else:
                    own.then_wait(dve.scalar_tensor_tensor(W[:], F[:], 3 * a, Z[:], ALU.mult, ALU.add))
                    dve.tensor_scalar_mul(W[:], W[:], 1 / 3).then_inc(n_ready, 1)

            def stage_end(t, s, u):
                a = STEP[s] / CS
                ic = icb[s % 2][:, 0:2 * SC].rearrange("p (k x b) -> p k x b", k=DC, x=2)
                v = part[:].rearrange("p (k b) -> p k b", k=DC)
                base = X[:, 2 + s, 0:SC] if s < 3 else W[:, 0:SC]
                out = X[:, 2 + s, 0:SC] if s < 3 else Cn[:]
                dve.wait_ge(n_ready, t * 4 + s + 2)
                dve.wait_ge(ic_ready, t * 4 + s + 1)
                own.then_wait(dve.scalar_tensor_tensor(v, ic[:, :, 1, :], a, base.rearrange("p (k b) -> p k b", k=DC),
                                                       ALU.mult, ALU.add))
                dve.scalar_tensor_tensor(out.rearrange("p (k b) -> p k b", k=DC), ic[:, :, 0, :], a, v,
                                         ALU.mult, ALU.add).then_inc(q_ready, 1)
                dve.wait_ge(q_ready, t * 4 + s + 2)
                if s == 3:
                    dve.tensor_scalar(X[:, 1 - u, 0:SC], Cn[:], CLAMP, -CLAMP, ALU.min, ALU.max).then_inc(q_state, 1)
                    dve.wait_ge(q_state, t + 2)

            def take_block(fb, first=False):
                dve.wait_ge(xs_ready, (fb + 1) * BS)
                if not first:
                    dve.wait_ge(up_done, fb * HC)
                dve.tensor_copy(Xa[:].rearrange("p a k n -> p (a k n)"),
                                Xb[:].rearrange("p a k t b -> p (a k t b)")).then_inc(xa_ready, 1)

            def gated(idx, hc):
                dve.wait_ge(th_done, idx + 1)
                ffn.start(idx)
                return ffn.mark(dve.scalar_tensor_tensor(ga, th, 1.0, gate_ps[hc % 2][:, 0:P], ALU.add, ALU.mult))

            def hidden(idx, hc):
                dve.wait_ge(dve_ffn, idx + 1)
                dve.wait_ge(up_done, idx + 1)
                dve.scalar_tensor_tensor(hf, ga, 0.5 / (WS * WS), up_ps[hc % 2][:, 0:P], ALU.mult, ALU.mult).then_inc(hf_done, 1)

            def hidden_low(idx):
                dve.wait_ge(hid_hi, idx + 1)
                dve.tensor_tensor(hid[:, 1, :], hf, hid[:, 0, :], ALU.subtract).then_inc(hid_done, 1)

            for t in range(BS):
                own.start(t)
                for s in range(4):
                    stage_ops(t, s, t % 2)
                    if s in (1, 2) and t > 0:
                        up_low(t - 1, s - 1)
                    if s == 3 and t == BS - 1:
                        up_low(t, 0)
                    if t * 4 + s > FIRST_DOWN:
                        down_low(t * 4 + s - FIRST_DOWN - 1)
                    butterfly_pieces("dve", dve, t * 4 + s)
                    stage_end(t, s, t % 2)
                own.finish()
            up_low(HC - 1, 1)
            down_low(HC - 1)

            def block_steps(ob, first):
                for hc in range(HC):
                    t = ob * BS + hc
                    prev = not (first and hc == 0)
                    own.start(t)
                    for s in range(4):
                        stage_ops(t, s, hc % 2)
                        if s == 0 and prev:
                            hidden(t - BS - 1, hc - 1)
                        if s == 0 and hc == 0:
                            take_block(ob - 1, first)
                        if s == 1 and prev:
                            hidden_low(t - BS - 1)
                        if s == 2:
                            gated(t - BS, hc)
                        stage_end(t, s, hc % 2)
                    own.finish()

            block_steps(1, True)
            with dve.Fori(2, NB) as ob:
                block_steps(ob, False)
            take_block(NB - 1)
            for hc in range(HC + 1):
                idx = hc + (NB - 1) * BS
                hidden(idx - 1, hc - 1)
                hidden_low(idx - 1)
                if hc < HC:
                    gated(idx, hc)

        @block.gpsimd
        def _(pool):
            own = Tally(pool, pool_own, 4, halt)

            def net_drive(t, s, u):
                n = X[:, 1 + s if s else u, SC:2 * SC]
                pool.wait_ge(n_ready, t * 4 + s + 1)
                pool.sem_inc(halt, 1)
                if s == 0 and not (isinstance(t, int) and t == 0):
                    pool.tensor_scalar(n, W[:, SC:2 * SC], (CLAMP - SHIFT) / EPS, (-CLAMP - SHIFT) / EPS,
                                       ALU.min, ALU.max).then_inc(n_state, 1)
                    pool.wait_ge(n_state, t + 1)
                    pool.sem_inc(halt, 1)
                own.then_wait(pool.tensor_scalar_mul(gt[:], n, -EPS))
                pool.tensor_tensor(G[:, s % 2, :], gt[:], Dr[:, t, :], ALU.add).then_inc(drive_ready, 1)

            def split_trace(t, hc, u):
                pool.wait_ge(q_state, t + 2)
                pool.sem_inc(halt, 1)
                q = X[:, 1 - u, 0:SC].rearrange("p (k b) -> p k b", k=DC)
                pool.tensor_copy(Xb[:, 0, :, hc, :], q).then_inc(trace_hi, 1)
                pool.wait_ge(trace_hi, t + 1)
                pool.sem_inc(halt, 1)
                pool.tensor_tensor(Xb[:, 1, :, hc, :], q, Xb[:, 0, :, hc, :], ALU.subtract).then_inc(xs_ready, 1)

            for t in range(BS):
                own.start(t)
                for s in range(4):
                    if s == 0 and t == 0:
                        pool.wait_ge(drive_ok, 1)
                    net_drive(t, s, t % 2)
                    if t > 0 and s == 0:
                        split_trace(t - 1, t - 1, (t - 1) % 2)
                    butterfly_pieces("pool", pool, t * 4 + s)
                own.finish()
            pool.wait_ge(drive_ok, NB)
            pool.sem_inc(halt, 1)
            pool.wait_ge(up_hi, 2 * HC)
            pool.wait_ge(up_lo, 2 * HC)
            pool.sem_inc(evac, 1)

            def add_residual(fb):
                pool.wait_ge(xres_in, 16 * fb + 16)
                pool.sem_inc(halt, 1)
                pool.wait_ge(sum_out, fb + 2)
                pool.tensor_tensor(x1t, xsum[:], xres, ALU.add).then_inc(evac, 1)

            def block_steps(ob, first):
                for hc in range(HC):
                    t = ob * BS + hc
                    own.start(t)
                    for s in range(4):
                        net_drive(t, s, hc % 2)
                        if s == 0:
                            if hc == 1:
                                pool.wait_ge(xa_ready, ob)
                                pool.sem_inc(halt, 1)
                            split_trace(t - 1, (hc - 1) % BS, (hc - 1) % 2)
                        if hc == 1 and s == 2 and not first:
                            add_residual(ob - 2)
                    own.finish()

            block_steps(1, True)
            with pool.Fori(2, NB) as ob:
                block_steps(ob, False)
            split_trace(S - 1, BS - 1, 1)
            add_residual(NB - 2)
            add_residual(NB - 1)


def attention(nc, x1_dram, qk_dram, mask, b0, w_qk, ident, moe_up, WU, YH, YL):
    qk_tiles = qk_dram.rearrange("b a o p s n -> b a o p s n")
    qk_heads = qk_dram.rearrange("b a o (j r d) s n -> b a o r s d j n", j=NH // 4, r=2)
    with ExitStack() as ctx:
        def sb(name, shape, dt=F32):
            return ctx.enter_context(nc.sbuf_tensor(name, shape, dt))

        def sem(name):
            return ctx.enter_context(nc.semaphore(name))

        VW = 2 * DH + 1
        V = sb("V", [P, B, DC, NH, VW], F16)

        with ExitStack() as c1:
            def sb1(name, shape, dt=F32):
                return c1.enter_context(nc.sbuf_tensor(name, shape, dt))

            def sem1(name):
                return c1.enter_context(nc.semaphore(name))

            def psum1(name):
                return c1.enter_context(nc.psum_tensor(name, [P, 512], F32))

            wst = sb1("wst", [P, 3, CT, C])
            wsp = sb1("wsp", [P, 2, 3, CT, C], F16)
            xb = sb1("xb", [P, 2, CT, D])
            xh = sb1("xh", [P, 2, 2, CT, D], F16)
            qkp = sb1("qkp", [P, 2, 2, 2, 2, D], F16)
            kf = sb1("kf", [P, 2, D])
            masks = sb1("masks", [P, B, D])
            qp = [psum1(f"qp{i}") for i in range(2)]
            kp = [psum1(f"kp{i}") for i in range(2)]
            vp = [psum1(f"vp{i}") for i in range(4)]
            in_w, w_hi, w_lo = sem1("in_w"), sem1("w_hi"), sem1("w_lo")
            in_x, in_m, x_hi, x_lo = [sem1("in_x0"), sem1("in_x1")], sem1("in_m"), sem1("x_hi"), sem1("x_lo")
            q_mm, k_mm, v_mm = sem1("q_mm"), sem1("k_mm"), sem1("v_mm")
            q_hi, q_lo, k_full, k_hi, k_lo, v_hi, v_lo = (sem1("q_hi"), sem1("q_lo"), sem1("k_full"), sem1("k_hi"),
                                                          sem1("k_lo"), sem1("v_hi"), sem1("v_lo"))
            qk_out = [sem1("qk_out0"), sem1("qk_out1")]
            ones_ok = sem1("ones_ok")
            halt = sem1("halt")
            block = c1.enter_context(nc.Block())

            @block.sync
            def _(sp):
                sp.dma_start(wst[:], w_qk).then_inc(in_w, 16)
                with sp.Fori(0, B // 2) as bb:
                    for j in range(2):
                        b = bb * 2 + j
                        sp.wait_ge(x_lo, b + 1)
                        sp.dma_start(xb[:, j], x1_dram[b]).then_inc(in_x[j], 16)

            @block.gpsimd
            def _(pool):
                pool.sem_inc(x_lo, 2)
                with pool.Fori(0, B // 2) as bb:
                    for j in range(2):
                        b = bb * 2 + j
                        pool.wait_ge(in_x[j], 16 * bb + 16)
                        pool.sem_inc(halt, 1)
                        pool.wait_ge(v_lo, 4 * b + 4)
                        pool.sem_inc(halt, 1)
                        pool.tensor_copy(xh[:, j, 0], xb[:, j]).then_inc(x_hi, 1)
                        pool.wait_ge(x_hi, b + 1)
                        pool.sem_inc(halt, 1)
                        pool.tensor_tensor(xh[:, j, 1], xb[:, j], xh[:, j, 0], ALU.subtract).then_inc(x_lo, 1)

            @block.tensor
            def _(pe):
                pe.wait_ge(w_lo, 1)
                pe.wait_ge(w_hi, 1)
                with pe.Fori(0, B // 2) as bb:
                    for j in range(2):
                        b = bb * 2 + j
                        pe.wait_ge(x_hi, b + 1)
                        pe.wait_ge(x_lo, b + 3)
                        for which, ps, done in ((0, qp, q_mm), (1, kp, k_mm)):
                            pe.wait_ge(k_full if which else q_lo, 2 * b + 2)
                            for ot in range(2):
                                n = 0
                                for wp, xp in ((0, 0), (1, 0), (0, 1)):
                                    for ct in range(CT):
                                        last = pe.matmul(ps[ot][:, :], wsp[:, wp, which, ct, ot * P:(ot + 1) * P],
                                                         xh[:, j, xp, ct, :], start=(n == 0), stop=(n == 5))
                                        n += 1
                                last.then_inc(done, 1)
                        pe.wait_ge(v_lo, 4 * b + 8)
                        for kc in range(DC):
                            n = 0
                            for wp, xp in ((0, 0), (1, 0), (0, 1)):
                                for ct in range(CT):
                                    last = pe.matmul(vp[kc][:, 0:C], xh[:, j, xp, ct, kc * P:(kc + 1) * P],
                                                     wsp[:, wp, 2, ct, :], start=(n == 0), stop=(n == 5))
                                    n += 1
                            last.then_inc(v_mm, 1)

            @block.scalar
            def _(act):
                act.wait_ge(in_w, 16)
                act.activation(wsp[:, 0].rearrange("p a c n -> p (a c n)"), wst[:].rearrange("p a c n -> p (a c n)"), ACT.Copy, scale=WS).then_inc(w_hi, 1)
                act.dma_start(masks[:], mask.partition_broadcast(P)).then_inc(in_m, 16)
                for j in range(2):
                    act.sem_inc(qk_out[j], 64)
                with act.Fori(0, B // 2) as bb:
                    for j in range(2):
                        b = bb * 2 + j
                        act.wait_ge(qk_out[j], 64 * bb + 64)
                        for ot in range(2):
                            act.wait_ge(q_mm, 2 * b + ot + 1)
                            act.activation(qkp[:, j, 0, ot, 0, :], qp[ot][:, :], ACT.Copy, scale=1 / WS).then_inc(q_hi, 1)
                        for ot in range(2):
                            act.wait_ge(k_full, 2 * b + ot + 3)
                            act.activation(qkp[:, j, 1, ot, 0, :], kf[:, ot], ACT.Copy).then_inc(k_hi, 1)
                        for kc in range(DC):
                            act.wait_ge(v_mm, 4 * b + kc + 1)
                            act.activation(V[:, b, kc, :, DH:2 * DH], vp[kc][:, 0:C].rearrange("p (h d) -> p h d", h=NH),
                                           ACT.Copy).then_inc(v_hi, 1)
                        act.wait_ge(q_lo, 2 * b + 4)
                        for ot in range(2):
                            act.dma_start(qk_tiles[b, 0, ot], qkp[:, j, 0, ot]).then_inc(qk_out[j], 16)
                        act.wait_ge(k_lo, 2 * b + 4)
                        for ot in range(2):
                            act.dma_start(qk_tiles[b, 1, ot], qkp[:, j, 1, ot]).then_inc(qk_out[j], 16)
                for j in range(2):
                    act.wait_ge(qk_out[j], 64 * (B // 2) + 64)

            @block.vector
            def _(dve):
                dve.wait_ge(w_hi, 1)
                dve.scalar_tensor_tensor(wsp[:, 1].rearrange("p a c n -> p (a c n)"), wst[:].rearrange("p a c n -> p (a c n)"), WS,
                                         wsp[:, 0].rearrange("p a c n -> p (a c n)"), ALU.mult, ALU.subtract).then_inc(w_lo, 1)
                dve.memset(V[:, :, :, :, 2 * DH:VW].rearrange("p b k h x -> p (b k h) x"), WS).then_inc(ones_ok, 1)
                dve.sem_inc(v_lo, 8)
                for s in (q_lo, k_full, k_lo):
                    dve.sem_inc(s, 2)
                with dve.Fori(0, B // 2) as bb:
                    for j in range(2):
                        b = bb * 2 + j
                        for ot in range(2):
                            dve.wait_ge(q_hi, 2 * b + ot + 1)
                            dve.scalar_tensor_tensor(qkp[:, j, 0, ot, 1, :], qp[ot][:, :], 1 / WS, qkp[:, j, 0, ot, 0, :],
                                                     ALU.mult, ALU.subtract).then_inc(q_lo, 1)
                        for ot in range(2):
                            dve.wait_ge(in_m, 16)
                            dve.wait_ge(k_mm, 2 * b + ot + 1)
                            dve.wait_ge(k_lo, 2 * b + ot + 1)
                            dve.scalar_tensor_tensor(kf[:, ot], kp[ot][:, :], -1 / (WS * DH ** 0.5), masks[:, b], ALU.mult, ALU.mult).then_inc(k_full, 1)
                        for ot in range(2):
                            dve.wait_ge(k_hi, 2 * b + ot + 1)
                            dve.tensor_tensor(qkp[:, j, 1, ot, 1, :], kf[:, ot], qkp[:, j, 1, ot, 0, :], ALU.subtract).then_inc(k_lo, 1)
                        for kc in range(DC):
                            dve.wait_ge(v_hi, 4 * b + kc + 1)
                            dve.tensor_tensor(V[:, b, kc, :, 0:DH], vp[kc][:, 0:C].rearrange("p (h d) -> p h d", h=NH),
                                              V[:, b, kc, :, DH:2 * DH], ALU.subtract).then_inc(v_lo, 1)

        idS = sb("idS", [P, P])
        QR = sb("QR", [P, NH // 2, D], F16)
        KR = sb("KR", [P, NH // 2, D], F16)
        mrow = sb("mrow", [P, D])
        mt = sb("mt", [P, 2, D])
        negC = sb("negC", [P, D])
        b0S = sb("b0S", [P, 1])
        negL = sb("negL", [P, DC, D])
        nM = sb("nM", [P, 4, DC])
        ri = sb("ri", [P, DC])
        Pr = sb("Pr", [P, 2, DC, D])
        PT = sb("PT", [P, 2, 2, DC, D], F16)
        yn = sb("yn", [P, 4, DC, 2 * DH])
        yf = sb("yf", [P, DC, DH])
        wstage = sb("wstage", [P, 2, 1024])
        Lps = [ctx.enter_context(nc.psum_tensor(f"Lps{i}", [P, 512], F32)) for i in range(2)]
        Tps = [ctx.enter_context(nc.psum_tensor(f"Tps{i}", [P, 512], F32)) for i in range(4)]
        Ops = [ctx.enter_context(nc.psum_tensor(f"Ops{i}", [P, DC, 128], F32)) for i in range(2)]
        in_id, qk_in = sem("in_id"), [sem("qk_in0"), sem("qk_in1")]
        in_mask, negc_t, negc_ok = sem("in_mask"), sem("negc_t"), sem("negc_ok")
        s_L, s_neg, s_exp, s_T, s_hi, s_lo, s_pv, s_norm, s_y, s_ri = (
            sem("s_L"), sem("s_neg"), sem("s_exp"), sem("s_T"), sem("s_hi"), sem("s_lo"), sem("s_pv"),
            sem("s_norm"), sem("s_y"), sem("s_ri"))
        s_yh, in_moe, moe_t, moe_hi, moe_lo = sem("s_yh"), [sem("in_moe0"), sem("in_moe1")], sem("moe_t"), sem("moe_hi"), sem("moe_lo")
        halt = sem("halt2")
        block = ctx.enter_context(nc.Block())

        AHEAD = 8

        def load_qk(sp, b, half):
            for tensor, dst in ((0, QR), (1, KR)):
                for par in range(2):
                    for slot in range(4):
                        part = slot % 2 if tensor == 0 else slot // 2
                        row = par * 64 + slot * 16
                        sp.dma_start(dst[row:row + 16, half * 4:(half + 1) * 4, :],
                                     qk_heads[b, tensor, half, par, part]).then_inc(qk_in[half], 16)

        QKI = 16 * 16

        @block.sync
        def _(sp):
            sp.dma_start(idS[:], ident).then_inc(in_id, 16)
            sp.dma_start(b0S[:], b0.partition_broadcast(P)).then_inc(in_id, 16)
            sp.dma_start(mrow[:], mask[0].partition_broadcast(P)).then_inc(in_mask, 16)
            for half in range(2):
                load_qk(sp, 0, half)
            with sp.Fori(0, B - 1) as b:
                sp.wait_ge(negc_t, 3 * b + 3)
                sp.dma_start(mrow[:], mask[b + 1].partition_broadcast(P)).then_inc(in_mask, 16)
                for half in range(2):
                    sp.wait_ge(s_L, b * 64 + 32 * (half + 1))
                    load_qk(sp, b + 1, half)
            sp.wait_ge(negc_t, 3 * B)
            sp.dma_start(mrow[:], mask[0].partition_broadcast(P)).then_inc(in_mask, 16)

        def before(b, h, d):
            return (b, h - d) if h >= d else (b - 1, h - d + NH)

        def all_heads(eng, step):
            for h in range(NH):
                step(0, h)
            with eng.Fori(1, B) as b:
                for h in range(NH):
                    step(b, h)
            for h in range(3):
                step(B, h)

        def exists(b, h, d):
            if not isinstance(b, int):
                return True
            return 0 <= b * NH + h - d < B * NH

        @block.gpsimd
        def _(pool):
            pool.sem_inc(s_y, AHEAD)
            pool.wait_ge(in_id, 32)
            pool.sem_inc(halt, 1)

            def mask_terms(b):
                pool.wait_ge(in_mask, 16 * b + 16)
                pool.sem_inc(halt, 1)
                pool.wait_ge(negc_ok, b + 1)
                pool.sem_inc(halt, 1)
                pool.tensor_scalar(mt[:, 0], mrow[:], -1.0, 1.0, ALU.mult, ALU.add).then_inc(negc_t, 1)
                pool.wait_ge(negc_t, 3 * b + 1)
                pool.sem_inc(halt, 1)
                pool.tensor_scalar_mul(mt[:, 0], mt[:, 0], NEG).then_inc(negc_t, 1)
                pool.tensor_scalar(mt[:, 1], mrow[:], b0S[:, 0:1], None, ALU.mult).then_inc(negc_t, 1)

            def mask_sum(b):
                pool.wait_ge(negc_t, 3 * b + 3)
                pool.sem_inc(halt, 1)
                pool.wait_ge(s_neg, 64 * b + AHEAD)
                pool.sem_inc(halt, 1)
                pool.tensor_tensor(negC[:], mt[:, 0], mt[:, 1], ALU.subtract).then_inc(negc_ok, 1)

            def load_weights(b):
                if not isinstance(b, int):
                    pool.wait_ge(moe_lo, 4 * b)
                    pool.sem_inc(halt, 1)
                for j in range(2):
                    pool.dma_start(wstage[:, j], moe_up[b * 2 + j]).then_inc(in_moe[j], 16)

            def scale_weights(b, j):
                pool.wait_ge(in_moe[j], 16 * b + 16)
                pool.sem_inc(halt, 1)
                pool.tensor_scalar_mul(wstage[:, j], wstage[:, j], WS).then_inc(moe_t, 1)

            def split_weights(b, j, which):
                n = b * 2 + j
                w = wstage[:, j].rearrange("p (w k m) -> p w k m", w=2, k=DC)
                o = WU[:, n, which]
                pool.wait_ge(moe_t, n + 1)
                pool.sem_inc(halt, 1)
                pool.tensor_copy(o[:, 0], w[:, which]).then_inc(moe_hi, 1)
                pool.wait_ge(moe_hi, 2 * n + which + 1)
                pool.sem_inc(halt, 1)
                pool.tensor_tensor(o[:, 1], w[:, which], o[:, 0], ALU.subtract).then_inc(moe_lo, 1)

            def split_output(b, h):
                i = b * NH + h
                cols = slice(h * DH, (h + 1) * DH)
                pool.wait_ge(s_norm, i + 1 + AHEAD)
                pool.sem_inc(halt, 1)
                pool.tensor_tensor(yf[:], yn[:, h % 4, :, 0:DH], yn[:, h % 4, :, DH:2 * DH], ALU.add).then_inc(s_y, 1)
                pool.wait_ge(s_y, i + 1 + AHEAD)
                pool.sem_inc(halt, 1)
                pool.tensor_copy(YH[:, b, :, cols], yf[:]).then_inc(s_yh, 1)
                pool.wait_ge(s_yh, 2 * i + 1)
                pool.sem_inc(halt, 1)
                pool.tensor_tensor(YL[:, b, :, cols], yf[:], YH[:, b, :, cols], ALU.subtract).then_inc(s_yh, 1)
                pool.wait_ge(s_yh, 2 * i + 2)
                pool.sem_inc(halt, 1)

            def step(b, h):
                real = exists(b, h, 0)
                if h == 0 and real:
                    mask_sum(b)
                if h == 1 and real:
                    load_weights(b)
                if exists(b, h, 3):
                    split_output(*before(b, h, 3))
                if not real:
                    return
                if h in (4, 8):
                    scale_weights(b, h // 4 - 1)
                if h in (5, 6, 9, 10):
                    split_weights(b, (h - 5) // 4, (h - 5) % 4)
                if h == 12:
                    mask_terms(b + 1)

            pool.sem_inc(negc_ok, 1)
            mask_terms(0)

            all_heads(pool, step)

        @block.tensor
        def _(pe):
            for s in (s_T, s_pv):
                pe.sem_inc(s, AHEAD)
            pe.wait_ge(in_id, 32)

            def scores(b, h, qt):
                n = (b * NH + h) * DC + qt
                base = 64 * (h % 2)
                pe.wait_ge(s_neg, n - 1 + AHEAD)
                pe.matmul(Lps[qt % 2][:, :], QR[base:base + 64, h // 2, qt * P:(qt + 1) * P],
                          KR[base:base + 64, h // 2, :], start=True, stop=True).then_inc(s_L, 1)

            def transposes(b, h, kc):
                i = b * NH + h
                if kc == 0:
                    pe.wait_ge(s_exp, i * DC + DC + AHEAD)
                pe.wait_ge(s_lo, DC * i + kc - DC + 1 + AHEAD)
                for qt in range(DC):
                    last = pe.transpose(Tps[kc][:, qt * P:(qt + 1) * P], Pr[:, h % 2, qt, kc * P:(kc + 1) * P], idS[:])
                last.then_inc(s_T, 1)

            def values(b, h):
                i = b * NH + h
                pe.wait_ge(s_lo, DC * i + DC + AHEAD)
                pe.wait_ge(s_norm, i - 1 + AHEAD)
                for qt in range(DC):
                    out = Ops[h % 2][:, qt]
                    for kc in range(DC):
                        pe.matmul(out[:, 0:VW], PT[:, h % 2, 0, kc, qt * P:(qt + 1) * P], V[:, b, kc, h],
                                  start=(kc == 0), stop=False, skip_group_check=True)
                    for kc in range(DC):
                        last = pe.matmul(out[:, DH:VW], PT[:, h % 2, 1, kc, qt * P:(qt + 1) * P], V[:, b, kc, h, DH:VW],
                                         start=False, stop=(kc == DC - 1), skip_group_check=True)
                last.then_inc(s_pv, 1)

            def step(b, h):
                def score(qt):
                    if exists(b, h, 0):
                        if h % (NH // 2) == 0 and qt == 0:
                            pe.wait_ge(qk_in[h // (NH // 2)], b * QKI + QKI)
                        scores(b, h, qt)

                def transpose(kc):
                    if exists(b, h, 1):
                        transposes(*before(b, h, 1), kc)

                for qt, kcs in ((0, ()), (1, (0, 1)), (2, (2, 3)), (3, ())):
                    score(qt)
                    for kc in kcs:
                        transpose(kc)
                if exists(b, h, 2):
                    values(*before(b, h, 2))

            all_heads(pe, step)

        @block.scalar
        def _(act):
            act.sem_inc(s_exp, AHEAD)
            act.sem_inc(s_hi, AHEAD)

            def exps(b, h, qt):
                i = b * NH + h
                n = i * DC + qt
                act.wait_ge(s_neg, n + 1 + AHEAD)
                if qt == 0:
                    act.wait_ge(s_T, i * DC - DC + AHEAD)
                act.activation(Pr[:, h % 2, qt, :], negL[:, qt, :], ACT.Exp, bias=nM[:, h % 4, qt:qt + 1],
                               scale=-1.0).then_inc(s_exp, 1)

            def transposed_high(b, h, kc):
                i = b * NH + h
                act.wait_ge(s_T, i * DC + kc + 1 + AHEAD)
                act.wait_ge(s_pv, i - 1 + AHEAD)
                act.activation(PT[:, h % 2, 0, kc, :], Tps[kc][:, :], ACT.Copy).then_inc(s_hi, 1)

            def step(b, h):
                for qt, kcs in ((0, (0, 1)), (1, (2,)), (2, (3,)), (3, ())):
                    for kc in kcs:
                        if exists(b, h, 1):
                            transposed_high(*before(b, h, 1), kc)
                    if exists(b, h, 0):
                        exps(b, h, qt)

            all_heads(act, step)

        @block.vector
        def _(dve):
            for s in (s_neg, s_lo, s_norm):
                dve.sem_inc(s, AHEAD)

            def negate_and_max(b, h, qt):
                n = (b * NH + h) * DC + qt
                dve.wait_ge(s_L, n + 1)
                dve.wait_ge(s_exp, n - 3 + AHEAD)
                dve.sem_inc(halt, 1)
                dve.tensor_tensor_reduce(out=negL[:, qt, :], in0=Lps[qt % 2][:, :], in1=negC[:], scale=1.0,
                                         scalar=3.0e38, op0=ALU.add, op1=ALU.min,
                                         accum_out=nM[:, h % 4, qt:qt + 1]).then_inc(s_neg, 1)

            def invert_sums(b, h):
                i = b * NH + h
                dve.wait_ge(s_pv, i + 1 + AHEAD)
                dve.wait_ge(s_norm, i + AHEAD)
                dve.reciprocal(ri[:].unsqueeze(2), Ops[h % 2][:, :, 2 * DH:VW]).then_inc(s_ri, 1)

            def normalize(b, h):
                i = b * NH + h
                dve.wait_ge(s_y, i - 3 + AHEAD)
                dve.wait_ge(s_ri, i + 1)
                dve.tensor_tensor(yn[:, h % 4], Ops[h % 2][:, :, 0:2 * DH],
                                  ri[:].unsqueeze(2).to_broadcast([P, DC, 2 * DH]), ALU.mult).then_inc(s_norm, 1)

            def transposed_low(b, h, kc):
                dve.wait_ge(s_hi, (b * NH + h) * DC + kc + 1 + AHEAD)
                dve.tensor_tensor(PT[:, h % 2, 1, kc, :], Tps[kc][:, :], PT[:, h % 2, 0, kc, :], ALU.subtract).then_inc(s_lo, 1)

            def step(b, h):
                if h == 0 and exists(b, h, 0):
                    dve.wait_ge(negc_ok, b + 2)
                    dve.sem_inc(halt, 1)
                for qt, kcs in ((0, ()), (1, (0,)), (2, (1,)), (3, (2, 3))):
                    if exists(b, h, 0):
                        negate_and_max(b, h, qt)
                    for kc in kcs:
                        if kc == DC - 1 and exists(b, h, 2):
                            invert_sums(*before(b, h, 2))
                        if exists(b, h, 1):
                            transposed_low(*before(b, h, 1), kc)
                if exists(b, h, 2):
                    normalize(*before(b, h, 2))

            all_heads(dve, step)


def experts(nc, x1_dram, router, w_down, iota, WU, WD, YH, YL, out):
    with ExitStack() as ctx:
        def sb(name, shape, dt=F32):
            return ctx.enter_context(nc.sbuf_tensor("moe_" + name, shape, dt))

        def sem(name):
            return ctx.enter_context(nc.semaphore("moe_" + name))

        def psum(name):
            return ctx.enter_context(nc.psum_tensor("moe_" + name, [P, 512], F32))

        TT = 4
        NG = B // 2
        NT = NG * TT
        dst = sb("dst", [P, HC, D])
        rst = sb("rst", [P, DC, E])
        rw = sb("rw", [P, 2, DC, E], F16)
        io = sb("io", [P, E])
        sc = sb("sc", [P, NT, E])
        top = sb("top", [P, NT, 8])
        idx = sb("idx", [P, NT, 8], U32)
        idf = sb("idf", [P, NT, 2])
        dif = sb("dif", [P, NT])
        ex = sb("ex", [P, NT])
        den = sb("den", [P, NT])
        wt = sb("wt", [P, 2, NT])
        c1 = sb("c1", [P, NT, E])
        comb = sb("comb", [P, NT * E])
        th = sb("th", [P, 2, 512])
        ga = sb("ga", [P, 512])
        hf = sb("hf", [P, 512])
        hid = sb("hid", [P, FC, 2, 512], F16)
        acc = sb("acc", [P, TT, D])
        gp = [psum("gp0"), psum("gp1")]
        up = [psum("up0"), psum("up1")]
        dp = [psum(f"dp{i}") for i in range(TT)]
        FIRST = 2 * FC
        in_d = [sem("in_d0"), sem("in_d1")]
        in_r, d_scaled, d_hi, d_lo, r_hi, r_lo = (sem("in_r"), sem("d_scaled"), sem("d_hi"), sem("d_lo"), sem("r_hi"),
                                                  sem("r_lo"))
        sc_mm, dif_ok, ex_ok, comb_ok, own = sem("sc_mm"), sem("dif_ok"), sem("ex_ok"), sem("comb_ok"), sem("own_dve")
        g_mm, u_mm, th_ok, hid_ok, d_mm, folded = sem("g_mm"), sem("u_mm"), sem("th_ok"), sem("hid_ok"), sem("d_mm"), sem("folded")
        acc_in, stored, ffn_own, halt = sem("acc_in"), sem("stored"), sem("ffn_own"), sem("halt3")
        block = ctx.enter_context(nc.Block())

        @block.sync
        def _(sp):
            sp.dma_start(rst[:], router).then_inc(in_r, 16)
            sp.dma_start(io[:], iota).then_inc(in_r, 16)
            sp.dma_start(dst[:, 0:FIRST], w_down[:, 0:FIRST]).then_inc(in_d[0], 16)
            sp.dma_start(dst[:, FIRST:HC], w_down[:, FIRST:HC]).then_inc(in_d[1], 16)
            with sp.Fori(0, NG) as g:
                for tt in range(TT):
                    sp.dma_start(acc[:, tt], x1_dram[g * 2 + tt // 2][:, tt % 2]).then_inc(acc_in, 16)
                for tt in range(TT):
                    sp.wait_ge(folded, (g * E + E) * TT + tt + 1)
                    sp.dma_start(out[g * 2 + tt // 2][:, tt % 2], acc[:, tt]).then_inc(stored, 16)
                sp.wait_ge(stored, (g * TT + TT) * 16)
                sp.sem_inc(halt, 1)

        @block.gpsimd
        def _(pool):
            def split_down(n):
                w = dst[:, bass.ds(n, 1)]
                pool.tensor_copy(WD[:, bass.ds(n, 1), 0], w).then_inc(d_hi, 1)
                pool.wait_ge(d_hi, n + 1)
                pool.sem_inc(halt, 1)
                pool.tensor_tensor(WD[:, bass.ds(n, 1), 1], w, WD[:, bass.ds(n, 1), 0], ALU.subtract).then_inc(d_lo, 1)

            for k, (first, last) in enumerate(((0, FIRST), (FIRST, HC))):
                pool.wait_ge(in_d[k], 16)
                pool.tensor_scalar_mul(dst[:, first:last], dst[:, first:last], WS).then_inc(d_scaled, 1)
                pool.wait_ge(d_scaled, k + 1)
                pool.sem_inc(halt, 1)
                with pool.Fori(first, last) as n:
                    split_down(n)

        @block.tensor
        def _(pe):
            pe.wait_ge(r_lo, 1)

            def gate_up(g, e, fc):
                n = (g * E + e) * FC + fc
                pe.wait_ge(hid_ok, n - FC + 1 + FC)
                for which, ps, done in ((0, gp[fc], g_mm), (1, up[fc], u_mm)):
                    k = 0
                    for wp, Yp in ((0, YH), (1, YH), (0, YL)):
                        for qt in range(DC):
                            last = pe.matmul(ps[:, :], WU[:, e * FC + fc, which, wp, qt, :],
                                             Yp[:, bass.ds(g * 2, 2), qt, :], start=(k == 0), stop=(k == 3 * DC - 1))
                            k += 1
                    last.then_inc(done, 1)

            def down(g, e):
                pe.wait_ge(hid_ok, (g * E + e) * FC + FC + FC)
                pe.wait_ge(d_lo, e * FC + FC)
                for tt in range(TT):
                    pe.wait_ge(folded, (g * E + e) * TT + tt + 1)
                    k = 0
                    for fc in range(FC):
                        for hp, wp in ((0, 0), (0, 1), (1, 0)):
                            last = pe.matmul(dp[tt][:, :], hid[:, fc, hp, tt * P:(tt + 1) * P], WD[:, e * FC + fc, wp, :],
                                             start=(k == 0), stop=(k == 3 * FC - 1))
                            k += 1
                    last.then_inc(d_mm, 1)

            for tt in range(NT):
                k = 0
                for wp, Yp in ((0, YH), (1, YH), (0, YL)):
                    for qt in range(DC):
                        last = pe.matmul(dp[0][:, tt * E:(tt + 1) * E], Yp[:, tt // 2, qt, (tt % 2) * P:(tt % 2 + 1) * P],
                                         rw[:, wp, qt, :], start=(k == 0), stop=(k == 3 * DC - 1))
                        k += 1
            last.then_inc(sc_mm, 1)
            with pe.Fori(0, NG) as g:
                gate_up(g, 0, 0)
                gate_up(g, 0, 1)
                with pe.Fori(1, E) as e:
                    gate_up(g, e, 0)
                    down(g, e - 1)
                    gate_up(g, e, 1)
                down(g, E - 1)

        @block.scalar
        def _(act):
            act.wait_ge(in_r, 32)
            act.activation(rw[:, 0].rearrange("p k e -> p (k e)"), rst[:].rearrange("p k e -> p (k e)"), ACT.Copy, scale=WS).then_inc(r_hi, 1)

            def gate_tanh(g, e, fc):
                n = (g * E + e) * FC + fc
                act.wait_ge(g_mm, n + 1)
                act.wait_ge(hid_ok, n + 1)
                act.activation(th[:, fc], gp[fc][:, :], ACT.Tanh, scale=0.5 / WS).then_inc(th_ok, 1)

            act.wait_ge(dif_ok, 1)
            act.activation(ex[:], dif[:], ACT.Exp, scale=1 / WS).then_inc(ex_ok, 1)
            with act.Fori(0, NG) as g:
                with act.Fori(0, E) as e:
                    for fc in range(FC):
                        gate_tanh(g, e, fc)

        @block.vector
        def _(dve):
            dve.wait_ge(in_r, 32)
            dve.wait_ge(r_hi, 1)
            dve.scalar_tensor_tensor(rw[:, 1].rearrange("p k e -> p (k e)"), rst[:].rearrange("p k e -> p (k e)"), WS,
                                     rw[:, 0].rearrange("p k e -> p (k e)"), ALU.mult, ALU.subtract).then_inc(r_lo, 1)
            dve.sem_inc(hid_ok, FC)

            def route():
                k = [0]

                def step(ins):
                    ins.then_inc(own, 1)
                    k[0] += 1
                    dve.wait_ge(own, k[0])

                dve.wait_ge(sc_mm, 1)
                step(dve.tensor_copy(sc[:].rearrange("p t e -> p (t e)"), dp[0][:, 0:NT * E]))
                dve.sem_inc(folded, TT)
                for tt in range(NT):
                    last = dve.max(top[:, tt], sc[:, tt])
                step(last)
                for tt in range(NT):
                    last = dve.max_index(idx[:, tt], top[:, tt], sc[:, tt])
                step(last)
                dve.tensor_tensor(dif[:], top[:, :, 1], top[:, :, 0], ALU.subtract).then_inc(dif_ok, 1)
                step(dve.tensor_copy(idf[:], idx[:, :, 0:2]))
                dve.wait_ge(ex_ok, 1)
                step(dve.tensor_scalar(den[:], ex[:], WS, WS, ALU.mult, ALU.add))
                step(dve.reciprocal(wt[:, 0], den[:]))
                step(dve.tensor_tensor(wt[:, 1], wt[:, 0], ex[:], ALU.mult))
                for tt in range(NT):
                    last = dve.tensor_scalar(c1[:, tt], io[:], idf[:, tt, 0:1], wt[:, 0, tt:tt + 1], ALU.is_equal, ALU.mult)
                    last = dve.tensor_scalar(comb[:, tt * E:(tt + 1) * E], io[:], idf[:, tt, 1:2], wt[:, 1, tt:tt + 1], ALU.is_equal, ALU.mult)
                step(last)
                dve.tensor_tensor(comb[:], comb[:], c1[:].rearrange("p t e -> p (t e)"), ALU.add).then_inc(comb_ok, 1)
                dve.wait_ge(comb_ok, 1)

            def hidden(g, e, fc):
                n = (g * E + e) * FC + fc
                dve.wait_ge(th_ok, n + 1)
                dve.scalar_tensor_tensor(ga[:], th[:, fc], 1.0, gp[fc][:, :], ALU.add, ALU.mult).then_inc(ffn_own, 1)
                dve.wait_ge(ffn_own, 3 * n + 1)
                dve.wait_ge(u_mm, n + 1)
                dve.wait_ge(hid_ok, n + FC)
                dve.scalar_tensor_tensor(hf[:], ga[:], 0.5 / (WS * WS), up[fc][:, :], ALU.mult, ALU.mult).then_inc(ffn_own, 1)
                dve.wait_ge(ffn_own, 3 * n + 2)
                dve.tensor_copy(hid[:, fc, 0], hf[:]).then_inc(ffn_own, 1)
                dve.wait_ge(ffn_own, 3 * n + 3)
                dve.tensor_tensor(hid[:, fc, 1], hf[:], hid[:, fc, 0], ALU.subtract).then_inc(hid_ok, 1)

            def fold(g, e):
                for tt in range(TT):
                    n = (g * E + e) * TT + tt
                    dve.wait_ge(d_mm, n + 1)
                    dve.wait_ge(folded, n + 1)
                    dve.scalar_tensor_tensor(acc[:, tt], dp[tt][:, :], comb[:, bass.ds((g * TT + tt) * E + e, 1)],
                                             acc[:, tt], ALU.mult, ALU.add).then_inc(folded, 1)

            route()
            with dve.Fori(0, NG) as g:
                hidden(g, 0, 0)
                hidden(g, 0, 1)
                dve.wait_ge(acc_in, (g + 1) * TT * 16)
                dve.sem_inc(halt, 1)
                with dve.Fori(1, E) as e:
                    fold(g, e - 1)
                    hidden(g, e, 0)
                    hidden(g, e, 1)
                fold(g, E - 1)


def hadamard(n):
    import numpy as np
    h = np.ones((1, 1), np.float32)
    while h.shape[0] < n:
        h = np.block([[h, h], [h, -h]])
    return np.ascontiguousarray(h.astype(np.float32))


def lay_out(v):
    import numpy as np
    a = {k: np.asarray(x) for k, x in v.items()}
    c = np.ascontiguousarray

    def slices(gate, up):
        w = np.stack([gate, up], 1).reshape(HC, 2, P, DC, P)
        return c(w.transpose(4, 0, 1, 3, 2).reshape(P, HC * 2 * DC * P))

    x = a["x"]
    r = {
        "drive": c(x.reshape(B, S, DC, P).transpose(3, 1, 2, 0).reshape(P, S, SC)),
        "cond": c(a["cond_2048"].reshape(B, DC, P).transpose(2, 1, 0).reshape(P, SC)),
        "bias": c(a["L0_cond_bias"].reshape(DC, P).T),
        "coup": c(a["L0_cond_coupling"].T.reshape(DC, P, D).transpose(1, 0, 2).reshape(P, DC * D)),
        "had": hadamard(P),
        "w_up": slices(a["L0_ffn_W1"].reshape(HC, P, D), a["L0_ffn_W3"].reshape(HC, P, D)),
        "w_down": c(a["L0_ffn_W2"].T.reshape(HC, P, D).transpose(1, 0, 2)),
        "x_tb": c(x.transpose(1, 0, 2).reshape(NB, P, D)),
        "mask": c(a["cond_2048"]),
        "b0": c(a["L1_cond_b"].reshape(1)),
        "w_qkv": c(np.stack([a[n].T.reshape(CT, P, C) for n in ("L1_cond_Wq", "L1_cond_Wk", "L1_cond_Wv")], 1)
                   .transpose(2, 1, 0, 3)),
        "ident": np.eye(P, dtype=np.float32),
        "router": c(a["L1_ffn_router_w"].reshape(DC, P, E).transpose(1, 0, 2)),
        "moe_up": c(slices(a["L1_ffn_gate_proj"].transpose(0, 2, 1).reshape(HC, P, D),
                           a["L1_ffn_up_proj"].transpose(0, 2, 1).reshape(HC, P, D))
                    .reshape(P, HC, 2 * DC * P).transpose(1, 0, 2)),
        "moe_down": c(a["L1_ffn_down_proj"].reshape(HC, P, D).transpose(1, 0, 2)),
        "iota": np.broadcast_to(np.arange(E, dtype=np.float32), (P, E)).copy(),
    }
    return r


def build(nc, d, out):
    x1 = nc.dram_tensor("x1", (S, B, D), F32, kind="Internal").ap()
    qk = nc.dram_tensor("qk", (B, 2, 2, P, 2, D), F16, kind="Internal").ap()
    x1_blocks = x1.rearrange("(n t) b d -> n (t b) d", t=BS)
    x1_batch = x1.rearrange("(c p) b d -> b p c d", p=P)
    out_batch = out.rearrange("b (c p) d -> b p c d", p=P)
    with nc.sbuf_tensor("WU", [P, HC, 2, 2, DC, P], F16) as WU:
        with nc.sbuf_tensor("WD", [P, HC, 2, D], F16) as WD:
            oscillator_and_ffn(nc, d["drive"], d["cond"], d["bias"], d["coup"], d["had"], d["w_up"], d["w_down"],
                               d["x_tb"], x1_blocks, WU, WD)
        with nc.sbuf_tensor("YH", [P, B, DC, C], F16) as YH, nc.sbuf_tensor("YL", [P, B, DC, C], F16) as YL:
            attention(nc, x1_batch, qk, d["mask"], d["b0"], d["w_qkv"], d["ident"], d["moe_up"], WU, YH, YL)
            with nc.sbuf_tensor("WE", [P, HC, 2, D], F16) as WE:
                experts(nc, x1_batch, d["router"], d["moe_down"], d["iota"], WU, WE, YH, YL, out_batch)


def kernel(**inputs):
    import concourse.bacc as bacc
    from concourse.bass_utils import run_bass_kernel_spmd

    nc = bacc.Bacc("TRN2", target_bir_lowering=False, num_devices=1)
    arrays = lay_out(inputs)
    d = {n: nc.dram_tensor(n, a.shape, F32, kind="ExternalInput").ap() for n, a in arrays.items()}
    out = nc.dram_tensor("out", (B, S, D), F32, kind="ExternalOutput").ap()
    build(nc, d, out)
    return run_bass_kernel_spmd(nc, [arrays], core_ids=[0]).results[0]["out"]
```
